# Optimizing a Trainium2 kernel written in Bass

```python
import numpy as np
import jax
import jax.numpy as jnp

def _softmax(x, axis=-1):
    return jax.nn.softmax(x, axis=axis)
def _gelu(x):
    return jax.nn.gelu(x, approximate=True)
def _silu(x):
    return jax.nn.silu(x)
def _sigmoid(x):
    return jax.nn.sigmoid(x)
def _layernorm(x, axis=-1, eps=1e-5):
    m = jnp.mean(x, axis=axis, keepdims=True)
    v = jnp.var(x, axis=axis, keepdims=True)
    return (x - m) / jnp.sqrt(v + eps)
def _scatter_add(tgt, idx, src, axis=0):
    return tgt.at[idx].add(src)
def _segment_sum(src, seg, n):
    return jax.ops.segment_sum(src, seg, n)

kernel_name = 'mk_adj_resnorm_d4_adj_128_378319'

def setup_inputs(seed: int = 0):
    np.random.seed(seed)
    _w = jnp.asarray
    def _rec_inputs():
        import jax
        import jax.numpy as jnp
        _gk = jax.random.key(seed)
        x = -0.001547 + 1.001 * jax.random.normal(jax.random.fold_in(_gk, 1), (128, 64, 128), jnp.float32)
        _a = jax.random.bernoulli(jax.random.fold_in(_gk, 2), 0.0625, (128, 64, 64))
        _a = jnp.logical_or(_a, jnp.swapaxes(_a, -1, -2))
        _a = jnp.logical_or(_a, jnp.eye(64, dtype=bool))
        _af = _a.astype(jnp.float32)
        _af = _af * jax.random.uniform(jax.random.fold_in(_gk, 3), (128, 64, 64), jnp.float32, 0.05, 0.999994)
        adj = _af
        return x, adj
    x, adj = _rec_inputs()
    def _L0_gnn_setup():
        import jax, jax.numpy as jnp
        import numpy as np
        B, N, D, L = (4, 512, 128, 2)
        key = jax.random.key(seed)
        ks = jax.random.split(key, 6)
        node_feats = jax.random.normal(ks[0], (B, N, D), dtype=jnp.float32)
        adj_mask = jax.random.uniform(ks[1], (B, N, N), dtype=jnp.float32)
        w1 = jax.random.normal(ks[2], (L, D, 2 * D), dtype=jnp.float32) * 0.05
        b1 = jax.random.normal(ks[3], (L, D), dtype=jnp.float32) * 0.05
        w2 = jax.random.normal(ks[4], (L, D, D), dtype=jnp.float32) * 0.05
        b2 = jax.random.normal(ks[5], (L, D), dtype=jnp.float32) * 0.05
        return {'node_feats': node_feats, 'adj_mask': adj_mask, 'w1': w1, 'b1': b1, 'w2': w2, 'b2': b2}
    _L0_gnn_all = _L0_gnn_setup()
    _L0_gnn_in = {k: v for k, v in _L0_gnn_all.items() if k in ('w1', 'b1', 'w2', 'b2', )}
    del _L0_gnn_all

    def _L1_gnn_setup():
        import jax, jax.numpy as jnp
        import numpy as np
        B, N, F_IN, F_OUT = (4, 512, 128, 128)
        key = jax.random.key(seed)
        ks = jax.random.split(key, 12)
        s_in = 1.0 / np.sqrt(F_IN)
        s_out = 1.0 / np.sqrt(F_OUT)
        s_2o = 1.0 / np.sqrt(2 * F_OUT)
        node_features = jax.random.normal(ks[0], (B, N, F_IN), dtype=jnp.float32)
        raw = jax.random.uniform(ks[1], (B, N, N), dtype=jnp.float32)
        keep = jax.random.uniform(ks[2], (B, N, N)) > 0.5
        adjacency = jnp.where(keep, raw, 0.0)
        return {'node_features': node_features, 'adjacency': adjacency, 'W_self_w': jax.random.uniform(ks[3], (F_IN, F_OUT), minval=-s_in, maxval=s_in), 'W_self_b': jax.random.uniform(ks[4], (F_OUT,), minval=-s_in, maxval=s_in), 'W_nb_w': jax.random.uniform(ks[5], (F_IN, F_OUT), minval=-s_in, maxval=s_in), 'W_nb_b': jax.random.uniform(ks[6], (F_OUT,), minval=-s_in, maxval=s_in), 'A1_w': jax.random.uniform(ks[7], (2 * F_OUT, F_OUT), minval=-s_2o, maxval=s_2o), 'A1_b': jax.random.uniform(ks[8], (F_OUT,), minval=-s_2o, maxval=s_2o), 'A2_w': jax.random.uniform(ks[9], (F_OUT, 1), minval=-s_out, maxval=s_out), 'A2_b': jax.random.uniform(ks[10], (1,), minval=-s_out, maxval=s_out)}
    _L1_gnn_all = _L1_gnn_setup()
    _L1_gnn_in = {k: v for k, v in _L1_gnn_all.items() if k in ('W_self_w', 'W_self_b', 'W_nb_w', 'W_nb_b', 'A1_w', 'A1_b', 'A2_w', 'A2_b', )}
    del _L1_gnn_all

    def _L2_gnn_setup():
        import jax, jax.numpy as jnp
        import numpy as np
        B, S, H, HID = (1, 1024, 128, 128)
        LN_EPS = 1e-05

        def _layernorm(y, gamma, beta):
            mu = jnp.mean(y, axis=-1, keepdims=True)
            var = jnp.mean(jnp.square(y - mu), axis=-1, keepdims=True)
            return (y - mu) * jax.lax.rsqrt(var + LN_EPS) * gamma + beta
        key = jax.random.key(seed)
        ks = jax.random.split(key, 8)
        x = jax.random.normal(ks[0], (B, S, H), dtype=jnp.float32)
        adj = jax.random.uniform(ks[1], (B, S, S), dtype=jnp.float32)
        W1 = jax.random.normal(ks[2], (2 * H, HID), dtype=jnp.float32) / np.sqrt(2 * H)
        b1 = jnp.zeros((HID,), dtype=jnp.float32)
        W2 = jax.random.normal(ks[3], (HID, HID), dtype=jnp.float32) / np.sqrt(HID)
        b2 = jnp.zeros((HID,), dtype=jnp.float32)
        gamma = jnp.ones((HID,), dtype=jnp.float32)
        beta = jnp.zeros((HID,), dtype=jnp.float32)
        return {'x': x, 'adj': adj, 'W1': W1, 'b1': b1, 'W2': W2, 'b2': b2, 'gamma': gamma, 'beta': beta}
    _L2_gnn_all = _L2_gnn_setup()
    _L2_gnn_in = {k: v for k, v in _L2_gnn_all.items() if k in ('W1', 'b1', 'W2', 'b2', 'gamma', 'beta', )}
    del _L2_gnn_all

    def _L3_gnn_setup():
        import jax, jax.numpy as jnp
        import numpy as np
        EPS = 1e-06
        key = jax.random.key(seed)
        k_x, k_a, k_w, k_b = jax.random.split(key, 4)
        B, N, Fin, Fout = (8, 2048, 128, 128)
        X = jax.random.normal(k_x, (B, N, Fin), dtype=jnp.float32)
        A = jax.random.uniform(k_a, (B, N, N), dtype=jnp.float32)
        bound = 1.0 / np.sqrt(Fin)
        W = jax.random.uniform(k_w, (Fout, Fin), minval=-bound, maxval=bound, dtype=jnp.float32)
        b = jax.random.uniform(k_b, (Fout,), minval=-bound, maxval=bound, dtype=jnp.float32)
        return {'X': X, 'A': A, 'W': W, 'b': b}
    _L3_gnn_all = _L3_gnn_setup()
    _L3_gnn_in = {k: v for k, v in _L3_gnn_all.items() if k in ('W', 'b', )}
    del _L3_gnn_all

    return {
        "x": x,
        "adj": adj,
        "L0_gnn_w1": _L0_gnn_in["w1"],
        "L0_gnn_b1": _L0_gnn_in["b1"],
        "L0_gnn_w2": _L0_gnn_in["w2"],
        "L0_gnn_b2": _L0_gnn_in["b2"],
        "L1_gnn_W_self_w": _L1_gnn_in["W_self_w"],
        "L1_gnn_W_self_b": _L1_gnn_in["W_self_b"],
        "L1_gnn_W_nb_w": _L1_gnn_in["W_nb_w"],
        "L1_gnn_W_nb_b": _L1_gnn_in["W_nb_b"],
        "L1_gnn_A1_w": _L1_gnn_in["A1_w"],
        "L1_gnn_A1_b": _L1_gnn_in["A1_b"],
        "L1_gnn_A2_w": _L1_gnn_in["A2_w"],
        "L1_gnn_A2_b": _L1_gnn_in["A2_b"],
        "L2_gnn_W1": _L2_gnn_in["W1"],
        "L2_gnn_b1": _L2_gnn_in["b1"],
        "L2_gnn_W2": _L2_gnn_in["W2"],
        "L2_gnn_b2": _L2_gnn_in["b2"],
        "L2_gnn_gamma": _L2_gnn_in["gamma"],
        "L2_gnn_beta": _L2_gnn_in["beta"],
        "L3_gnn_W": _L3_gnn_in["W"],
        "L3_gnn_b": _L3_gnn_in["b"],
    }

def reference(x, adj, L0_gnn_w1, L0_gnn_b1, L0_gnn_w2, L0_gnn_b2, L1_gnn_W_self_w, L1_gnn_W_self_b, L1_gnn_W_nb_w, L1_gnn_W_nb_b, L1_gnn_A1_w, L1_gnn_A1_b, L1_gnn_A2_w, L1_gnn_A2_b, L2_gnn_W1, L2_gnn_b1, L2_gnn_W2, L2_gnn_b2, L2_gnn_gamma, L2_gnn_beta, L3_gnn_W, L3_gnn_b):
    import jax
    import jax.numpy as jnp
    def _L0_gnn_ref(node_feats, adj_mask, w1, b1, w2, b2):
        import jax, jax.numpy as jnp
        import numpy as np
        B, N, D, L = (4, 512, 128, 2)
        h = node_feats
        d = h.shape[-1]
        n_layers = w1.shape[0]
        for l in range(n_layers):
            wi = w1[l][:, :d]
            wj = w1[l][:, d:]
            ai = jnp.einsum('bnd,od->bno', h, wi)
            aj = jnp.einsum('bnd,od->bno', h, wj)
            m = jax.nn.relu(ai[:, :, None, :] + aj[:, None, :, :] + b1[l])
            m = jnp.einsum('bijd,od->bijo', m, w2[l]) + b2[l]
            m = m * adj_mask[..., None]
            msg = m.sum(axis=2)
            h = h + msg
        return h

    def _L1_gnn_ref(node_features, adjacency, W_self_w, W_self_b, W_nb_w, W_nb_b, A1_w, A1_b, A2_w, A2_b):
        import jax, jax.numpy as jnp
        import numpy as np
        B, N, F_IN, F_OUT = (4, 512, 128, 128)
        h_self = node_features @ W_self_w + W_self_b
        h_nb = node_features @ W_nb_w + W_nb_b
        A1_i, A1_j = (A1_w[:F_OUT], A1_w[F_OUT:])
        pre = (h_self @ A1_i)[:, :, None, :] + (h_nb @ A1_j)[:, None, :, :] + A1_b
        scores = (jax.nn.relu(pre) @ A2_w)[..., 0] + A2_b[0]
        scores = jnp.where(adjacency == 0, -1000000000.0, scores)
        attn = jax.nn.softmax(scores, axis=-1)
        agg = jnp.einsum('bij,bjf->bif', attn, h_nb)
        return jax.nn.relu(h_self + agg)

    def _L2_gnn_ref(x, adj, W1, b1, W2, b2, gamma, beta):
        import jax, jax.numpy as jnp
        import numpy as np
        B, S, H, HID = (1, 1024, 128, 128)
        LN_EPS = 1e-05

        def _layernorm(y, gamma, beta):
            mu = jnp.mean(y, axis=-1, keepdims=True)
            var = jnp.mean(jnp.square(y - mu), axis=-1, keepdims=True)
            return (y - mu) * jax.lax.rsqrt(var + LN_EPS) * gamma + beta
        hi = jnp.einsum('bsh,hk->bsk', x, W1[:H])
        hj = jnp.einsum('bsh,hk->bsk', x, W1[H:])
        h = jax.nn.relu(hi[:, :, None, :] + hj[:, None, :, :] + b1)
        y = jnp.einsum('bijk,kl->bijl', h, W2) + b2
        y = _layernorm(y, gamma, beta)
        out = jnp.einsum('bij,bijh->bih', adj, y)
        return out

    def _L3_gnn_ref(X, A, W, b):
        import jax, jax.numpy as jnp
        import numpy as np
        EPS = 1e-06
        N = A.shape[-1]
        A_hat = A + jnp.eye(N, dtype=A.dtype)
        d_inv_sqrt = (jnp.sum(A_hat, axis=-1) + EPS) ** (-0.5)
        A_norm = d_inv_sqrt[:, :, None] * A_hat * d_inv_sqrt[:, None, :]
        support = jnp.einsum('bnm,bmf->bnf', A_norm, X)
        out = jnp.einsum('bnf,of->bno', support, W) + b
        return jax.nn.relu(out)

    x = _layernorm(x + _L0_gnn_ref(x, adj, L0_gnn_w1, L0_gnn_b1, L0_gnn_w2, L0_gnn_b2), axis=-1)
    x = _layernorm(x + _L1_gnn_ref(x, adj, L1_gnn_W_self_w, L1_gnn_W_self_b, L1_gnn_W_nb_w, L1_gnn_W_nb_b, L1_gnn_A1_w, L1_gnn_A1_b, L1_gnn_A2_w, L1_gnn_A2_b), axis=-1)
    x = _layernorm(x + _L2_gnn_ref(x, adj, L2_gnn_W1, L2_gnn_b1, L2_gnn_W2, L2_gnn_b2, L2_gnn_gamma, L2_gnn_beta), axis=-1)
    x = _layernorm(x + _L3_gnn_ref(x, adj, L3_gnn_W, L3_gnn_b), axis=-1)
    return x


_drawn_inputs = setup_inputs


def setup_inputs(seed=0):
    import zlib

    import numpy as np

    out = dict(_drawn_inputs(seed))
    spreads = {'L2_gnn_b1': (0.0, 0.1),
     'L2_gnn_b2': (0.0, 0.1),
     'L2_gnn_gamma': (1.0, 0.2),
     'L2_gnn_beta': (0.0, 0.1)}
    factors = {'L1_gnn_A1_w': 8.0, 'L1_gnn_A1_b': 8.0, 'L1_gnn_A2_w': 8.0}
    for name, (base, spread) in spreads.items():
        noise = np.random.default_rng([zlib.crc32(name.encode()), seed]).standard_normal(out[name].shape)
        drawn = base * np.exp(spread * noise) if base else spread * noise
        out[name] = jnp.asarray(drawn.astype(out[name].dtype))
    for name, factor in factors.items():
        out[name] = (out[name] * factor).astype(out[name].dtype)
    return out
```

```python
from contextlib import ExitStack

import numpy as np
import concourse.bass as bass
from concourse import mybir

ALU = mybir.AluOpType
ACT = mybir.ActivationFunctionType
F32 = mybir.dt.float32
BF16 = mybir.dt.bfloat16
AX = mybir.AxisListType

P = 128
NB, N, D = 128, 64, 128
NU = NB // 2
GU = 8
NG = NU // GU
QU = 4
CH = 512
QROWS = 24
EPS = 1e-5
NEG = 1e9

INPUTS = ["x", "adj", "L0_gnn_w1", "L0_gnn_b1", "L0_gnn_w2", "L0_gnn_b2",
          "L1_gnn_W_self_w", "L1_gnn_W_self_b", "L1_gnn_W_nb_w", "L1_gnn_W_nb_b",
          "L1_gnn_A1_w", "L1_gnn_A1_b", "L1_gnn_A2_w", "L1_gnn_A2_b",
          "L2_gnn_W1", "L2_gnn_b1", "L2_gnn_W2", "L2_gnn_b2", "L2_gnn_gamma", "L2_gnn_beta",
          "L3_gnn_W", "L3_gnn_b"]


def ds(start, size):
    return bass.ds(start, size)


def program(nc, out, parts_dram, ident_d, pick_d, sel_d, **inp):
    ctx = ExitStack()

    def sb(name, shape, dt=F32):
        return ctx.enter_context(nc.sbuf_tensor(name, shape, dt))

    def sem(name):
        return ctx.enter_context(nc.semaphore(name))

    def after(eng, semaphore, count):
        if isinstance(count, int) and count <= 0:
            return
        eng.wait_ge(semaphore, count)

    with ctx:
        x = sb("x", [P, NU, D])
        adj_blocks = sb("adj_blocks", [P, NU, P])
        w_blocks = sb("w_blocks", [P, NU, P])
        pairs = sb("pairs", [P, 4, 4 * CH])
        adj_rows = sb("adj_rows", [P, 2, CH])
        block_stage = sb("block_stage", [P, 2, GU, P])
        xs = sb("xs", [P, 4, D])
        xt_dup = sb("xt_dup", [P, 2, 2, 2, N])
        xt_flat = xt_dup[:, :, :, :, :].rearrange("p z b c i -> p z (b c i)")
        plain_xt = slice(N, 3 * N)
        x_first = sb("x_first", [P, 4, D])
        scratch = sb("scratch", [P, 9752])
        ident = sb("ident", [P, P])
        pick = sb("pick", [P, 4, P])
        sel = sb("sel", [QROWS, 4, P], BF16)
        wraw = pairs[:, 0, 0:8 * P].rearrange("p (k c) -> p k c", k=8)
        sel_f = pairs[0:QROWS, 1, 0:4 * P].rearrange("p (k c) -> p k c", k=4)
        wt = sb("wt", [P, 8, P])
        WI, WJ, W2T = (0, 3), (1, 4), (2, 5)
        L3T = 6
        wl = sb("wl", [P, 8, P])
        WSELF, WNB, A1I, A1J, W1A, W1B, W2, W2G = range(8)
        rows = sb("rows", [P, 12, P])
        R_B1, R_B2, R_BSELF, R_BNB, R_B2C, R_GAMMA, R_BETA, R_L3B, R_B1L2 = (0, 1), (2, 3), 4, 5, 6, 7, 8, 9, 10
        cols = sb("cols", [P, 8])
        C_BSELF, C_BNB, C_A1B, C_B1, C_A2, C_A2B, C_B2C, C_EPS = range(8)
        window_a2 = sb("window_a2", [P, 63])
        window_two = sb("window_two", [P, 64])
        window_mean = sb("window_mean", [P, 63])
        ones = sb("ones", [P, 1])
        w2_mean = sb("w2_mean", [P, 2])
        node = sb("node", [P, NU, 8])
        MEAN, RSTD, SUM_W, SUM_ADJ, DINV = range(5)
        node_now = sb("node_now", [P, 4, 8])
        degree = sb("degree", [P, NU])
        halves = sb("halves", [P, NU, 6])
        half_sum = sb("half_sum", [P, NU])
        half_gap = sb("half_gap", [P, NU])
        gap_sq = sb("gap_sq", [P, NU])
        var = sb("var", [P, NU])
        var_eps = sb("var_eps", [P, NU])
        std = sb("std", [P, NU])

        off = [0]

        def view(*shape, dt=F32):
            n = int(np.prod(shape)) // (2 if dt == BF16 else 1)
            v = scratch[:, off[0]:off[0] + n]
            off[0] += n
            if dt == BF16:
                v = v.bitcast(BF16)
            return v
        windows = view(4, 4, 4, 32).rearrange("p (z q k m) -> p z q k m", z=4, q=4, k=4)
        spread = view(2, 2048, dt=BF16).rearrange("p (z c) -> p z c", z=2)
        c_pos = view(4, 2, D).rearrange("p (z b d) -> p z b d", z=4, b=2)
        c_neg = view(4, 2, D).rearrange("p (z b d) -> p z b d", z=4, b=2)
        r_sb = view(2, 4, D).rearrange("p (z e d) -> p z e d", z=2, e=4)
        a_sb = view(2, D).rearrange("p (z d) -> p z d", z=2)
        a_full = view(D)
        a_rest = view(D)
        parts = view(2, 3, D, dt=BF16).rearrange("p (z t d) -> p z t d", z=2, t=3)
        rt_sb = view(2, D).rearrange("p (z d) -> p z d", z=2)
        o_sb = view(2, D).rearrange("p (z d) -> p z d", z=2)
        f_a = view(D)
        f_b = view(D)
        f_c = view(D)
        f_d = view(D)
        x_raw = view(D)
        off[0] = 0
        xs4 = view(4, D).rearrange("p (u d) -> p u d", u=4)
        xs4_raw = view(4, D).rearrange("p (u d) -> p u d", u=4)
        xt4 = view(CH)
        hs4 = view(CH)
        hn4 = view(CH)
        p4 = view(2, CH).rearrange("p (z c) -> p z c", z=2)
        q4 = view(2, CH).rearrange("p (z c) -> p z c", z=2)
        squares = view(2, 2 * CH).rearrange("p (h c) -> p h c", h=2)
        is_zero = view(CH)
        mask = view(CH)
        fill = view(CH)
        score_a = view(CH)
        score_b = view(CH)
        weights = view(CH)
        row_max = view(8)
        row_sum = view(8)
        row_inv = view(8)
        off[0] = 0
        block_now = view(2, P).rearrange("p (z c) -> p z c", z=2)
        n_sb = view(2, 2, D).rearrange("p (z b d) -> p z b d", z=2, b=2)
        n_full = view(2, 2, D).rearrange("p (z b d) -> p z b d", z=2, b=2)
        xd = view(2, D).rearrange("p (z d) -> p z d", z=2)
        agg_a = view(2, D).rearrange("p (z d) -> p z d", z=2)
        x_raw2 = view(D)
        y_out = view(2, GU, D).rearrange("p (z u d) -> p z u d", z=2, u=GU)

        wide = [ctx.enter_context(nc.psum_tensor(f"wide{h}", [P, 2 * CH], F32)) for h in range(2)]
        sums = [ctx.enter_context(nc.psum_tensor(f"sums{h}", [P, CH], F32)) for h in range(2)]
        misc_a = ctx.enter_context(nc.psum_tensor("misc_a", [P, CH], F32))
        misc_b = ctx.enter_context(nc.psum_tensor("misc_b", [P, CH], F32))

        loaded = {k: sem(f"loaded_{k}") for k in ("x", "const", "raw", "flat", "row", "col")}
        consts = sem("consts")
        wt_filled, wt_out = sem("wt_filled"), sem("wt_out")
        prep = sem("prep")
        b2c_filled, b2c_out = sem("b2c_filled"), sem("b2c_out")
        norm_steps = [sem(f"norm_steps{n}") for n in range(4)]
        node_zero = sem("node_zero")
        waited = sem("waited")
        stats_done = [sem(f"stats_done{n}") for n in range(4)]
        std_done = [sem(f"std_done{n}") for n in range(4)]
        norm_ready = [sem(f"norm_ready{n}") for n in range(4)]
        dinv_steps = sem("dinv_steps")
        out_done = [sem("out_even"), sem("out_odd")]
        y_ready = sem("y_ready")

        def alone(eng):
            eng.sem_inc(waited)

        def signals(phase, names):
            return {nm: sem(f"{phase}_{nm}") for nm in names.split()}

        near_names = ("staged noded windowed t_filled xt_out ac_filled a_out c_out split parts_put flat0 flat1 spreaded maxed "
                      "weighted r_out rt_filled rt_out o_filled o_out fin x_new ")
        near_sems = signals("near", near_names + "first_in0 first_in1 first_in2 first_in3 rawed")
        block_names = "turned blocks_out summed_w sum_out"
        feat_names = "staged rawed lin_filled lin_out formed scored adj_in0 adj_in1 inverted weighed "
        feat = {"l1a": signals("l1a", feat_names + "masked shifted topped cut exped totalled " + block_names),
                "l2a": signals("l2a", feat_names + "relued y_filled squared std_out " + block_names)}
        first = signals("s", "adj_in0 adj_in1 " + block_names)
        agg_names = "staged rawed block_in t_filled xt_out n_filled n_out n_biased o_filled o_sum x_new"
        agg_sems = signals("agg", agg_names)

        x_dram = inp["x"].rearrange("(u b) i d -> (b i) u d", b=2)
        out_dram = out.rearrange("(u b) i d -> (b i) u d", b=2)
        adj_chunks = inp["adj"].rearrange("(g bb) (ib i) j -> g (bb ib) (i j)", g=NG, ib=8) \
            .rearrange("g (t q) c -> g q t c", q=4)

        def load_adj_rows(sp, g, z, signal):
            for q in range(4):
                sp.dma_start(adj_rows[32 * q:32 * q + 32, z, :], adj_chunks[g, q]).then_inc(signal, 16)

        def four_unit_rounds(eng, body, total=NU, step=4):
            body(0)
            with eng.Fori(1, total // step - 1) as r:
                body(r)
            body(total // step - 1)

        def two_rounds(eng, body, total, step=2):
            body(0)
            with eng.Fori(1, total // step - 1) as r:
                body(r)
            body(total // step - 1)

        def pe_turn(pe, s, g, src, ready, count):
            pe.wait_ge(ready, count)
            after(pe, s["blocks_out"], 2 * g)
            after(pe, s["sum_out"], g)
            for i4 in range(4):
                m = nc.tensor.transpose(misc_b[:, i4 * P:(i4 + 1) * P], src[:, i4 * P:(i4 + 1) * P], ident[:, :])
            m.then_inc(s["turned"], 1)

        def act_blocks(act, s, g, z, before):
            act.wait_ge(s["turned"], g + 1)
            after(act, moved[z], 8 * (before + g - z))
            for par in range(2):
                h = slice(64 * par, 64 * par + 64)
                dst = block_stage[h, z].rearrange("p u (t q i r) -> p (u t) q i r", t=4, q=4, i=4)[:, :, :, :, par]
                src = misc_b[h, :].rearrange("p (i q t) -> p t q i", i=4, q=4)
                for q in range(4):
                    c = nc.scalar.copy(dst[:, :, q], src[:, :, q])
                c.then_inc(s["blocks_out"], 1)

        def pe_row_sums(pe, s, g, z):
            pe.wait_ge(s["blocks_out"], 2 * g + 2)
            for u in range(GU):
                m = nc.tensor.matmul(misc_b[:, u:u + 1], block_stage[:, z, u, :], ones[:, :], start=True, stop=True)
            m.then_inc(s["summed_w"], 1)

        def act_row_sums(act, s, g, dst):
            act.wait_ge(s["summed_w"], g + 1)
            alone(act)
            nc.scalar.copy(node[:, ds(g * GU, GU), dst], misc_b[:, 0:GU]).then_inc(s["sum_out"], 1)

        def sp_blocks(sp, s, g, z, dst):
            sp.wait_ge(s["blocks_out"], 2 * g + 2)
            alone(sp)
            sp.dma_start(dst[:, ds(g * GU, GU), :], block_stage[:, z]).then_inc(moved[z], 16)

        moved = [sem("moved_even"), sem("moved_odd")]

        class Near:
            def __init__(self, name, wi, wj, w2, b1_row, blocks, moments_in, moments_out, start_on):
                self.name, self.s, self.base = name, near_sems, NU * ("l0a", "l0b", "l2b").index(name)
                self.wi, self.wj, self.w2, self.b1_row, self.blocks = wi, wj, w2, b1_row, blocks
                self.moments_in, self.moments_out, self.start_on = moments_in, moments_out, start_on

        near_phases = {
            "l0a": Near("l0a", wt[:, WI[0], :], wt[:, WJ[0], :], wt[:, W2T[0], :], rows[:, R_B1[0], :],
                        adj_blocks, None, None, None),
            "l0b": Near("l0b", wt[:, WI[1], :], wt[:, WJ[1], :], wt[:, W2T[1], :], rows[:, R_B1[1], :],
                        adj_blocks, None, 0, None),
            "l2b": Near("l2b", wl[:, W1A, :], wl[:, W1B, :], wl[:, W2G, :], rows[:, R_B1L2, :],
                        w_blocks, 1, 2, None),
        }

        flat = [near_sems["flat0"], near_sems["flat1"]]
        first_in = [near_sems["first_in0"], near_sems["first_in1"], near_sems["first_in2"], near_sems["first_in3"]]

        def near_pe(pe, ph):
            s, base = ph.s, ph.base

            def turn(u, z):
                pe.wait_ge(s["staged"], u + 1)
                after(pe, s["xt_out"], u)
                after(pe, s["o_out"], u - 3)
                nc.tensor.transpose(misc_a[:, 0:P], xs[:, z, :], ident[:, :]).then_inc(s["t_filled"], 1)

            def project(u, z):
                pe.wait_ge(s["xt_out"], u + 1)
                after(pe, s["c_out"], u)
                after(pe, s["rt_out"], u - 2)
                nc.tensor.matmul(misc_b[:, 0:P], xt_flat[:, z % 2, plain_xt], ph.wi, start=True, stop=True)
                for b in range(2):
                    m = nc.tensor.matmul(misc_b[:, (1 + b) * P:(2 + b) * P], xt_flat[:, z % 2, b * P:(b + 1) * P], ph.wj,
                                         start=True, stop=True)
                m.then_inc(s["ac_filled"], 1)

            def spread_half(u, z, k, b):
                if k == 0 and b == 0:
                    pe.wait_ge(flat[z % 2], 8 * (u - z % 2) + 16)
                after(pe, s["maxed"], 8 * u + 2 * k + b - 1)
                for q in range(2):
                    m = nc.tensor.matmul(wide[b][:, q * CH:(q + 1) * CH], sel[:, 2 * b + q, :],
                                         spread[0:QROWS, z % 2, k * CH:(k + 1) * CH], start=True, stop=True)
                m.then_inc(s["spreaded"], 1)

            def weigh(u, z, k):
                pe.wait_ge(s["maxed"], 8 * u + 2 * k + 2)
                if k == 0:
                    pe.wait_ge(s["windowed"], u + 1)
                    after(pe, s["r_out"], u - 1)
                for q in range(4):
                    m = nc.tensor.matmul(sums[z % 2][32 * q:32 * q + 32, :], windows[:, z, q, k, :],
                                         pairs[:, k, q * CH:(q + 1) * CH], start=(k == 0), stop=(k == 3))
                m.then_inc(s["weighted"], 1)

            def gather(u, z):
                pe.wait_ge(s["r_out"], u + 1)
                after(pe, s["c_out"], min(u + 3, base + NU) if isinstance(u, int) else u + 3)
                after(pe, s["rt_out"], u)
                for e in range(4):
                    m = nc.tensor.matmul(misc_b[:, 0:P], r_sb[:, z % 2, e, :], pick[:, e, :],
                                         start=(e == 0), stop=(e == 3))
                    if e > 0:
                        continue
                    for b in range(2):
                        nc.tensor.matmul(misc_b[:, b * N:(b + 1) * N], c_pos[:, z, b, :],
                                         ph.blocks[:, ds(u - ph.base, 1), b * N:(b + 1) * N].rearrange("p a c -> p (a c)"),
                                         start=False, stop=False, skip_group_check=True)
                m.then_inc(s["rt_filled"], 1)

            def output(u, z, last_t):
                pe.wait_ge(s["rt_out"], u + 1)
                after(pe, s["xt_out"], last_t)
                after(pe, s["o_out"], u)
                nc.tensor.matmul(misc_a[:, 0:P], rt_sb[:, z % 2, :], ph.w2, start=True, stop=True).then_inc(s["o_filled"], 1)

            for u in range(2):
                turn(base + u, u)
                project(base + u, u)

            def body(r):
                for z in range(4):
                    u = base + 4 * r + z
                    static = isinstance(r, int)
                    ahead = not static or r < NU // 4 - 1 or z < 2
                    behind = not static or r > 0 or z > 0
                    zm, zp = (z - 1) % 4, (z + 2) % 4
                    last_t = min(u + 3, base + NU) if static else u + 3
                    for k in range(4):
                        spread_half(u, z, k, 0)
                        if k == 0 and ahead:
                            turn(u + 2, zp)
                        if k == 1 and behind:
                            gather(u - 1, zm)
                        if k == 2 and ahead:
                            project(u + 2, zp)
                        if k == 3 and behind:
                            output(u - 1, zm, last_t)
                        spread_half(u, z, k, 1)
                        if k > 0:
                            weigh(u, z, k - 1)
                        elif behind:
                            weigh(u - 1, zm, 3)
            four_unit_rounds(pe, body)
            weigh(base + NU - 1, 3, 3)
            gather(base + NU - 1, 3)
            output(base + NU - 1, 3, base + NU)

        def near_act(act, ph):
            s, base = ph.s, ph.base

            def copy_xt(u, z):
                act.wait_ge(s["t_filled"], u + 1)
                after(act, s["ac_filled"], u - 1)
                src = misc_a[:, 0:P].rearrange("p (b i) -> p b i", b=2)
                nc.scalar.copy(xt_dup[:, z % 2, :, 0, :], src)
                nc.scalar.copy(xt_dup[:, z % 2, :, 1, :], src).then_inc(s["xt_out"], 1)

            def copy_ac(u, z):
                act.wait_ge(s["ac_filled"], u + 1)
                after(act, s["split"], 5 * (u - 2) + 1)
                nc.scalar.copy(a_sb[:, z % 2, :], misc_b[:, 0:P]).then_inc(s["a_out"], 1)
                after(act, s["maxed"], 8 * (u - 3))
                after(act, s["rt_filled"], u - 3)
                src = misc_b[:, P:3 * P].rearrange("p (b d) -> p b d", b=2)
                nc.scalar.mul(c_neg[:, z], src, -1.0)
                nc.scalar.copy(c_pos[:, z], src).then_inc(s["c_out"], 1)

            def copy_r(u, z):
                act.wait_ge(s["weighted"], 4 * u + 4)
                after(act, s["rt_filled"], u - 1)
                nc.scalar.copy(r_sb[:, z % 2], sums[z % 2][:, :].rearrange("p (e d) -> p e d", e=4)).then_inc(s["r_out"], 1)

            def copy_rt(u, z):
                act.wait_ge(s["rt_filled"], u + 1)
                after(act, s["o_filled"], u - 1)
                nc.scalar.copy(rt_sb[:, z % 2, :], misc_b[:, 0:P]).then_inc(s["rt_out"], 1)

            def copy_o(u, z):
                act.wait_ge(s["o_filled"], u + 1)
                after(act, s["x_new"], u - 1)
                nc.scalar.copy(o_sb[:, z % 2, :], misc_a[:, 0:P]).then_inc(s["o_out"], 1)

            for u in range(2):
                copy_xt(base + u, u)
                copy_ac(base + u, u)

            def body(r):
                for z in range(4):
                    u = base + 4 * r + z
                    static = isinstance(r, int)
                    ahead = not static or r < NU // 4 - 1 or z < 2
                    behind = not static or r > 0 or z > 0
                    zm, zp = (z - 1) % 4, (z + 2) % 4
                    if ahead:
                        copy_xt(u + 2, zp)
                    if behind:
                        copy_r(u - 1, zm)
                        copy_rt(u - 1, zm)
                    if ahead:
                        copy_ac(u + 2, zp)
                    if behind:
                        copy_o(u - 1, zm)
            four_unit_rounds(act, body)
            copy_r(base + NU - 1, 3)
            copy_rt(base + NU - 1, 3)
            copy_o(base + NU - 1, 3)

        def near_dve(v, ph):
            s, base = ph.s, ph.base

            def form(u, z, k, b):
                v.wait_ge(s["spreaded"], 8 * u + 2 * k + b + 1)
                if k == 0 and b == 0:
                    v.wait_ge(s["c_out"], u + 1)
                if b == 0:
                    after(v, s["weighted"], 4 * u + k - 3)
                nc.vector.tensor_tensor(
                    pairs[:, k, b * 2 * CH:(b + 1) * 2 * CH].rearrange("p (i d) -> p i d", d=D),
                    wide[b][:, :].rearrange("p (i d) -> p i d", d=D),
                    c_neg[:, z, b, :].unsqueeze(1).to_broadcast([P, 8, D]), ALU.max).then_inc(s["maxed"], 1)

            def stats(u):
                v.wait_ge(s["x_new"], u + 1)
                alone(v)
                nc.vector.bn_stats(halves[:, ds(u - ph.base, 1), :].rearrange("p a d -> p (a d)"),
                                   x[:, ds(u - ph.base, 1), :].rearrange("p a d -> p (a d)")) \
                    .then_inc(stats_done[ph.moments_out], 1)

            def body(r):
                for z in range(4):
                    u = base + 4 * r + z
                    behind = ph.moments_out is not None and (not isinstance(r, int) or r > 0 or z >= 2)
                    for k in range(4):
                        for b in range(2):
                            form(u, z, k, b)
                        if behind and k == 1:
                            stats(u - 2)
            four_unit_rounds(v, body)
            if ph.moments_out is not None:
                for u in (base + NU - 2, base + NU - 1):
                    stats(u)

        def near_pool(g_eng, ph):
            s, base = ph.s, ph.base
            l0b, l2 = ph.name == "l0b", ph.name == "l2b"
            row_sums = SUM_W if l2 else SUM_ADJ
            b2 = rows[:, R_B2C, :] if l2 else rows[:, R_B2[1 if l0b else 0], :]

            def stage(u, z):
                src = x[:, ds(u - ph.base, 1), :].rearrange("p a d -> p (a d)")
                after(g_eng, s["x_new"], u - 3)
                after(g_eng, s["weighted"], 4 * (u - 3))
                alone(g_eng)
                nc.gpsimd.tensor_copy(node_now[:, z, :], node[:, ds(u - ph.base, 1), :].rearrange("p a k -> p (a k)")) \
                    .then_inc(s["noded"], 1)
                if ph.moments_in is None:
                    nc.gpsimd.tensor_copy(xs[:, z, :], src).then_inc(s["staged"], 1)
                else:
                    after(g_eng, s["staged"], u)
                    alone(g_eng)
                    nc.gpsimd.tensor_copy(x_raw, src).then_inc(s["rawed"], 1)
                    g_eng.wait_ge(s["rawed"], u - base + 1)
                    g_eng.wait_ge(s["noded"], u + 1)
                    alone(g_eng)
                    nc.gpsimd.tensor_scalar(xs[:, z, :], x_raw, node_now[:, z, MEAN:MEAN + 1],
                                            node_now[:, z, RSTD:RSTD + 1], ALU.subtract, ALU.mult) \
                        .then_inc(s["staged"], 1)
                blk = ph.blocks[:, ds(u - ph.base, 1), :].rearrange("p a (q k m) -> p (a q) k m", q=4, k=4)
                for k in range(4):
                    cp = nc.gpsimd.tensor_copy(windows[:, z, :, k, 8 * k:8 * k + 8], blk[:, :, k, :])
                cp.then_inc(s["windowed"], 1)

            def split(u, z):
                g_eng.wait_ge(s["a_out"], u + 1)
                nc.gpsimd.tensor_tensor(a_full, a_sb[:, z % 2, :], ph.b1_row, ALU.add).then_inc(s["split"], 1)
                g_eng.wait_ge(s["split"], 5 * u + 1)
                after(g_eng, s["parts_put"], 32 * (u - 1))
                alone(g_eng)
                nc.gpsimd.tensor_copy(parts[:, z % 2, 0, :], a_full).then_inc(s["split"], 1)
                g_eng.wait_ge(s["split"], 5 * u + 2)
                nc.gpsimd.tensor_tensor(a_rest, a_full, parts[:, z % 2, 0, :], ALU.subtract).then_inc(s["split"], 1)
                g_eng.wait_ge(s["split"], 5 * u + 3)
                alone(g_eng)
                nc.gpsimd.tensor_copy(parts[:, z % 2, 1, :], a_rest).then_inc(s["split"], 1)
                g_eng.wait_ge(s["split"], 5 * u + 4)
                nc.gpsimd.tensor_tensor(parts[:, z % 2, 2, :], a_rest, parts[:, z % 2, 1, :], ALU.subtract) \
                    .then_inc(s["split"], 1)

            nf = 4 if (l0b or l2) else 2
            fin_before = {"l0a": 0, "l0b": 2 * NU, "l2b": 6 * NU}[ph.name]

            def finish(u, z):
                g_eng.wait_ge(s["noded"], u + 1)
                after(g_eng, s["x_new"], u)
                if l0b:
                    g_eng.wait_ge(first_in[z], 4 * (u - base - z) + 16)
                alone(g_eng)
                nc.gpsimd.tensor_scalar(f_a, b2, node_now[:, z, row_sums:row_sums + 1], None, ALU.mult) \
                    .then_inc(s["fin"], 1)
                if l2:
                    nc.gpsimd.tensor_scalar(f_c, rows[:, R_BETA, :], node_now[:, z, SUM_ADJ:SUM_ADJ + 1], None,
                                            ALU.mult).then_inc(s["fin"], 1)
                if l0b:
                    nc.gpsimd.tensor_copy(f_c, x_first[:, z, :]).then_inc(s["fin"], 1)
                n = nf * (u - base) + fin_before
                if nf == 4:
                    g_eng.wait_ge(s["fin"], n + 2)
                    nc.gpsimd.tensor_tensor(f_d, f_a, f_c, ALU.add).then_inc(s["fin"], 1)
                    g_eng.wait_ge(s["fin"], n + 3)
                    nc.gpsimd.tensor_tensor(f_b, f_d, xs[:, z, :], ALU.add).then_inc(s["fin"], 1)
                    g_eng.wait_ge(s["fin"], n + 4)
                else:
                    g_eng.wait_ge(s["fin"], n + 1)
                    nc.gpsimd.tensor_tensor(f_b, f_a, xs[:, z, :], ALU.add).then_inc(s["fin"], 1)
                    g_eng.wait_ge(s["fin"], n + 2)
                g_eng.wait_ge(s["o_out"], u + 1)
                alone(g_eng)
                dst = x[:, ds(u - ph.base, 1), :].rearrange("p a d -> p (a d)")
                nc.gpsimd.tensor_tensor(dst, f_b, o_sb[:, z % 2, :], ALU.add).then_inc(s["x_new"], 1)

            for u in range(3):
                stage(base + u, u)
            for u in range(2):
                split(base + u, u)

            def body(r):
                for z in range(4):
                    u = base + 4 * r + z
                    static = isinstance(r, int)
                    if not static or r > 0 or z > 0:
                        finish(u - 1, (z - 1) % 4)
                    if not static or r < NU // 4 - 1 or z < 1:
                        stage(u + 3, (z + 3) % 4)
                    if not static or r < NU // 4 - 1 or z < 2:
                        split(u + 2, (z + 2) % 4)
            four_unit_rounds(g_eng, body)
            finish(base + NU - 1, 3)

        def near_sp(sp, ph):
            s, base = ph.s, ph.base

            def put_parts(u, z):
                sp.wait_ge(s["split"], 5 * (u + 1))
                alone(sp)
                after(sp, flat[z % 2], 8 * (u - z % 2))
                alone(sp)
                for par in range(2):
                    sp.dma_start(parts_dram[z % 2, par].rearrange("t i d -> i t d"), parts[par::2, z % 2, :, :]) \
                        .then_inc(s["parts_put"], 16)

            def get_parts(u, z):
                sp.wait_ge(s["parts_put"], 32 * (u + 1))
                alone(sp)
                after(sp, s["spreaded"], 8 * (u - 1))
                alone(sp)
                sp.dma_start(spread[0:QROWS, z % 2, :],
                             parts_dram[z % 2].rearrange("a t (q i) d -> (a t q) (i d)", q=4)).then_inc(flat[z % 2], 16)

            def first_input(u, z):
                after(sp, s["x_new"], u - 3)
                alone(sp)
                sp.dma_start(x_first[:, z, :], x_dram[:, ds(u - ph.base, 1), :].rearrange("p a d -> p (a d)")) \
                    .then_inc(first_in[z], 16)

            for u in range(2):
                put_parts(base + u, u)
                get_parts(base + u, u)
            if ph.name == "l0b":
                for u in range(3):
                    first_input(base + u, u)

            def body(r):
                for z in range(4):
                    u = base + 4 * r + z
                    static = isinstance(r, int)
                    if ph.name == "l0b" and (not static or r < NU // 4 - 1 or z < 1):
                        first_input(u + 3, (z + 3) % 4)
                    if not static or r < NU // 4 - 1 or z < 2:
                        put_parts(u + 2, (z + 2) % 4)
                        get_parts(u + 2, (z + 2) % 4)
            four_unit_rounds(sp, body)

        def dve_var(v, n):
            steps = norm_steps[n]
            even, odd = halves[:, :, 1], halves[:, :, 4]
            v.wait_ge(stats_done[n], NU)
            nc.vector.tensor_tensor(half_sum[:, :], even, odd, ALU.add).then_inc(steps, 1)
            nc.vector.tensor_tensor(half_gap[:, :], even, odd, ALU.subtract).then_inc(steps, 1)
            nc.vector.tensor_tensor(var[:, :], halves[:, :, 2], halves[:, :, 5], ALU.add).then_inc(steps, 1)
            v.wait_ge(steps, 3)
            nc.vector.tensor_scalar(node[:, :, MEAN], half_sum[:, :], 0.5, None, ALU.mult).then_inc(steps, 1)
            nc.vector.scalar_tensor_tensor(out=gap_sq[:, :], in0=half_gap[:, :], scalar=0.25, in1=half_gap[:, :],
                                           op0=ALU.mult, op1=ALU.mult).then_inc(steps, 1)
            v.wait_ge(steps, 5)
            nc.vector.scalar_tensor_tensor(out=var_eps[:, :], in0=var[:, :], scalar=1.0 / D, in1=gap_sq[:, :],
                                           op0=ALU.mult, op1=ALU.add).then_inc(steps, 1)

        def act_std(act, n):
            act.wait_ge(norm_steps[n], 6)
            nc.scalar.activation(std[:, :], var_eps[:, :], ACT.Sqrt, bias=cols[:, C_EPS:C_EPS + 1]) \
                .then_inc(std_done[n], 1)

        def dve_rstd(v, n):
            v.wait_ge(std_done[n], 1)
            nc.vector.reciprocal(node[:, :, RSTD], std[:, :]).then_inc(norm_ready[n], 1)

        class Feat:
            def __init__(self, name, moments_in):
                self.name, self.s, self.moments_in = name, feat[name], moments_in
                self.l1 = name == "l1a"
                self.groups_before = NG if self.l1 else 2 * NG
                if self.l1:
                    self.chain = [(WSELF, "x", "hs"), (WNB, "x", "hn"), (A1I, "hs", "p"), (A1J, "hn", "q")]
                else:
                    self.chain = [(W1A, "x", "p"), (W1B, "x", "q")]
                self.steps = 1 + len(self.chain)

        feat_phases = {"l1a": Feat("l1a", 0), "l2a": Feat("l2a", 1)}
        NQ = NU // QU
        TILES = 16
        LIN_AT = (1, 4, 7, 10, 13)

        def group_rounds(eng, body):
            body(0)
            with eng.Fori(1, NG - 1) as g:
                body(g)
            body(NG - 1)

        def feat_pe(pe, ph):
            s = ph.s
            src_of = {"x": xt4, "hs": hs4, "hn": hn4}

            def project(quad, j):
                after(pe, s["lin_out"], ph.steps * quad + j)
                if j == 0:
                    pe.wait_ge(s["staged"], QU * (quad + 1))
                    for n in range(QU):
                        m = nc.tensor.transpose(misc_a[:, n * P:(n + 1) * P], xs4[:, n, :], ident[:, :])
                else:
                    w, src, _ = ph.chain[j - 1]
                    m = nc.tensor.matmul(misc_a[:, :], wl[:, w, :], src_of[src], start=True, stop=True)
                m.then_inc(s["lin_filled"], 1)

            def score(quad, qz, tau, gz):
                tile, t = TILES * quad + tau, TILES * qz + tau
                pe.wait_ge(s["formed"], tile + 1)
                for q in range(4):
                    m = nc.tensor.matmul(sums[gz][32 * q:32 * q + 32, :], window_a2[:, 31 - t:63 - t],
                                         pairs[:, tau % 4, q * CH:(q + 1) * CH], start=False, stop=(t == 31))
                m.then_inc(s["scored"], 1)

            def score_c(quad, qz, gz):
                for bb in range(8):
                    t = 16 * qz + 2 * bb
                    mov = q4[:, qz, bb * N:(bb + 1) * N].unsqueeze(1).to_broadcast([P, 8, N])
                    for q in range(4):
                        nc.tensor.matmul(sums[gz][32 * q:32 * q + 32, :].rearrange("p (i j) -> p i j", j=N),
                                         window_two[:, 31 - t:63 - t], mov, start=(t == 0), stop=False)

            def square_in(quad, tau, h):
                tile = TILES * quad + tau
                if h == 0:
                    pe.wait_ge(s["relued"], tile + 1)
                after(pe, s["squared"], 2 * tile + h - 1)
                for c in range(2):
                    m = nc.tensor.matmul(wide[h][:, c * CH:(c + 1) * CH], wl[:, W2, :],
                                         pairs[:, tau % 4, (2 * h + c) * CH:(2 * h + c + 1) * CH],
                                         start=True, stop=True)
                m.then_inc(s["y_filled"], 1)

            def mean(tile, t, gz):
                pe.wait_ge(s["squared"], 2 * tile + 2)
                for q in range(4):
                    m = nc.tensor.matmul(sums[gz][32 * q:32 * q + 32, :], window_mean[:, 31 - t:63 - t],
                                         squares[:, q // 2, (q % 2) * CH:(q % 2 + 1) * CH],
                                         start=(t == 0), stop=(t == 31))
                m.then_inc(s["scored"], 1)

            def finish(g, gz):
                pe_turn(pe, s, g, weights, s["weighed"], g + 1)

            for j in range(ph.steps):
                project(0, j)

            def body_gz(g, gz):
                for qz in range(2):
                    quad = 2 * g + qz
                    static = isinstance(g, int)
                    ahead = not static or quad + 1 < NQ
                    behind = not static or g >= 1
                    pe.wait_ge(s["lin_out"], ph.steps * (quad + 1))
                    if qz == 0:
                        after(pe, s["shifted"] if ph.l1 else s["std_out"], g - 1)
                    if ph.l1:
                        score_c(quad, qz, gz)
                    for tau in range(TILES):
                        t = TILES * qz + tau
                        if ph.l1:
                            score(quad, qz, tau, gz)
                        else:
                            square_in(quad, tau, 0)
                            if t > 0:
                                mean(TILES * quad + tau - 1, t - 1, gz)
                            elif behind:
                                mean(TILES * quad + tau - 1, 31, 1 - gz)
                            square_in(quad, tau, 1)
                        if ahead and tau in LIN_AT[:ph.steps]:
                            project(quad + 1, LIN_AT.index(tau))
                        if behind and qz == 0 and tau == 12:
                            finish(g - 1, 1 - gz)
                        if behind and qz == 0 and tau == 14:
                            pe_row_sums(pe, s, g - 1, 1 - gz)

            def body(r):
                for gz in range(2):
                    body_gz(2 * r + gz, gz)
            two_rounds(pe, body, NG)
            if not ph.l1:
                mean(32 * NG - 1, 31, 1)
            finish(NG - 1, 1)
            pe_row_sums(pe, s, NG - 1, 1)

        def feat_act(act, ph):
            s = ph.s
            dst_of = {"hs": hs4, "hn": hn4}

            def project(quad, qz, j):
                act.wait_ge(s["lin_filled"], ph.steps * quad + j + 1)
                if j == 0:
                    nc.scalar.copy(xt4, misc_a[:, :]).then_inc(s["lin_out"], 1)
                    return
                w, _, dst = ph.chain[j - 1]
                if dst in ("p", "q"):
                    after(act, s["formed"], TILES * (quad - 1))
                    if ph.l1 and dst == "q":
                        after(act, s["scored"], TILES * (quad - 1))
                if dst == "q":
                    out_q = q4[:, qz, :]
                    if ph.l1:
                        nc.scalar.mul(out_q, misc_a[:, :], -1.0).then_inc(s["lin_out"], 1)
                    else:
                        nc.scalar.copy(out_q, misc_a[:, :]).then_inc(s["lin_out"], 1)
                    return
                bias = {"hs": C_BSELF, "hn": C_BNB, "p": C_A1B if ph.l1 else C_B1}[dst]
                d = p4[:, qz, :] if dst == "p" else dst_of[dst]
                nc.scalar.activation(d, misc_a[:, :], ACT.Identity, bias=cols[:, bias:bias + 1]).then_inc(s["lin_out"], 1)

            def relu(tile, slot):
                act.wait_ge(s["formed"], tile + 1)
                nc.scalar.activation(pairs[:, slot, :], pairs[:, slot, :], ACT.Relu).then_inc(s["relued"], 1)

            def square(tile, h):
                act.wait_ge(s["y_filled"], 2 * tile + h + 1)
                after(act, s["scored"], tile)
                nc.scalar.activation(squares[:, h, :], wide[h][:, :], ACT.Square,
                                     bias=cols[:, C_B2C:C_B2C + 1]).then_inc(s["squared"], 1)

            def weigh(g, gz):
                if ph.l1:
                    act.wait_ge(s["cut"], g + 1)
                    after(act, s["weighed"], g)
                    nc.scalar.activation(score_a, score_b, ACT.Exp).then_inc(s["exped"], 1)
                else:
                    act.wait_ge(s["scored"], 32 * (g + 1))
                    after(act, s["inverted"], g)
                    nc.scalar.activation(score_a, sums[gz][:, :], ACT.Sqrt,
                                         bias=cols[:, C_EPS:C_EPS + 1]).then_inc(s["std_out"], 1)

            for j in range(ph.steps):
                project(0, 0, j)
            if not ph.l1:
                relu(0, 0)

            def body_gz(g, gz):
                for qz in range(2):
                    quad = 2 * g + qz
                    static = isinstance(g, int)
                    ahead = not static or quad + 1 < NQ
                    behind = not static or g >= 1
                    for tau in range(TILES):
                        tile = TILES * quad + tau
                        if not ph.l1:
                            if not static or tile + 1 < 32 * NG:
                                relu(tile + 1, (tau + 1) % 4)
                            square(tile, 0)
                            square(tile, 1)
                        if ahead and tau in LIN_AT[:ph.steps]:
                            project(quad + 1, 1 - qz, LIN_AT.index(tau))
                        if behind and qz == 0 and tau == 3:
                            weigh(g - 1, 1 - gz)
                        if behind and qz == 0 and tau == 12:
                            act_blocks(act, s, g - 1, 1 - gz, ph.groups_before)
                        if behind and qz == 0 and tau == 14:
                            act_row_sums(act, s, g - 1, SUM_W)

            def body(r):
                for gz in range(2):
                    body_gz(2 * r + gz, gz)
            two_rounds(act, body, NG)
            weigh(NG - 1, 1)
            act_blocks(act, s, NG - 1, 1, ph.groups_before)
            act_row_sums(act, s, NG - 1, SUM_W)

        def feat_dve(v, ph):
            s = ph.s

            def form(quad, qz, tau):
                tile = TILES * quad + tau
                after(v, s["scored"] if ph.l1 else s["y_filled"], tile - 3 if ph.l1 else 2 * (tile - 3))
                bb, ih = tau // 2, tau % 2
                i0 = bb * N + ih * 32
                a = p4[:, qz, i0:i0 + 32].unsqueeze(2).to_broadcast([P, 32, N])
                c = q4[:, qz, bb * N:(bb + 1) * N].unsqueeze(1).to_broadcast([P, 32, N])
                nc.vector.tensor_tensor(pairs[:, tau % 4, :].rearrange("p (i j) -> p i j", j=N), a, c,
                                        ALU.max if ph.l1 else ALU.add).then_inc(s["formed"], 1)

            def r3(t):
                return t.rearrange("p (i j) -> p i j", j=N)

            def b3(t):
                return t.unsqueeze(2).to_broadcast([P, 8, N])

            def shift(g, gz):
                v.wait_ge(s["scored"], 32 * (g + 1))
                v.wait_ge(s["masked"], 3 * (g + 1))
                nc.vector.scalar_tensor_tensor(out=score_a, in0=sums[gz][:, :], scalar=cols[:, C_A2B:C_A2B + 1],
                                               in1=mask, op0=ALU.add, op1=ALU.mult).then_inc(s["shifted"], 1)

            def top(g):
                v.wait_ge(s["topped"], 2 * g + 1)
                nc.vector.tensor_reduce(row_max, r3(score_b), AX.X, ALU.max).then_inc(s["topped"], 1)

            def cut(g):
                v.wait_ge(s["topped"], 2 * g + 2)
                nc.vector.tensor_tensor(r3(score_b), r3(score_b), b3(row_max), ALU.subtract).then_inc(s["cut"], 1)

            def total(g):
                v.wait_ge(s["exped"], g + 1)
                nc.vector.tensor_reduce(row_sum, r3(score_a), AX.X, ALU.add).then_inc(s["totalled"], 1)

            def invert(g):
                if ph.l1:
                    v.wait_ge(s["totalled"], g + 1)
                    nc.vector.reciprocal(row_inv, row_sum).then_inc(s["inverted"], 1)
                else:
                    v.wait_ge(s["std_out"], g + 1)
                    after(v, s["weighed"], g)
                    nc.vector.reciprocal(score_b, score_a).then_inc(s["inverted"], 1)

            def end_step(g, gz, tau):
                if ph.l1:
                    if tau == 1:
                        shift(g, gz)
                    if tau == 2:
                        top(g)
                    if tau == 3:
                        cut(g)
                    if tau == 5:
                        total(g)
                    if tau == 6:
                        invert(g)
                elif tau == 6:
                    invert(g)

            v.wait_ge(s["lin_out"], ph.steps)

            def body_gz(g, gz):
                for qz in range(2):
                    quad = 2 * g + qz
                    behind = not isinstance(g, int) or g >= 1
                    v.wait_ge(s["lin_out"], ph.steps * (quad + 1))
                    for tau in range(TILES):
                        form(quad, qz, tau)
                        if behind and qz == 0:
                            end_step(g - 1, 1 - gz, tau)

            def body(r):
                for gz in range(2):
                    body_gz(2 * r + gz, gz)
            two_rounds(v, body, NG)
            for tau in range(8):
                end_step(NG - 1, 1, tau)

        def feat_pool(g_eng, ph):
            s = ph.s

            def stage(quad):
                after(g_eng, s["lin_filled"], ph.steps * (quad - 1) + 1)
                after(g_eng, s["staged"], QU * quad)
                alone(g_eng)
                nc.gpsimd.tensor_copy(xs4_raw, x[:, ds(QU * quad, QU), :]).then_inc(s["rawed"], 1)
                nc.gpsimd.tensor_copy(node_now[:, :, :], node[:, ds(QU * quad, QU), :]).then_inc(s["rawed"], 1)
                g_eng.wait_ge(s["rawed"], 2 * (quad + 1))
                alone(g_eng)
                for n in range(QU):
                    nc.gpsimd.tensor_scalar(xs4[:, n, :], xs4_raw[:, n, :], node_now[:, n, MEAN:MEAN + 1],
                                            node_now[:, n, RSTD:RSTD + 1], ALU.subtract, ALU.mult) \
                        .then_inc(s["staged"], 1)

            def masks(g, gz):
                g_eng.wait_ge([s["adj_in0"], s["adj_in1"]][gz], 32 * (g - gz) + 64)
                alone(g_eng)
                nc.gpsimd.tensor_scalar(is_zero, adj_rows[:, gz, :], 0.0, None, ALU.is_equal).then_inc(s["masked"], 1)
                g_eng.wait_ge(s["masked"], 3 * g + 1)
                alone(g_eng)
                nc.gpsimd.tensor_scalar(mask, is_zero, -1.0, 1.0, ALU.mult, ALU.add).then_inc(s["masked"], 1)
                nc.gpsimd.tensor_scalar(fill, is_zero, -NEG, None, ALU.mult).then_inc(s["masked"], 1)

            def fill_in(g):
                g_eng.wait_ge(s["shifted"], g + 1)
                nc.gpsimd.tensor_tensor(score_b, score_a, fill, ALU.add).then_inc(s["topped"], 1)

            def weigh(g, gz):
                after(g_eng, s["turned"], g)
                g_eng.wait_ge(s["inverted"], g + 1)
                if ph.l1:
                    nc.gpsimd.tensor_tensor(weights.rearrange("p (i j) -> p i j", j=N),
                                            score_a.rearrange("p (i j) -> p i j", j=N),
                                            row_inv.unsqueeze(2).to_broadcast([P, 8, N]), ALU.mult) \
                        .then_inc(s["weighed"], 1)
                else:
                    g_eng.wait_ge([s["adj_in0"], s["adj_in1"]][gz], 32 * (g - gz) + 64)
                    nc.gpsimd.tensor_tensor(weights, score_b, adj_rows[:, gz, :], ALU.mult).then_inc(s["weighed"], 1)

            stage(0)

            def body_gz(g, gz):
                static = isinstance(g, int)
                stage(2 * g + 1)
                if not static or g >= 1:
                    if ph.l1:
                        masks(g - 1, 1 - gz)
                        fill_in(g - 1)
                    weigh(g - 1, 1 - gz)
                if not static or g + 1 < NG:
                    stage(2 * g + 2)

            def body(r):
                for gz in range(2):
                    body_gz(2 * r + gz, gz)
            two_rounds(g_eng, body, NG)
            if ph.l1:
                masks(NG - 1, 1)
                fill_in(NG - 1)
            weigh(NG - 1, 1)

        def feat_sp(sp, ph):
            s = ph.s

            def body(r):
                for gz in range(2):
                    g = 2 * r + gz
                    after(sp, s["weighed"], g - 1)
                    alone(sp)
                    load_adj_rows(sp, g, gz, [s["adj_in0"], s["adj_in1"]][gz])
                    if not isinstance(g, int) or g >= 1:
                        sp_blocks(sp, s, g - 1, 1 - gz, w_blocks)
            two_rounds(sp, body, NG)
            sp_blocks(sp, s, NG - 1, 1, w_blocks)

        class Agg:
            def __init__(self, name, blocks, w_self, w_nb, moments_in, moments_out):
                self.name, self.s, self.base = name, agg_sems, NU * ("l1b", "l3").index(name)
                self.blocks, self.w_self, self.w_nb = blocks, w_self, w_nb
                self.moments_in, self.moments_out = moments_in, moments_out
                self.l1 = name == "l1b"

        agg_phases = {"l1b": Agg("l1b", w_blocks, wl[:, WSELF, :], wl[:, WNB, :], 0, 1),
                      "l3": Agg("l3", adj_blocks, wt[:, L3T, :], wt[:, L3T, :], 2, 3)}

        def agg_pool(g_eng, ph):
            s, base = ph.s, ph.base

            def stage(u, z):
                after(g_eng, s["x_new"], u - 3)
                after(g_eng, s["o_filled"], u - 1)
                after(g_eng, s["staged"], u if ph.l1 else 2 * u - base)
                alone(g_eng)
                nc.gpsimd.tensor_copy(x_raw2, x[:, ds(u - ph.base, 1), :].rearrange("p a d -> p (a d)")).then_inc(s["rawed"], 1)
                nc.gpsimd.tensor_copy(node_now[:, z, :], node[:, ds(u - ph.base, 1), :].rearrange("p a k -> p (a k)")) \
                    .then_inc(s["rawed"], 1)
                nc.gpsimd.tensor_copy(block_now[:, z % 2, :], ph.blocks[:, ds(u - ph.base, 1), :].rearrange("p a c -> p (a c)")) \
                    .then_inc(s["block_in"], 1)
                g_eng.wait_ge(s["rawed"], 2 * u + 2)
                alone(g_eng)
                nc.gpsimd.tensor_scalar(xs[:, z, :], x_raw2, node_now[:, z, MEAN:MEAN + 1],
                                        node_now[:, z, RSTD:RSTD + 1], ALU.subtract, ALU.mult).then_inc(s["staged"], 1)
                if not ph.l1:
                    g_eng.wait_ge(s["staged"], 2 * u + 1 - base)
                    after(g_eng, s["t_filled"], u - 1)
                    alone(g_eng)
                    nc.gpsimd.tensor_scalar(xd[:, z % 2, :], xs[:, z, :], node_now[:, z, DINV:DINV + 1], None,
                                            ALU.mult).then_inc(s["staged"], 1)

            def bias(u, z):
                g_eng.wait_ge(s["n_out"], u + 1)
                after(g_eng, s["o_filled"], u - 1)
                b = rows[:, R_BNB, :].unsqueeze(1).to_broadcast([P, 2, D])
                nc.gpsimd.tensor_tensor(n_full[:, z % 2], n_sb[:, z % 2], b, ALU.add).then_inc(s["n_biased"], 1)

            stage(base, 0)

            def body(r):
                for z in range(4):
                    u = base + 4 * r + z
                    if not isinstance(r, int) or r < NU // 4 - 1 or z < 3:
                        stage(u + 1, (z + 1) % 4)
                    if ph.l1:
                        bias(u, z)
            four_unit_rounds(g_eng, body)

        def agg_pe(pe, ph):
            s, base = ph.s, ph.base
            def turn(u, z):
                pe.wait_ge(s["staged"], u + 1 if ph.l1 else 2 * (u + 1) - base)
                after(pe, s["xt_out"], u)
                src = xs[:, z, :] if ph.l1 else xd[:, z % 2, :]
                nc.tensor.transpose(misc_a[:, 0:P], src, ident[:, :]).then_inc(s["t_filled"], 1)

            def neighbours(u, z):
                pe.wait_ge(s["xt_out"], u + 1)
                after(pe, s["n_out"], u)
                for b in range(2):
                    m = nc.tensor.matmul(misc_b[:, b * D:(b + 1) * D], xt_flat[:, z % 2, b * P:(b + 1) * P], ph.w_nb,
                                         start=True, stop=True)
                m.then_inc(s["n_filled"], 1)

            def combine(u, z):
                after(pe, s["o_sum"], u - 1)
                pe.wait_ge(s["block_in"], u + 1)
                if ph.l1:
                    pe.wait_ge(s["n_biased"], u + 1)
                else:
                    pe.wait_ge(s["n_out"], u + 1)
                n = n_full if ph.l1 else n_sb
                for b in range(2):
                    nc.tensor.matmul(sums[z % 2][b * N:(b + 1) * N, 0:D], block_now[:, z % 2, b * N:(b + 1) * N],
                                     n[:, z % 2, b, :], start=True, stop=False)
                m = nc.tensor.matmul(sums[z % 2][:, 0:D], xt_flat[:, z % 2, plain_xt], ph.w_self,
                                     start=False, stop=True)
                m.then_inc(s["o_filled"], 1)

            turn(base, 0)

            def body(r):
                for z in range(4):
                    u = base + 4 * r + z
                    neighbours(u, z)
                    if not isinstance(r, int) or r < NU // 4 - 1 or z < 3:
                        turn(u + 1, (z + 1) % 4)
                    combine(u, z)
            four_unit_rounds(pe, body)

        def agg_act(act, ph):
            s, base = ph.s, ph.base

            def body(r):
                for z in range(4):
                    u = base + 4 * r + z
                    act.wait_ge(s["t_filled"], u + 1)
                    after(act, s["o_filled"], u - 1)
                    src = misc_a[:, 0:P].rearrange("p (b i) -> p b i", b=2)
                    nc.scalar.copy(xt_dup[:, z % 2, :, 0, :], src)
                    nc.scalar.copy(xt_dup[:, z % 2, :, 1, :], src).then_inc(s["xt_out"], 1)
                    act.wait_ge(s["n_filled"], u + 1)
                    if ph.l1:
                        after(act, s["n_biased"], u - 1)
                    nc.scalar.copy(n_sb[:, z % 2], misc_b[:, 0:2 * D].rearrange("p (b d) -> p b d", b=2)) \
                        .then_inc(s["n_out"], 1)
            four_unit_rounds(act, body)

        def agg_dve(v, ph):
            s, base = ph.s, ph.base

            def finish(u, z):
                v.wait_ge(s["o_filled"], u + 1)
                o = sums[z % 2][:, 0:D]
                if ph.l1:
                    nc.vector.tensor_tensor(agg_a[:, z % 2, :], o, rows[:, R_BSELF, :], ALU.add).then_inc(s["o_sum"], 1)
                else:
                    nc.vector.scalar_tensor_tensor(out=agg_a[:, z % 2, :], in0=o, scalar=node_now[:, z, DINV:DINV + 1],
                                                   in1=rows[:, R_L3B, :], op0=ALU.mult, op1=ALU.add) \
                        .then_inc(s["o_sum"], 1)
                v.wait_ge(s["o_sum"], u + 1)
                nc.vector.scalar_tensor_tensor(out=x[:, ds(u - ph.base, 1), :].rearrange("p a d -> p (a d)"),
                                               in0=agg_a[:, z % 2, :], scalar=0.0, in1=xs[:, z, :],
                                               op0=ALU.max, op1=ALU.add).then_inc(s["x_new"], 1)
                v.wait_ge(s["x_new"], u + 1)
                alone(v)
                nc.vector.bn_stats(halves[:, ds(u - ph.base, 1), :].rearrange("p a d -> p (a d)"),
                                   x[:, ds(u - ph.base, 1), :].rearrange("p a d -> p (a d)")) \
                    .then_inc(stats_done[ph.moments_out], 1)

            def body(r):
                for z in range(4):
                    finish(base + 4 * r + z, z)
            four_unit_rounds(v, body)

        block = ctx.enter_context(nc.Block())
        NRAW, NFLAT, NROW, NCOL = 7, 8, 11, 6

        @block.sync
        def _(sp):
            def vec(name, l=None):
                v = inp[name]
                return v if l is None else v[l]
            sp.dma_start(ident[:, :], ident_d).then_inc(loaded["const"], 16)
            load_adj_rows(sp, 0, 0, first["adj_in0"])
            load_adj_rows(sp, 1, 1, first["adj_in1"])
            for h in range(4):
                sp.dma_start(x[:, 16 * h:16 * h + 16, :], x_dram[:, 16 * h:16 * h + 16, :]).then_inc(loaded["x"], 16)
            for l in range(2):
                sp.dma_start(wraw[:, 3 * l, :], inp["L0_gnn_w1"][l, :, 0:D]).then_inc(loaded["raw"], 16)
                sp.dma_start(wraw[:, 3 * l + 1, :], inp["L0_gnn_w1"][l, :, D:2 * D]).then_inc(loaded["raw"], 16)
                sp.dma_start(wraw[:, 3 * l + 2, :], inp["L0_gnn_w2"][l]).then_inc(loaded["raw"], 16)
            sp.dma_start(wraw[:, 6, :], inp["L3_gnn_W"]).then_inc(loaded["raw"], 16)
            sp.dma_start(pick[:, :, :], pick_d).then_inc(loaded["const"], 16)
            sp.dma_start(sel_f[:, :, :], sel_d).then_inc(loaded["const"], 16)
            for k, v in ((WSELF, inp["L1_gnn_W_self_w"]), (WNB, inp["L1_gnn_W_nb_w"]),
                         (A1I, inp["L1_gnn_A1_w"][0:D, :]), (A1J, inp["L1_gnn_A1_w"][D:2 * D, :]),
                         (W1A, inp["L2_gnn_W1"][0:D, :]), (W1B, inp["L2_gnn_W1"][D:2 * D, :]),
                         (W2G, inp["L2_gnn_W2"])):
                sp.dma_start(wl[:, k, :], v).then_inc(loaded["flat"], 16)
            for k, v in ((R_B1[0], inp["L0_gnn_b1"][0:1, :]), (R_B1[1], inp["L0_gnn_b1"][1:2, :]),
                         (R_B2[0], inp["L0_gnn_b2"][0:1, :]), (R_B2[1], inp["L0_gnn_b2"][1:2, :]),
                         (R_BSELF, inp["L1_gnn_W_self_b"][None, :]), (R_BNB, inp["L1_gnn_W_nb_b"][None, :]),
                         (R_B2C, inp["L2_gnn_b2"][None, :]), (R_GAMMA, inp["L2_gnn_gamma"][None, :]),
                         (R_BETA, inp["L2_gnn_beta"][None, :]), (R_L3B, inp["L3_gnn_b"][None, :]),
                         (R_B1L2, inp["L2_gnn_b1"][None, :])):
                sp.dma_start(rows[:, k, :], v.to_broadcast([P, D])).then_inc(loaded["row"], 16)
            for k, v in ((C_BSELF, inp["L1_gnn_W_self_b"][:, None]), (C_BNB, inp["L1_gnn_W_nb_b"][:, None]),
                         (C_A1B, inp["L1_gnn_A1_b"][:, None]), (C_B1, inp["L2_gnn_b1"][:, None]),
                         (C_A2, inp["L1_gnn_A2_w"]),
                         (C_A2B, inp["L1_gnn_A2_b"][None, :].to_broadcast([P, 1]))):
                sp.dma_start(cols[:, k:k + 1], v).then_inc(loaded["col"], 16)
            for g in range(NG):
                sp_blocks(sp, first, g, g % 2, adj_blocks)
                if g + 2 < NG:
                    load_adj_rows(sp, g + 2, g % 2, [first["adj_in0"], first["adj_in1"]][g % 2])
            near_sp(sp, near_phases["l0a"])
            near_sp(sp, near_phases["l0b"])
            feat_sp(sp, feat_phases["l1a"])
            feat_sp(sp, feat_phases["l2a"])
            near_sp(sp, near_phases["l2b"])
            for g in range(NG):
                sp.wait_ge(y_ready, GU * (g + 1))
                sp.dma_start(out_dram[:, GU * g:GU * g + GU, :], y_out[:, g % 2]).then_inc(out_done[g % 2], 16)
            for z in range(2):
                sp.wait_ge(out_done[z], 8 * NG)

        def pool_windows(g_eng, phase_ready):
            nc.gpsimd.memset(windows.rearrange("p z q k m -> p (z q k m)"), 0.0).then_inc(phase_ready, 1)

        windows_zero = [sem("windows_zero0"), sem("windows_zero1")]

        @block.gpsimd
        def _(g_eng):
            nc.gpsimd.memset(block_stage[:, :, :, :].rearrange("p z u c -> p (z u c)"), 0.0).then_inc(consts, 1)
            for w in (window_a2, window_two, window_mean):
                nc.gpsimd.memset(w[:, :], 0.0).then_inc(consts, 1)
            nc.gpsimd.memset(ones[:, :], 1.0).then_inc(consts, 1)
            nc.gpsimd.memset(node[:, :, :], 0.0).then_inc(node_zero, 1)
            g_eng.wait_ge(consts, 5)
            nc.gpsimd.memset(window_mean[:, 31:32], 1.0 / D).then_inc(consts, 1)
            g_eng.wait_ge(loaded["col"], 16 * NCOL)
            nc.gpsimd.memset(cols[:, C_EPS:C_EPS + 1], EPS).then_inc(consts, 1)
            nc.gpsimd.tensor_copy(window_a2[:, 31:32], cols[:, C_A2:C_A2 + 1]).then_inc(consts, 1)
            for k in (31, 32):
                nc.gpsimd.tensor_scalar(window_two[:, k:k + 1], cols[:, C_A2:C_A2 + 1], -1.0, None, ALU.mult) \
                    .then_inc(consts, 1)
            g_eng.wait_ge(loaded["const"], 48)
            nc.gpsimd.tensor_copy(sel[:, :, :], sel_f[:, :, :]).then_inc(consts, 1)
            pool_windows(g_eng, windows_zero[0])
            g_eng.wait_ge(windows_zero[0], 1)
            g_eng.wait_ge(loaded["x"], 64)
            g_eng.wait_ge(loaded["row"], 16 * NROW)
            for z in range(2):
                g_eng.wait_ge(moved[z], 1 * 8 * NG)
            g_eng.wait_ge(first["sum_out"], NG)
            near_pool(g_eng, near_phases["l0a"])
            g_eng.wait_ge(near_sems["x_new"], NU)
            near_pool(g_eng, near_phases["l0b"])
            g_eng.wait_ge(norm_ready[0], 1)
            feat_pool(g_eng, feat_phases["l1a"])
            for z in range(2):
                g_eng.wait_ge(moved[z], 2 * 8 * NG)
            g_eng.wait_ge(feat["l1a"]["sum_out"], NG)
            agg_pool(g_eng, agg_phases["l1b"])
            g_eng.wait_ge(norm_ready[1], 1)
            feat_pool(g_eng, feat_phases["l2a"])
            for z in range(2):
                g_eng.wait_ge(moved[z], 3 * 8 * NG)
            g_eng.wait_ge(feat["l2a"]["sum_out"], NG)
            pool_windows(g_eng, windows_zero[1])
            g_eng.wait_ge(windows_zero[1], 1)
            g_eng.wait_ge(dinv_steps, 3)
            near_pool(g_eng, near_phases["l2b"])
            g_eng.wait_ge(norm_ready[2], 1)
            agg_pool(g_eng, agg_phases["l3"])
            g_eng.wait_ge(norm_ready[3], 1)
            for g in range(NG):
                if g >= 2:
                    g_eng.wait_ge(out_done[g % 2], 16 * (g // 2))
                for n in range(GU):
                    u = GU * g + n
                    nc.gpsimd.tensor_scalar(y_out[:, g % 2, n, :], x[:, u, :], node[:, u, MEAN:MEAN + 1],
                                            node[:, u, RSTD:RSTD + 1], ALU.subtract, ALU.mult).then_inc(y_ready, 1)

        @block.vector
        def _(v):
            v.wait_ge(loaded["flat"], 16 * 7)
            v.wait_ge(loaded["row"], 16 * NROW)
            nc.vector.tensor_reduce(w2_mean[:, 0:1], wl[:, W2G, :], AX.X, ALU.add).then_inc(prep, 1)
            nc.vector.tensor_reduce(w2_mean[:, 1:2], rows[:, R_B2C, :], AX.X, ALU.add).then_inc(prep, 1)
            v.wait_ge(prep, 2)
            nc.vector.tensor_scalar(w2_mean[:, :], w2_mean[:, :], 1.0 / D, None, ALU.mult).then_inc(prep, 1)
            v.wait_ge(prep, 3)
            nc.vector.tensor_scalar(wl[:, W2, :], wl[:, W2G, :], w2_mean[:, 0:1], None, ALU.subtract).then_inc(prep, 1)
            nc.vector.tensor_scalar(rows[:, 11, :], rows[:, R_B2C, :], w2_mean[:, 1:2], None, ALU.subtract) \
                .then_inc(prep, 1)
            v.wait_ge(prep, 5)
            nc.vector.tensor_tensor(wl[:, W2G, :], wl[:, W2, :], rows[:, R_GAMMA, :], ALU.mult).then_inc(prep, 1)
            nc.vector.tensor_tensor(rows[:, R_B2C, :], rows[:, 11, :], rows[:, R_GAMMA, :], ALU.mult).then_inc(prep, 1)
            near_dve(v, near_phases["l0a"])
            near_dve(v, near_phases["l0b"])
            dve_var(v, 0)
            dve_rstd(v, 0)
            feat_dve(v, feat_phases["l1a"])
            agg_dve(v, agg_phases["l1b"])
            dve_var(v, 1)
            dve_rstd(v, 1)
            feat_dve(v, feat_phases["l2a"])
            v.wait_ge(dinv_steps, 2)
            nc.vector.reciprocal(node[:, :, DINV], degree[:, :]).then_inc(dinv_steps, 1)
            near_dve(v, near_phases["l2b"])
            dve_var(v, 2)
            dve_rstd(v, 2)
            agg_dve(v, agg_phases["l3"])
            dve_var(v, 3)
            dve_rstd(v, 3)

        @block.scalar
        def _(act):
            act.wait_ge(consts, 11)
            for k in range(7):
                act.wait_ge(wt_filled, k + 1)
                nc.scalar.copy(wt[:, k, :], misc_a[:, 0:P]).then_inc(wt_out, 1)
            act.wait_ge(b2c_filled, 1)
            nc.scalar.copy(cols[:, C_B2C:C_B2C + 1], misc_a[:, 0:1]).then_inc(b2c_out, 1)
            act.wait_ge(node_zero, 1)
            for g in range(NG):
                act_blocks(act, first, g, g % 2, 0)
                act_row_sums(act, first, g, SUM_ADJ)
            near_act(act, near_phases["l0a"])
            near_act(act, near_phases["l0b"])
            act_std(act, 0)
            feat_act(act, feat_phases["l1a"])
            agg_act(act, agg_phases["l1b"])
            act_std(act, 1)
            feat_act(act, feat_phases["l2a"])
            act.wait_ge(first["sum_out"], NG)
            nc.scalar.activation(degree[:, :], node[:, :, SUM_ADJ], ACT.Copy, bias=1.0 + 1e-6).then_inc(dinv_steps, 1)
            act.wait_ge(dinv_steps, 1)
            nc.scalar.activation(degree[:, :], degree[:, :], ACT.Sqrt).then_inc(dinv_steps, 1)
            near_act(act, near_phases["l2b"])
            act_std(act, 2)
            agg_act(act, agg_phases["l3"])
            act_std(act, 3)

        @block.tensor
        def _(pe):
            pe.wait_ge(loaded["const"], 48)
            pe.wait_ge(loaded["raw"], 16 * NRAW)
            pe.wait_ge(consts, 11)
            for k in range(7):
                after(pe, wt_out, k)
                nc.tensor.transpose(misc_a[:, 0:P], wraw[:, k, :], ident[:, :]).then_inc(wt_filled, 1)
            pe.wait_ge(prep, 7)
            pe.wait_ge(wt_out, 7)
            nc.tensor.matmul(misc_a[:, 0:1], rows[0:1, 11, :], ones[0:1, :], start=True, stop=True) \
                .then_inc(b2c_filled, 1)
            pe.wait_ge(b2c_out, 1)
            for g in range(NG):
                pe_turn(pe, first, g, adj_rows[:, g % 2, :], [first["adj_in0"], first["adj_in1"]][g % 2], 64 * (g // 2 + 1))
                pe_row_sums(pe, first, g, g % 2)
            pe.wait_ge(first["sum_out"], NG)
            near_pe(pe, near_phases["l0a"])
            near_pe(pe, near_phases["l0b"])
            feat_pe(pe, feat_phases["l1a"])
            agg_pe(pe, agg_phases["l1b"])
            feat_pe(pe, feat_phases["l2a"])
            near_pe(pe, near_phases["l2b"])
            agg_pe(pe, agg_phases["l3"])


def constants():
    ident = np.eye(P, dtype=np.float32)
    pick = np.zeros((P, 4, P), np.float32)
    for p in range(P):
        pick[p, (p % N // 2) % 4, p] = 1.0
    sel = np.zeros((QROWS, 4, P), np.float32)
    for q in range(4):
        for par in range(2):
            for part in range(3):
                sel[(3 * par + part) * 4 + q, q, par * N:(par + 1) * N] = 1.0
    return {"ident_d": ident, "pick_d": pick, "sel_d": sel}


def kernel(**inputs):
    import concourse.bacc as bacc
    from concourse.bass_utils import run_bass_kernel_spmd

    nc = bacc.Bacc("TRN2", target_bir_lowering=False, num_devices=1)
    arrays, aps = {}, {}
    for name in INPUTS:
        arrays[f"in_{name}"] = np.ascontiguousarray(inputs[name])
    for name, value in constants().items():
        arrays[f"in_{name}"] = value
    for name, a in arrays.items():
        aps[name[3:]] = nc.dram_tensor(name, a.shape, mybir.dt.from_np(a.dtype), kind="ExternalInput").ap()
    out = nc.dram_tensor("out", (NB, N, D), F32, kind="ExternalOutput").ap()
    parts_dram = nc.dram_tensor("parts_dram", (2, 2, 3, N, D), BF16, kind="Internal").ap()
    program(nc, out, parts_dram, **aps)
    r = run_bass_kernel_spmd(nc, [arrays], core_ids=[0])
    return r.results[0]["out"]
```

```python
from contextlib import ExitStack

import numpy as np
import concourse.bass as bass
from concourse import mybir

ALU = mybir.AluOpType
ACT = mybir.ActivationFunctionType
F32 = mybir.dt.float32
BF16 = mybir.dt.bfloat16
AX = mybir.AxisListType

P = 128
NB, N, D = 128, 64, 128
NU = NB // 2
GU = 8
NG = NU // GU
QU = 4
CH = 512
SCRATCH = 10368
QROWS = 24
EPS = 1e-5
NEG = 1e9

INPUTS = ["x", "adj", "L0_gnn_w1", "L0_gnn_b1", "L0_gnn_w2", "L0_gnn_b2",
          "L1_gnn_W_self_w", "L1_gnn_W_self_b", "L1_gnn_W_nb_w", "L1_gnn_W_nb_b",
          "L1_gnn_A1_w", "L1_gnn_A1_b", "L1_gnn_A2_w", "L1_gnn_A2_b",
          "L2_gnn_W1", "L2_gnn_b1", "L2_gnn_W2", "L2_gnn_b2", "L2_gnn_gamma", "L2_gnn_beta",
          "L3_gnn_W", "L3_gnn_b"]


def ds(start, size):
    return bass.ds(start, size)


def program(nc, out, parts_dram, ident_d, sel_d, **inp):
    ctx = ExitStack()

    def sb(name, shape, dt=F32):
        return ctx.enter_context(nc.sbuf_tensor(name, shape, dt))

    def sem(name):
        return ctx.enter_context(nc.semaphore(name))

    def after(eng, semaphore, count):
        if isinstance(count, int) and count <= 0:
            return
        eng.wait_ge(semaphore, count)

    with ctx:
        x = sb("x", [P, NU, D])
        adj_blocks = sb("adj_blocks", [P, NU, P])
        w_blocks = sb("w_blocks", [P, NU, P])
        pairs = sb("pairs", [P, 4, 4 * CH])
        adj_rows = sb("adj_rows", [P, 2, CH])
        block_stage = sb("block_stage", [P, 2, GU, P])
        xs = sb("xs", [P, 4, D])
        xt_dup = sb("xt_dup", [P, 4, 2, 2, N])
        xt_flat = xt_dup[:, :, :, :, :].rearrange("p z b c i -> p z (b c i)")
        plain_xt = slice(N, 3 * N)
        scratch = sb("scratch", [P, SCRATCH])
        ident = sb("ident", [P, P])
        sel = sb("sel", [QROWS, 4, P], BF16)
        wraw = pairs[:, 0, 0:8 * P].rearrange("p (k c) -> p k c", k=8)
        sel_f = pairs[0:QROWS, 1, 0:4 * P].rearrange("p (k c) -> p k c", k=4)
        wt = sb("wt", [P, 8, P])
        WI, WJ, W2T = (0, 3), (1, 4), (2, 5)
        L3T = 6
        wl = sb("wl", [P, 8, P])
        WSELF, WNB, A1I, A1J, W1A, W1B, W2, W2G = range(8)
        rows = sb("rows", [P, 12, P])
        R_B1, R_B2, R_BSELF, R_BNB, R_B2C, R_GAMMA, R_BETA, R_L3B, R_B1L2 = (0, 1), (2, 3), 4, 5, 6, 7, 8, 9, 10
        cols = sb("cols", [P, 8])
        C_BSELF, C_BNB, C_A1B, C_B1, C_A2, C_A2B, C_B2C, C_EPS = range(8)
        window_a2 = sb("window_a2", [P, 63])
        window_two = sb("window_two", [P, 64])
        window_mean = sb("window_mean", [P, 63])
        pick_last = sb("pick_last", [P, P])
        ones = sb("ones", [P, 1])
        w2_mean = sb("w2_mean", [P, 2])
        node = sb("node", [P, NU, 5])
        RSTD, SHIFT, SUM_W, SUM_ADJ, DINV = range(5)
        RSTD_DINV, SHIFT_DINV = SUM_W, SUM_ADJ
        degree = sb("degree", [P, NU])
        halves = sb("halves", [P, NU, 6])
        half_sum, half_gap, gap_sq, var, var_eps, std, node_mean = \
            (pairs[:, 3, n * NU:(n + 1) * NU] for n in range(7))

        off = [0]

        def view(*shape, dt=F32):
            n = int(np.prod(shape)) // (2 if dt == BF16 else 1)
            v = scratch[:, off[0]:off[0] + n]
            off[0] += n
            if dt == BF16:
                v = v.bitcast(BF16)
            return v
        windows = view(4, 4, 160).rearrange("p (z q c) -> p z q c", z=4, q=4)
        spread = view(2, 2048, dt=BF16).rearrange("p (z c) -> p z c", z=2)
        c_pos = view(4, 2, D).rearrange("p (z b d) -> p z b d", z=4, b=2)
        c_neg = view(4, 2, D).rearrange("p (z b d) -> p z b d", z=4, b=2)
        r_sb = view(2, 4, D).rearrange("p (z e d) -> p z e d", z=2, e=4)
        a_sb = view(2, D).rearrange("p (z d) -> p z d", z=2)
        a_full = view(D)
        a_rest = view(D)
        parts = view(2, 3, D, dt=BF16).rearrange("p (z t d) -> p z t d", z=2, t=3)
        rt_sb = view(2, D).rearrange("p (z d) -> p z d", z=2)
        o_sb = view(2, D).rearrange("p (z d) -> p z d", z=2)
        f_a = view(4, D).rearrange("p (z d) -> p z d", z=4)
        f_b = view(D)
        f_c = view(4, D).rearrange("p (z d) -> p z d", z=4)
        f_d = view(D)
        x_first = f_c
        off[0] = 0
        xs4 = view(4, D).rearrange("p (u d) -> p u d", u=4)
        xt4 = view(CH)
        hs4 = view(CH)
        hn4 = view(CH)
        p4 = view(2, CH).rearrange("p (z c) -> p z c", z=2)
        q4 = view(2, CH).rearrange("p (z c) -> p z c", z=2)
        squares = view(2, 2 * CH).rearrange("p (h c) -> p h c", h=2)
        is_zero = view(CH)
        mask = view(CH)
        fill = view(CH)
        score_a = view(CH)
        score_b = view(CH)
        weights = view(CH)
        row_max = view(8)
        row_sum = view(8)
        row_inv = view(8)
        off[0] = 0
        block_now = view(4, P).rearrange("p (z c) -> p z c", z=4)
        n_sb = view(2, 2, D).rearrange("p (z b d) -> p z b d", z=2, b=2)
        n_full = view(2, 2, D).rearrange("p (z b d) -> p z b d", z=2, b=2)
        xd = view(4, D).rearrange("p (z d) -> p z d", z=4)
        agg_a = view(2, D).rearrange("p (z d) -> p z d", z=2)
        y_out = view(2, GU, D).rearrange("p (z u d) -> p z u d", z=2, u=GU)

        wide = [ctx.enter_context(nc.psum_tensor(f"wide{h}", [P, 2 * CH], F32)) for h in range(3)]
        misc_a = ctx.enter_context(nc.psum_tensor("misc_a", [P, CH], F32))
        sums = [ctx.enter_context(nc.psum_tensor("sums", [P, CH], F32)), wide[2][:, 0:CH]]
        misc_b = wide[2][:, CH:2 * CH]
        near_sums = sums[0]
        near_t, near_p = misc_a[:, 0:P], misc_a[:, P:4 * P]

        loaded = {k: sem(f"loaded_{k}") for k in ("x", "ident", "sel", "raw", "flat", "row", "col")}
        consts = sem("consts")
        wt_filled, wt_out = sem("wt_filled"), sem("wt_out")
        prep = sem("prep")
        b2c_filled, b2c_out = sem("b2c_filled"), sem("b2c_out")
        norm_steps = [sem(f"norm_steps{n}") for n in range(4)]
        node_zero = sem("node_zero")
        waited = sem("waited")
        stats_done = [sem(f"stats_done{n}") for n in range(4)]
        std_done = [sem(f"std_done{n}") for n in range(4)]
        norm_ready = [sem(f"norm_ready{n}") for n in range(4)]
        dinv_steps = sem("dinv_steps")
        out_done = [sem("out_even"), sem("out_odd")]
        y_ready = sem("y_ready")

        def alone(eng):
            eng.sem_inc(waited)

        def signals(phase, names):
            return {nm: sem(f"{phase}_{nm}") for nm in names.split()}

        near_names = ("staged based windowed t_filled xt_out ac_filled a_out c_out split parts_put flat0 flat1 spreaded maxed "
                      "weighted r_out rt_filled rt_out o_filled o_out fin x_new ")
        near_sems = signals("near", near_names + "first_in0 first_in1 first_in2 first_in3")
        block_names = "turned blocks_out summed_w sum_out"
        feat_names = "staged lin_filled lin_out formed scored adj_in0 adj_in1 inverted weighed "
        feat = {"l1a": signals("l1a", feat_names + "pooled relued masked shifted topped cut exped totalled " + block_names),
                "l2a": signals("l2a", feat_names + "relued y_filled squared std_out " + block_names)}
        first = signals("s", "adj_in0 adj_in1 " + block_names)
        agg_names = "staged block_in t_filled xt_out n_filled n_out n_biased o_filled o_sum x_new"
        agg_sems = signals("agg", agg_names)

        x_dram = inp["x"].rearrange("(u b) i d -> (b i) u d", b=2)
        out_dram = out.rearrange("(u b) i d -> (b i) u d", b=2)
        adj_chunks = inp["adj"].rearrange("(g bb) (ib i) j -> g (bb ib) (i j)", g=NG, ib=8) \
            .rearrange("g (t q) c -> g q t c", q=4)

        def load_adj_rows(sp, g, z, signal):
            for q in range(4):
                sp.dma_start(adj_rows[32 * q:32 * q + 32, z, :], adj_chunks[g, q]).then_inc(signal, 16)

        def four_unit_rounds(eng, body, total=NU, step=4):
            body(0)
            with eng.Fori(1, total // step - 1) as r:
                body(r)
            body(total // step - 1)

        def two_rounds(eng, body, total, step=2):
            body(0)
            with eng.Fori(1, total // step - 1) as r:
                body(r)
            body(total // step - 1)

        def pe_turn(pe, s, g, src, ready, count, bank, banks=1, sums_too=False):
            pe.wait_ge(ready, count)
            after(pe, s["blocks_out"], 2 * (g + 1 - banks))
            if sums_too:
                after(pe, s["sum_out"], g)
            for i4 in range(4):
                m = nc.tensor.transpose(bank[:, i4 * P:(i4 + 1) * P], src[:, i4 * P:(i4 + 1) * P], ident[:, :])
            m.then_inc(s["turned"], 1)

        def act_blocks(act, s, g, z, before, bank):
            act.wait_ge(s["turned"], g + 1)
            after(act, moved[z], 8 * (before + g - z))
            for par in range(2):
                h = slice(64 * par, 64 * par + 64)
                dst = block_stage[h, z].rearrange("p u (t q i r) -> p (u t) q i r", t=4, q=4, i=4)[:, :, :, :, par]
                src = bank[h, 0:CH].rearrange("p (i q t) -> p t q i", i=4, q=4)
                for q in range(4):
                    c = nc.scalar.copy(dst[:, :, q], src[:, :, q])
                c.then_inc(s["blocks_out"], 1)

        def pe_row_sums(pe, s, g, z, bank, banks=1):
            pe.wait_ge(s["blocks_out"], 2 * g + 2)
            after(pe, s["sum_out"], g + 1 - banks)
            for u in range(GU):
                m = nc.tensor.matmul(bank[:, u:u + 1], block_stage[:, z, u, :], ones[:, :], start=True, stop=True)
            m.then_inc(s["summed_w"], 1)

        def act_row_sums(act, s, g, dst, bank):
            act.wait_ge(s["summed_w"], g + 1)
            alone(act)
            nc.scalar.copy(node[:, ds(g * GU, GU), dst], bank[:, 0:GU]).then_inc(s["sum_out"], 1)

        def sp_blocks(sp, s, g, z, dst):
            sp.wait_ge(s["blocks_out"], 2 * g + 2)
            alone(sp)
            sp.dma_start(dst[:, ds(g * GU, GU), :], block_stage[:, z]).then_inc(moved[z], 16)

        moved = [sem("moved_even"), sem("moved_odd")]

        def blocks_complete(eng, phases):
            for z in range(2):
                eng.wait_ge(moved[z], phases * 8 * NG)

        class Near:
            def __init__(self, name, wi, wj, w2, b1_row, blocks, moments_in, moments_out, start_on):
                self.name, self.s, self.base = name, near_sems, NU * ("l0a", "l0b", "l2b").index(name)
                self.wi, self.wj, self.w2, self.b1_row, self.blocks = wi, wj, w2, b1_row, blocks
                self.moments_in, self.moments_out, self.start_on = moments_in, moments_out, start_on

        near_phases = {
            "l0a": Near("l0a", wt[:, WI[0], :], wt[:, WJ[0], :], wt[:, W2T[0], :], rows[:, R_B1[0], :],
                        adj_blocks, None, None, None),
            "l0b": Near("l0b", wt[:, WI[1], :], wt[:, WJ[1], :], wt[:, W2T[1], :], rows[:, R_B1[1], :],
                        adj_blocks, None, 0, None),
            "l2b": Near("l2b", wl[:, W1A, :], wl[:, W1B, :], wl[:, W2G, :], rows[:, R_B1L2, :],
                        w_blocks, 1, 2, None),
        }

        flat = [near_sems["flat0"], near_sems["flat1"]]
        first_in = [near_sems["first_in0"], near_sems["first_in1"], near_sems["first_in2"], near_sems["first_in3"]]

        def near_pe(pe, ph):
            s, base = ph.s, ph.base

            def turn(u, z):
                pe.wait_ge(s["staged"], u + 1)
                after(pe, s["c_out"], u)
                after(pe, s["o_out"], u - 3)
                nc.tensor.transpose(near_t, xs[:, z, :], ident[:, :]).then_inc(s["t_filled"], 1)

            def project(u, z):
                pe.wait_ge(s["xt_out"], u + 1)
                after(pe, s["rt_out"], u - 2)
                nc.tensor.matmul(near_p[:, 0:P], xt_flat[:, z % 2, plain_xt], ph.wi, start=True, stop=True)
                for b in range(2):
                    m = nc.tensor.matmul(near_p[:, (1 + b) * P:(2 + b) * P], xt_flat[:, z % 2, b * P:(b + 1) * P], ph.wj,
                                         start=True, stop=True)
                m.then_inc(s["ac_filled"], 1)

            def spread_half(u, z, k, b):
                if k == 0 and b == 0:
                    pe.wait_ge(flat[z % 2], 8 * (u - z % 2) + 16)
                n = 8 * z + 2 * k + b
                back = 3 if n >= 3 else (2, 2, 5)[n]
                after(pe, s["maxed"], 8 * u + 2 * k + b + 1 - back)
                for q in range(2):
                    m = nc.tensor.matmul(wide[n % 3][:, q * CH:(q + 1) * CH], sel[:, 2 * b + q, :],
                                         spread[0:QROWS, z % 2, k * CH:(k + 1) * CH], start=True, stop=True)
                m.then_inc(s["spreaded"], 1)

            def weigh(u, z, k):
                pe.wait_ge(s["maxed"], 8 * u + 2 * k + 2)
                if k == 0:
                    pe.wait_ge(s["windowed"], u + 1)
                    after(pe, s["r_out"], u)
                for q in range(4):
                    m = nc.tensor.matmul(near_sums[32 * q:32 * q + 32, :], windows[:, z, q, 32 * k:32 * k + 32],
                                         pairs[:, k, q * CH:(q + 1) * CH], start=(k == 0), stop=(k == 3))
                m.then_inc(s["weighted"], 1)

            def latest(u):
                return min(u + 4, base + NU) if isinstance(u, int) else u + 4

            def gather(u, z):
                pe.wait_ge(s["r_out"], u + 1)
                pe.wait_ge(s["xt_out"], latest(u))
                after(pe, s["o_out"], u)
                for b in range(2):
                    nc.tensor.matmul(near_p[:, b * N:(b + 1) * N], c_pos[:, z, b, :],
                                     ph.blocks[:, ds(u - ph.base, 1), b * N:(b + 1) * N].rearrange("p a c -> p (a c)"),
                                     start=(b == 0), stop=False)
                for e in range(3):
                    nc.tensor.matmul(near_p[:, 0:P].rearrange("p (k c) -> p k c", c=8)[:, :, 2 * e:2 * e + 2],
                                     r_sb[:, z % 2, e, :],
                                     ident[:, :].rearrange("p (k c) -> p k c", c=8)[:, :, 2 * e:2 * e + 2],
                                     start=False, stop=False)
                nc.tensor.matmul(near_p[:, 0:P], r_sb[:, z % 2, 3, :], pick_last[:, :],
                                 start=False, stop=True).then_inc(s["rt_filled"], 1)

            def output(u, z):
                pe.wait_ge(s["rt_out"], u + 1)
                pe.wait_ge(s["c_out"], latest(u))
                nc.tensor.matmul(near_t, rt_sb[:, z % 2, :], ph.w2, start=True, stop=True).then_inc(s["o_filled"], 1)

            for u in range(2):
                turn(base + u, u)
                project(base + u, u)

            def body(r):
                for z in range(4):
                    u = base + 4 * r + z
                    static = isinstance(r, int)
                    ahead = not static or r < NU // 4 - 1 or z < 2
                    behind = not static or r > 0 or z > 0
                    zm, zp = (z - 1) % 4, (z + 2) % 4
                    for k in range(4):
                        spread_half(u, z, k, 0)
                        if k == 1 and ahead:
                            turn(u + 2, zp)
                        if k == 2 and behind:
                            gather(u - 1, zm)
                        if k == 3 and ahead:
                            project(u + 2, zp)
                        spread_half(u, z, k, 1)
                        if k > 0:
                            weigh(u, z, k - 1)
                        elif behind:
                            weigh(u - 1, zm, 3)
                        if k == 3 and behind:
                            output(u - 1, zm)
            four_unit_rounds(pe, body)
            weigh(base + NU - 1, 3, 3)
            gather(base + NU - 1, 3)
            output(base + NU - 1, 3)

        def near_act(act, ph):
            s, base = ph.s, ph.base

            def copy_xt(u, z):
                act.wait_ge(s["t_filled"], u + 1)
                after(act, s["ac_filled"], u - 1)
                src = near_t.rearrange("p (b i) -> p b i", b=2)
                nc.scalar.copy(xt_dup[:, z % 2, :, 0, :], src)
                nc.scalar.copy(xt_dup[:, z % 2, :, 1, :], src).then_inc(s["xt_out"], 1)

            def copy_ac(u, z):
                act.wait_ge(s["ac_filled"], u + 1)
                after(act, s["split"], 5 * (u - 2) + 1)
                nc.scalar.copy(a_sb[:, z % 2, :], near_p[:, 0:P]).then_inc(s["a_out"], 1)
                after(act, s["maxed"], 8 * (u - 3))
                after(act, s["rt_filled"], u - 3)
                src = near_p[:, P:3 * P].rearrange("p (b d) -> p b d", b=2)
                nc.scalar.mul(c_neg[:, z], src, -1.0)
                nc.scalar.copy(c_pos[:, z], src).then_inc(s["c_out"], 1)

            def copy_r(u, z):
                act.wait_ge(s["weighted"], 4 * u + 4)
                after(act, s["rt_filled"], u - 1)
                nc.scalar.copy(r_sb[:, z % 2], near_sums[:, :].rearrange("p (e d) -> p e d", e=4)).then_inc(s["r_out"], 1)

            def copy_rt(u, z):
                act.wait_ge(s["rt_filled"], u + 1)
                after(act, s["o_filled"], u - 1)
                nc.scalar.copy(rt_sb[:, z % 2, :], near_p[:, 0:P]).then_inc(s["rt_out"], 1)

            def copy_o(u, z):
                act.wait_ge(s["o_filled"], u + 1)
                after(act, s["x_new"], u - 1)
                nc.scalar.copy(o_sb[:, z % 2, :], near_t).then_inc(s["o_out"], 1)

            def scaled(dst, row, u, col):
                return nc.scalar.activation(dst, row, ACT.Identity, scale=node[:, ds(u - ph.base, 1), col])

            l2 = ph.name == "l2b"

            def stage(u, z):
                after(act, s["x_new"], u - 3)
                after(act, s["weighted"], 4 * (u - 3))
                alone(act)
                src = x[:, ds(u - ph.base, 1), :].rearrange("p a d -> p (a d)")
                if ph.moments_in is None:
                    nc.scalar.copy(xs[:, z, :], src).then_inc(s["staged"], 1)
                else:
                    nc.scalar.activation(xs[:, z, :], src, ACT.Identity, scale=node[:, ds(u - ph.base, 1), RSTD],
                                         bias=node[:, ds(u - ph.base, 1), SHIFT]).then_inc(s["staged"], 1)
                dst = windows[:, z].rearrange("p q (k c) -> p q k c", k=4)[:, :, :, 0:8]
                blk = ph.blocks[:, ds(u - ph.base, 1), :].rearrange("p a (q k m) -> p (a q) k m", q=4, k=4)
                nc.scalar.copy(dst, blk).then_inc(s["windowed"], 1)
                if l2:
                    scaled(f_c[:, z, :], rows[:, R_BETA, :], u, SUM_ADJ)
                    scaled(f_a[:, z, :], rows[:, R_B2C, :], u, SUM_W).then_inc(s["based"], 1)
                else:
                    scaled(f_a[:, z, :], rows[:, R_B2[1 if ph.name == "l0b" else 0], :], u, SUM_ADJ) \
                        .then_inc(s["based"], 1)

            for u in range(3):
                stage(base + u, u)
            for u in range(2):
                copy_xt(base + u, u)
                copy_ac(base + u, u)

            def body(r):
                for z in range(4):
                    u = base + 4 * r + z
                    static = isinstance(r, int)
                    ahead = not static or r < NU // 4 - 1 or z < 2
                    behind = not static or r > 0 or z > 0
                    zm, zp = (z - 1) % 4, (z + 2) % 4
                    if behind:
                        copy_r(u - 1, zm)
                    if ahead:
                        copy_xt(u + 2, zp)
                    if behind:
                        copy_rt(u - 1, zm)
                    if ahead:
                        copy_ac(u + 2, zp)
                    if behind:
                        copy_o(u - 1, zm)
                    if not static or r < NU // 4 - 1 or z < 1:
                        stage(u + 3, (z + 3) % 4)
            four_unit_rounds(act, body)
            copy_r(base + NU - 1, 3)
            copy_rt(base + NU - 1, 3)
            copy_o(base + NU - 1, 3)

        def near_dve(v, ph):
            s, base = ph.s, ph.base

            def form(u, z, k, b):
                v.wait_ge(s["spreaded"], 8 * u + 2 * k + b + 1)
                if k == 0 and b == 0:
                    v.wait_ge(s["c_out"], u + 1)
                if b == 0:
                    after(v, s["weighted"], 4 * u + k - 3)
                nc.vector.tensor_tensor(
                    pairs[:, k, b * 2 * CH:(b + 1) * 2 * CH].rearrange("p (i d) -> p i d", d=D),
                    wide[(8 * z + 2 * k + b) % 3][:, :].rearrange("p (i d) -> p i d", d=D),
                    c_neg[:, z, b, :].unsqueeze(1).to_broadcast([P, 8, D]), ALU.max).then_inc(s["maxed"], 1)

            def stats(u):
                v.wait_ge(s["x_new"], u + 1)
                alone(v)
                nc.vector.bn_stats(halves[:, ds(u - ph.base, 1), :].rearrange("p a d -> p (a d)"),
                                   x[:, ds(u - ph.base, 1), :].rearrange("p a d -> p (a d)")) \
                    .then_inc(stats_done[ph.moments_out], 1)

            def body(r):
                for z in range(4):
                    u = base + 4 * r + z
                    behind = ph.moments_out is not None and (not isinstance(r, int) or r > 0 or z >= 2)
                    for k in range(4):
                        for b in range(2):
                            form(u, z, k, b)
                        if behind and k == 1:
                            stats(u - 2)
            four_unit_rounds(v, body)
            if ph.moments_out is not None:
                for u in (base + NU - 2, base + NU - 1):
                    stats(u)

        def near_pool(g_eng, ph):
            s, base = ph.s, ph.base
            l0b, l2 = ph.name == "l0b", ph.name == "l2b"
            def split(u, z):
                g_eng.wait_ge(s["a_out"], u + 1)
                after(g_eng, s["parts_put"], 32 * (u - 1))
                b1 = ph.b1_row
                high, mid, low = (parts[:, z % 2, n, :] for n in range(3))
                nc.gpsimd.tensor_tensor(a_full, a_sb[:, z % 2, :], b1, ALU.add).then_inc(s["split"], 1)
                nc.gpsimd.tensor_tensor(high, a_sb[:, z % 2, :], b1, ALU.add).then_inc(s["split"], 1)
                g_eng.wait_ge(s["split"], 5 * u + 2)
                nc.gpsimd.tensor_tensor(a_rest, a_full, high, ALU.subtract).then_inc(s["split"], 1)
                nc.gpsimd.tensor_tensor(mid, a_full, high, ALU.subtract).then_inc(s["split"], 1)
                g_eng.wait_ge(s["split"], 5 * u + 4)
                nc.gpsimd.tensor_tensor(low, a_rest, mid, ALU.subtract).then_inc(s["split"], 1)

            nf = {"l0a": 1, "l0b": 2, "l2b": 2}[ph.name]
            fin_before = {"l0a": 0, "l0b": NU, "l2b": 3 * NU}[ph.name]

            def finish(u, z):
                n = nf * (u - base) + fin_before
                g_eng.wait_ge(s["based"], u + 1)
                after(g_eng, s["x_new"], u)
                if l0b:
                    g_eng.wait_ge(first_in[z], 4 * (u - base - z) + 16)
                nc.gpsimd.tensor_tensor(f_b, f_a[:, z, :], xs[:, z, :], ALU.add).then_inc(s["fin"], 1)
                total = f_b
                if nf == 2:
                    g_eng.wait_ge(s["fin"], n + 1)
                    nc.gpsimd.tensor_tensor(f_d, f_b, x_first[:, z, :] if l0b else f_c[:, z, :], ALU.add) \
                        .then_inc(s["fin"], 1)
                    total = f_d
                g_eng.wait_ge(s["fin"], n + nf)
                g_eng.wait_ge(s["o_out"], u + 1)
                alone(g_eng)
                dst = x[:, ds(u - ph.base, 1), :].rearrange("p a d -> p (a d)")
                nc.gpsimd.tensor_tensor(dst, total, o_sb[:, z % 2, :], ALU.add).then_inc(s["x_new"], 1)

            for u in range(2):
                split(base + u, u)

            def body(r):
                for z in range(4):
                    u = base + 4 * r + z
                    static = isinstance(r, int)
                    if not static or r > 0 or z > 0:
                        finish(u - 1, (z - 1) % 4)
                    if not static or r < NU // 4 - 1 or z < 2:
                        split(u + 2, (z + 2) % 4)
            four_unit_rounds(g_eng, body)
            finish(base + NU - 1, 3)

        def near_sp(sp, ph):
            s, base = ph.s, ph.base

            def put_parts(u, z):
                sp.wait_ge(s["split"], 5 * (u + 1))
                alone(sp)
                after(sp, flat[z % 2], 8 * (u - z % 2))
                alone(sp)
                for par in range(2):
                    sp.dma_start(parts_dram[z % 2, par].rearrange("t i d -> i t d"), parts[par::2, z % 2, :, :]) \
                        .then_inc(s["parts_put"], 16)

            def get_parts(u, z):
                sp.wait_ge(s["parts_put"], 32 * (u + 1))
                alone(sp)
                after(sp, s["spreaded"], 8 * (u - 1))
                alone(sp)
                sp.dma_start(spread[0:QROWS, z % 2, :],
                             parts_dram[z % 2].rearrange("a t (q i) d -> (a t q) (i d)", q=4)).then_inc(flat[z % 2], 16)

            def first_input(u, z):
                after(sp, s["x_new"], u - 3)
                alone(sp)
                sp.dma_start(x_first[:, z, :], x_dram[:, ds(u - ph.base, 1), :].rearrange("p a d -> p (a d)")) \
                    .then_inc(first_in[z], 16)

            for u in range(2):
                put_parts(base + u, u)
                get_parts(base + u, u)
            if ph.name == "l0b":
                for u in range(3):
                    first_input(base + u, u)

            def body(r):
                for z in range(4):
                    u = base + 4 * r + z
                    static = isinstance(r, int)
                    if ph.name == "l0b" and (not static or r < NU // 4 - 1 or z < 1):
                        first_input(u + 3, (z + 3) % 4)
                    if not static or r < NU // 4 - 1 or z < 2:
                        put_parts(u + 2, (z + 2) % 4)
                        get_parts(u + 2, (z + 2) % 4)
            four_unit_rounds(sp, body)

        def dve_var(v, n):
            steps = norm_steps[n]
            even, odd = halves[:, :, 1], halves[:, :, 4]
            v.wait_ge(stats_done[n], NU)
            nc.vector.tensor_tensor(half_sum, even, odd, ALU.add).then_inc(steps, 1)
            nc.vector.tensor_tensor(half_gap, even, odd, ALU.subtract).then_inc(steps, 1)
            nc.vector.tensor_tensor(var, halves[:, :, 2], halves[:, :, 5], ALU.add).then_inc(steps, 1)
            v.wait_ge(steps, 3)
            nc.vector.tensor_scalar(node_mean, half_sum, 0.5, None, ALU.mult).then_inc(steps, 1)
            nc.vector.scalar_tensor_tensor(out=gap_sq, in0=half_gap, scalar=0.25, in1=half_gap,
                                           op0=ALU.mult, op1=ALU.mult).then_inc(steps, 1)
            v.wait_ge(steps, 5)
            nc.vector.scalar_tensor_tensor(out=var_eps, in0=var, scalar=1.0 / D, in1=gap_sq,
                                           op0=ALU.mult, op1=ALU.add).then_inc(steps, 1)

        def act_std(act, n):
            act.wait_ge(norm_steps[n], 6)
            nc.scalar.activation(std, var_eps, ACT.Sqrt, bias=cols[:, C_EPS:C_EPS + 1]) \
                .then_inc(std_done[n], 1)

        def dve_rstd(v, n):
            v.wait_ge(std_done[n], 1)
            nc.vector.reciprocal(node[:, :, RSTD], std).then_inc(norm_steps[n], 1)
            v.wait_ge(norm_steps[n], 7)
            nc.vector.scalar_tensor_tensor(out=node[:, :, SHIFT], in0=node_mean, scalar=-1.0,
                                           in1=node[:, :, RSTD], op0=ALU.mult, op1=ALU.mult) \
                .then_inc(norm_ready[n], 1)

        class Feat:
            def __init__(self, name, moments_in):
                self.name, self.s, self.moments_in = name, feat[name], moments_in
                self.l1 = name == "l1a"
                self.groups_before = NG if self.l1 else 2 * NG
                self.dve_tiles = 12 if self.l1 else TILES
                if self.l1:
                    self.chain = [(WSELF, "x", "hs"), (WNB, "x", "hn"), (A1I, "hs", "p"), (A1J, "hn", "q")]
                else:
                    self.chain = [(W1A, "x", "p"), (W1B, "x", "q")]
                self.steps = 1 + len(self.chain)

        NQ = NU // QU
        TILES = 16
        feat_phases = {"l1a": Feat("l1a", 0), "l2a": Feat("l2a", 1)}
        DVE_GRAPHS, POOL_GRAPHS = (0, 1, 2, 4, 5, 6), (3, 7)
        pool_tile = [pairs[:, 3, :], squares.rearrange("p h c -> p (h c)")]

        def place(pos):
            if pos % 4 == 3:
                m = pos // 4
                return True, m, POOL_GRAPHS[m // 2], m % 2
            n = pos - pos // 4
            return False, n, DVE_GRAPHS[n // 2], n % 2
        LIN_AT = (1, 4, 7, 10, 13)

        BLOCKS_AT = ((0, 12), (1, 1))

        def feat_pe(pe, ph):
            s = ph.s
            src_of = {"x": xt4, "hs": hs4, "hn": hn4}

            def project(quad, j):
                after(pe, s["lin_out"], ph.steps * quad + j)
                if j == 0:
                    pe.wait_ge(s["staged"], QU * (quad + 1))
                    for n in range(QU):
                        m = nc.tensor.transpose(misc_a[:, n * P:(n + 1) * P], xs4[:, n, :], ident[:, :])
                else:
                    w, src, _ = ph.chain[j - 1]
                    m = nc.tensor.matmul(misc_a[:, :], wl[:, w, :], src_of[src], start=True, stop=True)
                m.then_inc(s["lin_filled"], 1)

            def score_c(qz, bb, gz):
                t = 16 * qz + 2 * bb
                mov = q4[:, qz, bb * N:(bb + 1) * N].unsqueeze(1).to_broadcast([P, 8, N])
                for q in range(4):
                    nc.tensor.matmul(sums[gz][32 * q:32 * q + 32, :].rearrange("p (i j) -> p i j", j=N),
                                     window_two[:, 31 - t:63 - t], mov, start=False, stop=False)

            def score(quad, qz, pos, gz):
                pooled, n, bb, ih = place(pos)
                t = TILES * qz + 2 * bb + ih
                if pooled:
                    pe.wait_ge(s["relued"], 4 * quad + n + 1)
                    tile = pool_tile[n % 2]
                else:
                    pe.wait_ge(s["formed"], 12 * quad + n + 1)
                    tile = pairs[:, n % 3, :]
                for q in range(4):
                    m = nc.tensor.matmul(sums[gz][32 * q:32 * q + 32, :], window_a2[:, 31 - t:63 - t],
                                         tile[:, q * CH:(q + 1) * CH], start=(t == 0), stop=(t == 31))
                m.then_inc(s["scored"], 1)
                if not pooled and ih == 1:
                    score_c(qz, bb, gz)

            def square_in(quad, tau, h):
                tile = TILES * quad + tau
                if h == 0:
                    pe.wait_ge(s["relued"], tile + 1)
                after(pe, s["squared"], 2 * tile + h - 1)
                for c in range(2):
                    m = nc.tensor.matmul(wide[h][:, c * CH:(c + 1) * CH], wl[:, W2, :],
                                         pairs[:, tau % 4, (2 * h + c) * CH:(2 * h + c + 1) * CH],
                                         start=True, stop=True)
                m.then_inc(s["y_filled"], 1)

            def mean(tile, t, gz):
                pe.wait_ge(s["squared"], 2 * tile + 2)
                for q in range(4):
                    m = nc.tensor.matmul(sums[gz][32 * q:32 * q + 32, :], window_mean[:, 31 - t:63 - t],
                                         squares[:, q // 2, (q % 2) * CH:(q % 2 + 1) * CH],
                                         start=(t == 0), stop=(t == 31))
                m.then_inc(s["scored"], 1)

            def finish(g, gz):
                pe_turn(pe, s, g, weights, s["weighed"], g + 1, misc_b, sums_too=not ph.l1)

            for j in range(ph.steps):
                project(0, j)

            def body_gz(g, gz):
                for qz in range(2):
                    quad = 2 * g + qz
                    static = isinstance(g, int)
                    ahead = not static or quad + 1 < NQ
                    behind = not static or g >= 1
                    pe.wait_ge(s["lin_out"], ph.steps * (quad + 1))
                    if qz == 0:
                        after(pe, s["shifted"] if ph.l1 else s["std_out"], g - 1)
                    for tau in range(TILES):
                        t = TILES * qz + tau
                        if ph.l1:
                            score(quad, qz, tau, gz)
                        else:
                            square_in(quad, tau, 0)
                            if t > 0:
                                mean(TILES * quad + tau - 1, t - 1, gz)
                            elif behind:
                                mean(TILES * quad + tau - 1, 31, 1 - gz)
                            square_in(quad, tau, 1)
                        if ahead and tau in LIN_AT[:ph.steps]:
                            project(quad + 1, LIN_AT.index(tau))
                        if behind and (qz, tau) == BLOCKS_AT[ph.l1]:
                            finish(g - 1, 1 - gz)
                        if behind and not ph.l1 and (qz, tau) == (0, 14):
                            pe_row_sums(pe, s, g - 1, 1 - gz, misc_b)

            def body(r):
                for gz in range(2):
                    body_gz(2 * r + gz, gz)
            two_rounds(pe, body, NG)
            if not ph.l1:
                mean(32 * NG - 1, 31, 1)
            finish(NG - 1, 1)
            if not ph.l1:
                pe_row_sums(pe, s, NG - 1, 1, misc_b)

        def feat_act(act, ph):
            s = ph.s
            dst_of = {"hs": hs4, "hn": hn4}

            def project(quad, qz, j):
                act.wait_ge(s["lin_filled"], ph.steps * quad + j + 1)
                if j == 0:
                    nc.scalar.copy(xt4, misc_a[:, :]).then_inc(s["lin_out"], 1)
                    return
                w, _, dst = ph.chain[j - 1]
                if dst in ("p", "q"):
                    after(act, s["formed"], ph.dve_tiles * (quad - 1))
                    if ph.l1:
                        after(act, s["pooled"], 4 * (quad - 1))
                    if ph.l1 and dst == "q":
                        after(act, s["scored"], TILES * (quad - 1))
                if dst == "q":
                    out_q = q4[:, qz, :]
                    if ph.l1:
                        nc.scalar.mul(out_q, misc_a[:, :], -1.0).then_inc(s["lin_out"], 1)
                    else:
                        nc.scalar.copy(out_q, misc_a[:, :]).then_inc(s["lin_out"], 1)
                    return
                bias = {"hs": C_BSELF, "hn": C_BNB, "p": C_A1B if ph.l1 else C_B1}[dst]
                d = p4[:, qz, :] if dst == "p" else dst_of[dst]
                nc.scalar.activation(d, misc_a[:, :], ACT.Identity, bias=cols[:, bias:bias + 1]).then_inc(s["lin_out"], 1)

            def relu_pooled(quad, m):
                act.wait_ge(s["pooled"], 4 * quad + m + 1)
                nc.scalar.activation(pool_tile[m % 2], pool_tile[m % 2], ACT.Relu).then_inc(s["relued"], 1)

            def relu(tile, slot):
                act.wait_ge(s["formed"], tile + 1)
                nc.scalar.activation(pairs[:, slot, :], pairs[:, slot, :], ACT.Relu).then_inc(s["relued"], 1)

            def square(tile, h):
                act.wait_ge(s["y_filled"], 2 * tile + h + 1)
                after(act, s["scored"], tile)
                nc.scalar.activation(squares[:, h, :], wide[h][:, :], ACT.Square,
                                     bias=cols[:, C_B2C:C_B2C + 1]).then_inc(s["squared"], 1)

            def weigh(g, gz):
                if ph.l1:
                    act.wait_ge(s["cut"], g + 1)
                    after(act, s["weighed"], g)
                    nc.scalar.activation(score_a, score_b, ACT.Exp).then_inc(s["exped"], 1)
                else:
                    act.wait_ge(s["scored"], 32 * (g + 1))
                    after(act, s["inverted"], g)
                    nc.scalar.activation(score_a, sums[gz][:, :], ACT.Sqrt,
                                         bias=cols[:, C_EPS:C_EPS + 1]).then_inc(s["std_out"], 1)

            def stage(quad):
                after(act, s["lin_filled"], ph.steps * (quad - 1) + 1)
                alone(act)
                for n in range(QU):
                    u = QU * quad + n
                    nc.scalar.activation(xs4[:, n, :], x[:, ds(u, 1), :].rearrange("p a d -> p (a d)"), ACT.Identity,
                                         scale=node[:, ds(u, 1), RSTD], bias=node[:, ds(u, 1), SHIFT]) \
                        .then_inc(s["staged"], 1)

            stage(0)
            for j in range(ph.steps):
                project(0, 0, j)
            stage(1)
            if not ph.l1:
                relu(0, 0)

            def body_gz(g, gz):
                for qz in range(2):
                    quad = 2 * g + qz
                    static = isinstance(g, int)
                    ahead = not static or quad + 1 < NQ
                    behind = not static or g >= 1
                    for tau in range(TILES):
                        tile = TILES * quad + tau
                        if not ph.l1:
                            if not static or tile + 1 < 32 * NG:
                                relu(tile + 1, (tau + 1) % 4)
                            square(tile, 0)
                            square(tile, 1)
                        elif tau % 4 == 1:
                            relu_pooled(quad, tau // 4)
                        if ahead and tau in LIN_AT[:ph.steps]:
                            project(quad + 1, 1 - qz, LIN_AT.index(tau))
                        if tau == 15 and (not static or quad + 2 < NQ):
                            stage(quad + 2)
                        if behind and qz == 0 and tau == (8 if ph.l1 else 3):
                            weigh(g - 1, 1 - gz)
                        if behind and (qz, tau) == BLOCKS_AT[ph.l1]:
                            act_blocks(act, s, g - 1, 1 - gz, ph.groups_before, misc_b)
                        if behind and not ph.l1 and (qz, tau) == (0, 14):
                            act_row_sums(act, s, g - 1, SUM_W, misc_b)

            def body(r):
                for gz in range(2):
                    body_gz(2 * r + gz, gz)
            two_rounds(act, body, NG)
            weigh(NG - 1, 1)
            act_blocks(act, s, NG - 1, 1, ph.groups_before, misc_b)
            if not ph.l1:
                act_row_sums(act, s, NG - 1, SUM_W, misc_b)

        def feat_dve(v, ph):
            s = ph.s

            def form(quad, qz, n):
                if ph.l1:
                    bb, ih, slot = DVE_GRAPHS[n // 2], n % 2, n % 3
                    after(v, s["scored"], TILES * quad + (n - 2 + (n - 3) // 3 if n >= 3 else n - 3))
                else:
                    bb, ih, slot = n // 2, n % 2, n % 4
                    after(v, s["y_filled"], 2 * (TILES * quad + n - 3))
                i0 = bb * N + ih * 32
                a = p4[:, qz, i0:i0 + 32].unsqueeze(2).to_broadcast([P, 32, N])
                c = q4[:, qz, bb * N:(bb + 1) * N].unsqueeze(1).to_broadcast([P, 32, N])
                nc.vector.tensor_tensor(pairs[:, slot, :].rearrange("p (i j) -> p i j", j=N), a, c,
                                        ALU.max if ph.l1 else ALU.add).then_inc(s["formed"], 1)

            def r3(t):
                return t.rearrange("p (i j) -> p i j", j=N)

            def b3(t):
                return t.unsqueeze(2).to_broadcast([P, 8, N])

            def shift(g, gz):
                v.wait_ge(s["scored"], 32 * (g + 1))
                v.wait_ge(s["masked"], 3 * (g + 1))
                nc.vector.scalar_tensor_tensor(out=score_a, in0=sums[gz][:, :], scalar=cols[:, C_A2B:C_A2B + 1],
                                               in1=mask, op0=ALU.add, op1=ALU.mult).then_inc(s["shifted"], 1)

            def top(g):
                v.wait_ge(s["topped"], 2 * g + 1)
                nc.vector.tensor_reduce(row_max, r3(score_b), AX.X, ALU.max).then_inc(s["topped"], 1)

            def cut(g):
                v.wait_ge(s["topped"], 2 * g + 2)
                nc.vector.tensor_tensor(r3(score_b), r3(score_b), b3(row_max), ALU.subtract).then_inc(s["cut"], 1)

            def total(g):
                v.wait_ge(s["exped"], g + 1)
                nc.vector.tensor_reduce(row_sum, r3(score_a), AX.X, ALU.add).then_inc(s["totalled"], 1)

            def invert(g):
                if ph.l1:
                    v.wait_ge(s["totalled"], g + 1)
                    nc.vector.reciprocal(row_inv, row_sum).then_inc(s["inverted"], 1)
                else:
                    v.wait_ge(s["std_out"], g + 1)
                    after(v, s["weighed"], g)
                    nc.vector.reciprocal(score_b, score_a).then_inc(s["inverted"], 1)

            def end_step(g, gz, tau):
                if ph.l1:
                    if tau == 2:
                        shift(g, gz)
                    if tau == 5:
                        top(g)
                    if tau == 6:
                        cut(g)
                    if tau == 8:
                        total(g)
                    if tau == 9:
                        invert(g)
                elif tau == 6:
                    invert(g)

            v.wait_ge(s["lin_out"], ph.steps)

            def body_gz(g, gz):
                for qz in range(2):
                    quad = 2 * g + qz
                    behind = not isinstance(g, int) or g >= 1
                    v.wait_ge(s["lin_out"], ph.steps * (quad + 1))
                    for tau in range(ph.dve_tiles):
                        form(quad, qz, tau)
                        if behind and qz == 0:
                            end_step(g - 1, 1 - gz, tau)

            def body(r):
                for gz in range(2):
                    body_gz(2 * r + gz, gz)
            two_rounds(v, body, NG)
            for tau in range(10):
                end_step(NG - 1, 1, tau)

        def feat_pool(g_eng, ph):
            s = ph.s

            def masks(g, gz):
                g_eng.wait_ge([s["adj_in0"], s["adj_in1"]][gz], 32 * (g - gz) + 64)
                after(g_eng, s["shifted"], g)
                alone(g_eng)
                nc.gpsimd.tensor_scalar(is_zero, adj_rows[:, gz, :], 0.0, None, ALU.is_equal).then_inc(s["masked"], 1)
                g_eng.wait_ge(s["masked"], 3 * g + 1)
                alone(g_eng)
                nc.gpsimd.tensor_scalar(mask, is_zero, -1.0, 1.0, ALU.mult, ALU.add).then_inc(s["masked"], 1)
                nc.gpsimd.tensor_scalar(fill, is_zero, -NEG, None, ALU.mult).then_inc(s["masked"], 1)

            def fill_in(g):
                g_eng.wait_ge(s["shifted"], g + 1)
                nc.gpsimd.tensor_tensor(score_b, score_a, fill, ALU.add).then_inc(s["topped"], 1)

            def weigh(g, gz):
                after(g_eng, s["turned"], g)
                g_eng.wait_ge(s["inverted"], g + 1)
                if ph.l1:
                    nc.gpsimd.tensor_tensor(weights.rearrange("p (i j) -> p i j", j=N),
                                            score_a.rearrange("p (i j) -> p i j", j=N),
                                            row_inv.unsqueeze(2).to_broadcast([P, 8, N]), ALU.mult) \
                        .then_inc(s["weighed"], 1)
                else:
                    g_eng.wait_ge([s["adj_in0"], s["adj_in1"]][gz], 32 * (g - gz) + 64)
                    nc.gpsimd.tensor_tensor(weights, score_b, adj_rows[:, gz, :], ALU.mult).then_inc(s["weighed"], 1)

            def form(quad, qz, m):
                g_eng.wait_ge(s["lin_out"], ph.steps * (quad + 1))
                after(g_eng, s["scored"], TILES * quad + 4 * m - 4)
                bb, i0 = POOL_GRAPHS[m // 2], POOL_GRAPHS[m // 2] * N + (m % 2) * 32
                a = p4[:, qz, i0:i0 + 32].unsqueeze(2).to_broadcast([P, 32, N])
                c = q4[:, qz, bb * N:(bb + 1) * N].unsqueeze(1).to_broadcast([P, 32, N])
                nc.gpsimd.tensor_tensor(pool_tile[m % 2].rearrange("p (i j) -> p i j", j=N), a, c,
                                        ALU.subtract).then_inc(s["pooled"], 1)

            def body_gz(g, gz):
                behind = not isinstance(g, int) or g >= 1
                if not ph.l1:
                    if behind:
                        weigh(g - 1, 1 - gz)
                    return
                for m in range(4):
                    form(2 * g, 0, m)
                    if behind and m == 0:
                        fill_in(g - 1)
                    if behind and m == 2:
                        weigh(g - 1, 1 - gz)
                for m in range(4):
                    form(2 * g + 1, 1, m)
                    if m == 1:
                        masks(g, gz)

            def body(r):
                for gz in range(2):
                    body_gz(2 * r + gz, gz)
            two_rounds(g_eng, body, NG)
            if ph.l1:
                fill_in(NG - 1)
            weigh(NG - 1, 1)

        def feat_sp(sp, ph):
            s = ph.s

            def body(r):
                for gz in range(2):
                    g = 2 * r + gz
                    after(sp, s["weighed"], g - 1)
                    alone(sp)
                    load_adj_rows(sp, g, gz, [s["adj_in0"], s["adj_in1"]][gz])
                    if not isinstance(g, int) or g >= 1:
                        sp_blocks(sp, s, g - 1, 1 - gz, w_blocks)
            two_rounds(sp, body, NG)
            sp_blocks(sp, s, NG - 1, 1, w_blocks)

        class Agg:
            def __init__(self, name, blocks, w_self, w_nb, moments_in, moments_out):
                self.name, self.s, self.base = name, agg_sems, NU * ("l1b", "l3").index(name)
                self.blocks, self.w_self, self.w_nb = blocks, w_self, w_nb
                self.moments_in, self.moments_out = moments_in, moments_out
                self.l1 = name == "l1b"

        agg_phases = {"l1b": Agg("l1b", w_blocks, wl[:, WSELF, :], wl[:, WNB, :], 0, 1),
                      "l3": Agg("l3", adj_blocks, wt[:, L3T, :], wt[:, L3T, :], 2, 3)}

        def agg_pool(g_eng, ph):
            s, base = ph.s, ph.base

            def bias(u, z):
                g_eng.wait_ge(s["n_out"], u + 1)
                after(g_eng, s["o_filled"], u - 1)
                b = rows[:, R_BNB, :].unsqueeze(1).to_broadcast([P, 2, D])
                nc.gpsimd.tensor_tensor(n_full[:, z % 2], n_sb[:, z % 2], b, ALU.add).then_inc(s["n_biased"], 1)

            def body(r):
                for z in range(4):
                    bias(base + 4 * r + z, z)
            if ph.l1:
                four_unit_rounds(g_eng, body)

        def agg_pe(pe, ph):
            s, base = ph.s, ph.base

            def turn(u, z):
                pe.wait_ge(s["staged"], u + 1)
                after(pe, s["xt_out"], u)
                src = xs[:, z, :] if ph.l1 else xd[:, z, :]
                nc.tensor.transpose(misc_a[:, 0:P], src, ident[:, :]).then_inc(s["t_filled"], 1)

            def neighbours(u, z):
                pe.wait_ge(s["xt_out"], u + 1)
                after(pe, s["n_out"], u)
                for b in range(2):
                    m = nc.tensor.matmul(misc_b[:, b * D:(b + 1) * D], xt_flat[:, z, b * P:(b + 1) * P], ph.w_nb,
                                         start=True, stop=True)
                m.then_inc(s["n_filled"], 1)

            def combine(u, z):
                pe.wait_ge(s["block_in"], u + 1)
                after(pe, s["o_sum"], u - 1)
                pe.wait_ge(s["n_biased"] if ph.l1 else s["n_out"], u + 1)
                n = n_full if ph.l1 else n_sb
                for b in range(2):
                    nc.tensor.matmul(sums[z % 2][b * N:(b + 1) * N, 0:D], block_now[:, z, b * N:(b + 1) * N],
                                     n[:, z % 2, b, :], start=True, stop=False)
                nc.tensor.matmul(sums[z % 2][:, 0:D], xt_flat[:, z, plain_xt], ph.w_self,
                                 start=False, stop=True).then_inc(s["o_filled"], 1)

            turn(base, 0)
            turn(base + 1, 1)
            neighbours(base, 0)

            def body(r):
                for z in range(4):
                    u = base + 4 * r + z
                    if not isinstance(r, int) or r < NU // 4 - 1 or z < 2:
                        turn(u + 2, (z + 2) % 4)
                    if not isinstance(r, int) or r < NU // 4 - 1 or z < 3:
                        neighbours(u + 1, (z + 1) % 4)
                    combine(u, z)
            four_unit_rounds(pe, body)

        def agg_act(act, ph):
            s, base = ph.s, ph.base

            def stage(u, z):
                after(act, s["x_new"], u - 3)
                alone(act)
                at = ds(u - ph.base, 1)
                src = x[:, at, :].rearrange("p a d -> p (a d)")
                m = nc.scalar.activation(xs[:, z, :], src, ACT.Identity,
                                         scale=node[:, at, RSTD], bias=node[:, at, SHIFT])
                if not ph.l1:
                    m = nc.scalar.activation(xd[:, z, :], src, ACT.Identity,
                                             scale=node[:, at, RSTD_DINV], bias=node[:, at, SHIFT_DINV])
                m.then_inc(s["staged"], 1)

            def copy_xt(u, z):
                act.wait_ge(s["t_filled"], u + 1)
                src = misc_a[:, 0:P].rearrange("p (b i) -> p b i", b=2)
                nc.scalar.copy(xt_dup[:, z, :, 0, :], src)
                nc.scalar.copy(xt_dup[:, z, :, 1, :], src).then_inc(s["xt_out"], 1)

            def copy_n(u, z):
                act.wait_ge(s["n_filled"], u + 1)
                after(act, s["n_biased"] if ph.l1 else s["o_filled"], u - 1)
                nc.scalar.copy(n_sb[:, z % 2], misc_b[:, 0:2 * D].rearrange("p (b d) -> p b d", b=2)) \
                    .then_inc(s["n_out"], 1)

            for u in range(3):
                stage(base + u, u)
            copy_xt(base, 0)
            copy_xt(base + 1, 1)
            copy_n(base, 0)

            def body(r):
                for z in range(4):
                    u = base + 4 * r + z
                    static = isinstance(r, int)
                    if not static or r < NU // 4 - 1 or z < 2:
                        copy_xt(u + 2, (z + 2) % 4)
                    if not static or r < NU // 4 - 1 or z < 1:
                        stage(u + 3, (z + 3) % 4)
                    if not static or r < NU // 4 - 1 or z < 3:
                        copy_n(u + 1, (z + 1) % 4)
            four_unit_rounds(act, body)

        def agg_dve(v, ph):
            s, base = ph.s, ph.base

            def fetch(u, z):
                after(v, s["o_filled"], u - 3)
                nc.vector.tensor_copy(block_now[:, z, :], ph.blocks[:, ds(u - ph.base, 1), :].rearrange("p a c -> p (a c)")) \
                    .then_inc(s["block_in"], 1)

            def take(u, z):
                v.wait_ge(s["o_filled"], u + 1)
                after(v, s["x_new"], u - 1)
                o = sums[z % 2][:, 0:D]
                if ph.l1:
                    nc.vector.tensor_tensor(agg_a[:, z % 2, :], o, rows[:, R_BSELF, :], ALU.add) \
                        .then_inc(s["o_sum"], 1)
                else:
                    nc.vector.scalar_tensor_tensor(out=agg_a[:, z % 2, :], in0=o,
                                                   scalar=node[:, ds(u - ph.base, 1), DINV],
                                                   in1=rows[:, R_L3B, :], op0=ALU.mult, op1=ALU.add) \
                        .then_inc(s["o_sum"], 1)

            def add(u, z):
                v.wait_ge(s["o_sum"], u + 1)
                nc.vector.scalar_tensor_tensor(out=x[:, ds(u - ph.base, 1), :].rearrange("p a d -> p (a d)"),
                                               in0=agg_a[:, z % 2, :], scalar=0.0, in1=xs[:, z, :],
                                               op0=ALU.max, op1=ALU.add).then_inc(s["x_new"], 1)

            def stats(u):
                v.wait_ge(s["x_new"], u + 1)
                alone(v)
                nc.vector.bn_stats(halves[:, ds(u - ph.base, 1), :].rearrange("p a d -> p (a d)"),
                                   x[:, ds(u - ph.base, 1), :].rearrange("p a d -> p (a d)")) \
                    .then_inc(stats_done[ph.moments_out], 1)

            def body(r):
                for z in range(4):
                    u = base + 4 * r + z
                    take(u, z)
                    if not isinstance(r, int) or r > 0 or z > 0:
                        stats(u - 1)
                    add(u, z)
                    if not isinstance(r, int) or r < NU // 4 - 1 or z < 1:
                        fetch(u + 3, (z + 3) % 4)
            for u in range(3):
                fetch(base + u, u)
            four_unit_rounds(v, body)
            stats(base + NU - 1)

        block = ctx.enter_context(nc.Block())
        NRAW, NROW, NCOL = 5, 11, 6

        @block.sync
        def _(sp):
            sp.dma_start(ident[:, :], ident_d).then_inc(loaded["ident"], 16)
            load_adj_rows(sp, 0, 0, first["adj_in0"])
            load_adj_rows(sp, 1, 1, first["adj_in1"])
            for h in range(4):
                sp.dma_start(x[:, 16 * h:16 * h + 16, :], x_dram[:, 16 * h:16 * h + 16, :]).then_inc(loaded["x"], 16)
            for l in range(2):
                sp.dma_start(wraw[:, 3 * l:3 * l + 2, :], inp["L0_gnn_w1"][l].rearrange("o (h d) -> o h d", h=2)) \
                    .then_inc(loaded["raw"], 16)
                sp.dma_start(wraw[:, 3 * l + 2, :], inp["L0_gnn_w2"][l]).then_inc(loaded["raw"], 16)
            sp.dma_start(wraw[:, 6, :], inp["L3_gnn_W"]).then_inc(loaded["raw"], 16)
            sp.dma_start(sel_f[:, :, :], sel_d).then_inc(loaded["sel"], 16)
            for k, v in ((WSELF, inp["L1_gnn_W_self_w"]), (WNB, inp["L1_gnn_W_nb_w"]),
                         (A1I, inp["L1_gnn_A1_w"][0:D, :]), (A1J, inp["L1_gnn_A1_w"][D:2 * D, :]),
                         (W1A, inp["L2_gnn_W1"][0:D, :]), (W1B, inp["L2_gnn_W1"][D:2 * D, :]),
                         (W2G, inp["L2_gnn_W2"])):
                sp.dma_start(wl[:, k, :], v).then_inc(loaded["flat"], 16)
            for g in range(NG):
                sp_blocks(sp, first, g, g % 2, adj_blocks)
                if g + 2 < NG:
                    load_adj_rows(sp, g + 2, g % 2, [first["adj_in0"], first["adj_in1"]][g % 2])
            near_sp(sp, near_phases["l0a"])
            near_sp(sp, near_phases["l0b"])
            feat_sp(sp, feat_phases["l1a"])
            feat_sp(sp, feat_phases["l2a"])
            near_sp(sp, near_phases["l2b"])
            for g in range(NG):
                sp.wait_ge(y_ready, GU * (g + 1))
                sp.dma_start(out_dram[:, GU * g:GU * g + GU, :], y_out[:, g % 2]).then_inc(out_done[g % 2], 16)
            for z in range(2):
                sp.wait_ge(out_done[z], 8 * NG)

        def pool_windows(g_eng, phase_ready):
            nc.gpsimd.memset(windows.rearrange("p z q c -> p (z q c)"), 0.0).then_inc(phase_ready, 1)

        windows_zero = [sem("windows_zero0"), sem("windows_zero1")]

        @block.gpsimd
        def _(g_eng):
            for k, v in ((R_B1[0], inp["L0_gnn_b1"][0:1, :]), (R_B1[1], inp["L0_gnn_b1"][1:2, :]),
                         (R_B2[0], inp["L0_gnn_b2"][0:1, :]), (R_B2[1], inp["L0_gnn_b2"][1:2, :]),
                         (R_BSELF, inp["L1_gnn_W_self_b"][None, :]), (R_BNB, inp["L1_gnn_W_nb_b"][None, :]),
                         (R_B2C, inp["L2_gnn_b2"][None, :]), (R_GAMMA, inp["L2_gnn_gamma"][None, :]),
                         (R_BETA, inp["L2_gnn_beta"][None, :]), (R_L3B, inp["L3_gnn_b"][None, :]),
                         (R_B1L2, inp["L2_gnn_b1"][None, :])):
                g_eng.dma_start(rows[:, k, :], v.to_broadcast([P, D])).then_inc(loaded["row"], 16)
            for k, v in ((C_BSELF, inp["L1_gnn_W_self_b"][:, None]), (C_BNB, inp["L1_gnn_W_nb_b"][:, None]),
                         (C_A1B, inp["L1_gnn_A1_b"][:, None]), (C_B1, inp["L2_gnn_b1"][:, None]),
                         (C_A2, inp["L1_gnn_A2_w"]),
                         (C_A2B, inp["L1_gnn_A2_b"][None, :].to_broadcast([P, 1]))):
                g_eng.dma_start(cols[:, k:k + 1], v).then_inc(loaded["col"], 16)
            nc.gpsimd.memset(block_stage[:, :, :, :].rearrange("p z u c -> p (z u c)"), 0.0).then_inc(consts, 1)
            for w in (window_a2, window_two, window_mean, pick_last):
                nc.gpsimd.memset(w[:, :], 0.0).then_inc(consts, 1)
            nc.gpsimd.memset(ones[:, :], 1.0).then_inc(consts, 1)
            nc.gpsimd.memset(node[:, :, :], 0.0).then_inc(node_zero, 1)
            g_eng.wait_ge(consts, 6)
            nc.gpsimd.memset(window_mean[:, 31:32], 1.0 / D).then_inc(consts, 1)
            g_eng.wait_ge(loaded["col"], 16 * NCOL)
            nc.gpsimd.memset(cols[:, C_EPS:C_EPS + 1], EPS).then_inc(consts, 1)
            nc.gpsimd.tensor_copy(window_a2[:, 31:32], cols[:, C_A2:C_A2 + 1]).then_inc(consts, 1)
            for k in (31, 32):
                nc.gpsimd.tensor_scalar(window_two[:, k:k + 1], cols[:, C_A2:C_A2 + 1], -1.0, None, ALU.mult) \
                    .then_inc(consts, 1)
            g_eng.wait_ge(loaded["ident"], 16)
            nc.gpsimd.tensor_copy(pick_last[:, :].rearrange("p (k c) -> p k c", c=8)[:, :, 6:8],
                                  ident[:, :].rearrange("p (k c) -> p k c", c=8)[:, :, 6:8]).then_inc(consts, 1)
            g_eng.wait_ge(loaded["sel"], 16)
            nc.gpsimd.tensor_copy(sel[:, :, :], sel_f[:, :, :]).then_inc(consts, 1)
            pool_windows(g_eng, windows_zero[0])
            g_eng.wait_ge(loaded["row"], 16 * NROW)
            near_pool(g_eng, near_phases["l0a"])
            near_pool(g_eng, near_phases["l0b"])
            feat_pool(g_eng, feat_phases["l1a"])
            agg_pool(g_eng, agg_phases["l1b"])
            feat_pool(g_eng, feat_phases["l2a"])
            g_eng.wait_ge(feat["l2a"]["sum_out"], NG)
            pool_windows(g_eng, windows_zero[1])
            near_pool(g_eng, near_phases["l2b"])
            agg_pool(g_eng, agg_phases["l3"])

        @block.vector
        def _(v):
            v.wait_ge(loaded["flat"], 16 * 7)
            v.wait_ge(loaded["row"], 16 * NROW)
            nc.vector.tensor_reduce(w2_mean[:, 0:1], wl[:, W2G, :], AX.X, ALU.add).then_inc(prep, 1)
            nc.vector.tensor_reduce(w2_mean[:, 1:2], rows[:, R_B2C, :], AX.X, ALU.add).then_inc(prep, 1)
            v.wait_ge(prep, 2)
            nc.vector.tensor_scalar(w2_mean[:, :], w2_mean[:, :], 1.0 / D, None, ALU.mult).then_inc(prep, 1)
            v.wait_ge(prep, 3)
            nc.vector.tensor_scalar(wl[:, W2, :], wl[:, W2G, :], w2_mean[:, 0:1], None, ALU.subtract).then_inc(prep, 1)
            nc.vector.tensor_scalar(rows[:, 11, :], rows[:, R_B2C, :], w2_mean[:, 1:2], None, ALU.subtract) \
                .then_inc(prep, 1)
            v.wait_ge(prep, 5)
            nc.vector.tensor_tensor(wl[:, W2G, :], wl[:, W2, :], rows[:, R_GAMMA, :], ALU.mult).then_inc(prep, 1)
            nc.vector.tensor_tensor(rows[:, R_B2C, :], rows[:, 11, :], rows[:, R_GAMMA, :], ALU.mult).then_inc(prep, 1)
            near_dve(v, near_phases["l0a"])
            near_dve(v, near_phases["l0b"])
            dve_var(v, 0)
            dve_rstd(v, 0)
            feat_dve(v, feat_phases["l1a"])
            blocks_complete(v, 2)
            agg_dve(v, agg_phases["l1b"])
            dve_var(v, 1)
            dve_rstd(v, 1)
            feat_dve(v, feat_phases["l2a"])
            v.wait_ge(dinv_steps, 2)
            nc.vector.reciprocal(node[:, :, DINV], degree[:, :]).then_inc(dinv_steps, 1)
            near_dve(v, near_phases["l2b"])
            dve_var(v, 2)
            dve_rstd(v, 2)
            v.wait_ge(norm_ready[2], 1)
            for dst, src in ((RSTD_DINV, RSTD), (SHIFT_DINV, SHIFT)):
                nc.vector.tensor_tensor(node[:, :, dst], node[:, :, src], node[:, :, DINV], ALU.mult) \
                    .then_inc(norm_ready[2], 1)
            agg_dve(v, agg_phases["l3"])
            dve_var(v, 3)
            dve_rstd(v, 3)
            v.wait_ge(norm_ready[3], 1)
            for g in range(NG):
                if g >= 2:
                    v.wait_ge(out_done[g % 2], 16 * (g // 2))
                for n in range(GU):
                    u = GU * g + n
                    nc.vector.tensor_scalar(y_out[:, g % 2, n, :], x[:, u, :], node[:, u, RSTD:RSTD + 1],
                                            node[:, u, SHIFT:SHIFT + 1], ALU.mult, ALU.add).then_inc(y_ready, 1)

        @block.scalar
        def _(act):
            act.wait_ge(consts, 1)
            act.wait_ge(node_zero, 1)
            for g in range(NG):
                act_blocks(act, first, g, g % 2, 0, wide[g % 2])
                if g >= 1:
                    act_row_sums(act, first, g - 1, SUM_ADJ, sums[(g - 1) % 2])
            act_row_sums(act, first, NG - 1, SUM_ADJ, sums[(NG - 1) % 2])
            for k in range(7):
                act.wait_ge(wt_filled, k + 1)
                nc.scalar.copy(wt[:, k, :], (misc_a if k % 2 else misc_b)[:, 0:P]).then_inc(wt_out, 1)
            act.wait_ge(b2c_filled, 1)
            nc.scalar.copy(cols[:, C_B2C:C_B2C + 1], misc_a[:, 0:1]).then_inc(b2c_out, 1)

            act.wait_ge(windows_zero[0], 1)
            act.wait_ge(loaded["x"], 64)
            act.wait_ge(loaded["row"], 16 * NROW)
            act.wait_ge(first["sum_out"], NG)
            blocks_complete(act, 1)
            near_act(act, near_phases["l0a"])
            act.wait_ge(near_sems["x_new"], NU)
            near_act(act, near_phases["l0b"])
            act_std(act, 0)
            act.wait_ge(norm_ready[0], 1)
            feat_act(act, feat_phases["l1a"])
            blocks_complete(act, 2)
            agg_act(act, agg_phases["l1b"])
            act_std(act, 1)
            act.wait_ge(norm_ready[1], 1)
            feat_act(act, feat_phases["l2a"])
            nc.scalar.activation(degree[:, :], node[:, :, SUM_ADJ], ACT.Copy, bias=1.0 + 1e-6).then_inc(dinv_steps, 1)
            act.wait_ge(dinv_steps, 1)
            nc.scalar.activation(degree[:, :], degree[:, :], ACT.Sqrt).then_inc(dinv_steps, 1)
            act.wait_ge(dinv_steps, 3)
            act.wait_ge(windows_zero[1], 1)
            act.wait_ge(feat["l2a"]["sum_out"], NG)
            blocks_complete(act, 3)
            near_act(act, near_phases["l2b"])
            act_std(act, 2)
            act.wait_ge(norm_ready[2], 3)
            agg_act(act, agg_phases["l3"])
            act_std(act, 3)

        @block.tensor
        def _(pe):
            pe.wait_ge(consts, 6)
            pe.wait_ge(loaded["ident"], 16)
            for g in range(NG):
                pe_turn(pe, first, g, adj_rows[:, g % 2, :], [first["adj_in0"], first["adj_in1"]][g % 2],
                        64 * (g // 2 + 1), wide[g % 2], banks=2)
                if g >= 1:
                    pe_row_sums(pe, first, g - 1, (g - 1) % 2, sums[(g - 1) % 2], banks=2)
            pe_row_sums(pe, first, NG - 1, (NG - 1) % 2, sums[(NG - 1) % 2], banks=2)
            pe.wait_ge(loaded["raw"], 16 * NRAW)
            for k in range(7):
                after(pe, wt_out, k - 1)
                nc.tensor.transpose((misc_a if k % 2 else misc_b)[:, 0:P], wraw[:, k, :], ident[:, :]) \
                    .then_inc(wt_filled, 1)
            pe.wait_ge(prep, 7)
            pe.wait_ge(wt_out, 7)
            nc.tensor.matmul(misc_a[:, 0:1], rows[0:1, 11, :], ones[0:1, :], start=True, stop=True) \
                .then_inc(b2c_filled, 1)
            pe.wait_ge(b2c_out, 1)
            pe.wait_ge(consts, 13)
            pe.wait_ge(first["sum_out"], NG)
            near_pe(pe, near_phases["l0a"])
            near_pe(pe, near_phases["l0b"])
            feat_pe(pe, feat_phases["l1a"])
            agg_pe(pe, agg_phases["l1b"])
            feat_pe(pe, feat_phases["l2a"])
            near_pe(pe, near_phases["l2b"])
            agg_pe(pe, agg_phases["l3"])


def constants():
    ident = np.eye(P, dtype=np.float32)
    sel = np.zeros((QROWS, 4, P), np.float32)
    for q in range(4):
        for par in range(2):
            for part in range(3):
                sel[(3 * par + part) * 4 + q, q, par * N:(par + 1) * N] = 1.0
    return {"ident_d": ident, "sel_d": sel}


def kernel(**inputs):
    import concourse.bacc as bacc
    from concourse.bass_utils import run_bass_kernel_spmd

    nc = bacc.Bacc("TRN2", target_bir_lowering=False, num_devices=1)
    arrays, aps = {}, {}
    for name in INPUTS:
        arrays[f"in_{name}"] = np.ascontiguousarray(inputs[name])
    for name, value in constants().items():
        arrays[f"in_{name}"] = value
    for name, a in arrays.items():
        aps[name[3:]] = nc.dram_tensor(name, a.shape, mybir.dt.from_np(a.dtype), kind="ExternalInput").ap()
    out = nc.dram_tensor("out", (NB, N, D), F32, kind="ExternalOutput").ap()
    parts_dram = nc.dram_tensor("parts_dram", (2, 2, 3, N, D), BF16, kind="Internal").ap()
    program(nc, out, parts_dram, **aps)
    r = run_bass_kernel_spmd(nc, [arrays], core_ids=[0])
    return r.results[0]["out"]
```

```python
from contextlib import ExitStack

import numpy as np
import concourse.bass as bass
from concourse import mybir

ALU = mybir.AluOpType
ACT = mybir.ActivationFunctionType
F32 = mybir.dt.float32
BF16 = mybir.dt.bfloat16
AX = mybir.AxisListType

P = 128
NB, N, D = 128, 64, 128
NU = NB // 2
GU = 8
NG = NU // GU
QU = 4
CH = 512
SCRATCH = 10368
QROWS = 24
EPS = 1e-5
NEG = 1e9

INPUTS = ["x", "adj", "L0_gnn_w1", "L0_gnn_b1", "L0_gnn_w2", "L0_gnn_b2",
          "L1_gnn_W_self_w", "L1_gnn_W_self_b", "L1_gnn_W_nb_w", "L1_gnn_W_nb_b",
          "L1_gnn_A1_w", "L1_gnn_A1_b", "L1_gnn_A2_w", "L1_gnn_A2_b",
          "L2_gnn_W1", "L2_gnn_b1", "L2_gnn_W2", "L2_gnn_b2", "L2_gnn_gamma", "L2_gnn_beta",
          "L3_gnn_W", "L3_gnn_b"]


def ds(start, size):
    return bass.ds(start, size)


def program(nc, out, parts_dram, ident_d, sel_d, block_of_d, **inp):
    ctx = ExitStack()

    def sb(name, shape, dt=F32):
        return ctx.enter_context(nc.sbuf_tensor(name, shape, dt))

    def sem(name):
        return ctx.enter_context(nc.semaphore(name))

    def after(eng, semaphore, count):
        if isinstance(count, int) and count <= 0:
            return
        eng.wait_ge(semaphore, count)

    with ctx:
        x = sb("x", [P, NU, D])
        adj_blocks = sb("adj_blocks", [P, NU, P])
        w_blocks = sb("w_blocks", [P, NU, P])
        pairs = sb("pairs", [P, 4, 4 * CH])
        adj_rows = sb("adj_rows", [P, 2, CH])
        block_stage = sb("block_stage", [P, 2, GU, P])
        xs = sb("xs", [P, 4, D])
        xt_dup = sb("xt_dup", [P, 4, 2, 2, N])
        xt_flat = xt_dup[:, :, :, :, :].rearrange("p z b c i -> p z (b c i)")
        plain_xt = slice(N, 3 * N)
        scratch = sb("scratch", [P, SCRATCH])
        ident = sb("ident", [P, P])
        sel = sb("sel", [P, 4, P], BF16)
        wraw = pairs[:, 0, 0:8 * P].rearrange("p (k c) -> p k c", k=8)
        sel_f = pairs[0:QROWS, 1, 0:4 * P].rearrange("p (k c) -> p k c", k=4)
        adj_nodes = w_blocks[:, 0:NU // 2, :].rearrange("p u c -> p (u c)").rearrange("p (u j) -> p u j", j=N)
        wt = sb("wt", [P, 8, P])
        WI, WJ, W2T = (0, 3), (1, 4), (2, 5)
        L3T = 6
        wl = sb("wl", [P, 8, P])
        WSELF, WNB, A1I, A1J, W1A, W1B, W2, W2G = range(8)
        rows = sb("rows", [P, 12, P])
        R_B1, R_B2, R_BSELF, R_BNB, R_B2C, R_GAMMA, R_BETA, R_L3B, R_B1L2 = (0, 1), (2, 3), 4, 5, 6, 7, 8, 9, 10
        cols = sb("cols", [P, 8])
        C_BSELF, C_BNB, C_A1B, C_B1, C_A2, C_A2B, C_B2C, C_EPS = range(8)
        window_a2 = sb("window_a2", [P, 63])
        window_two = sb("window_two", [P, 64])
        window_mean = sb("window_mean", [P, 63])
        block_of = sb("block_of", [P, 4])
        ones = sb("ones", [P, 1])
        w2_mean = sb("w2_mean", [P, 2])
        node = sb("node", [P, NU, 5])
        RSTD, SHIFT, SUM_W, SUM_ADJ, DINV = range(5)
        RSTD_DINV, SHIFT_DINV = SUM_W, SUM_ADJ
        degree = sb("degree", [P, NU])
        halves = sb("halves", [P, NU, 6])
        half_sum, half_gap, gap_sq, var, var_eps, std, node_mean = \
            (pairs[:, 3, n * NU:(n + 1) * NU] for n in range(7))

        off = [0]

        def view(*shape, dt=F32):
            n = int(np.prod(shape)) // (2 if dt == BF16 else 1)
            v = scratch[:, off[0]:off[0] + n]
            off[0] += n
            if dt == BF16:
                v = v.bitcast(BF16)
            return v
        windows = view(4, 4, 160).rearrange("p (z q c) -> p z q c", z=4, q=4)
        spread = view(2, 2048, dt=BF16).rearrange("p (z c) -> p z c", z=2)
        c_pos = view(4, 2, D).rearrange("p (z b d) -> p z b d", z=4, b=2)
        c_neg = view(4, 2, D).rearrange("p (z b d) -> p z b d", z=4, b=2)
        r_sb = view(4, D).rearrange("p (e d) -> p e d", e=4)
        r_half = view(2, D).rearrange("p (h d) -> p h d", h=2)
        r_own = view(2, D).rearrange("p (z d) -> p z d", z=2)
        a_sb = view(2, D).rearrange("p (z d) -> p z d", z=2)
        a_full = view(D)
        a_rest = view(D)
        parts = view(2, 3, D, dt=BF16).rearrange("p (z t d) -> p z t d", z=2, t=3)
        rt_sb = view(2, D).rearrange("p (z d) -> p z d", z=2)
        o_sb = view(2, D).rearrange("p (z d) -> p z d", z=2)
        f_a = view(4, D).rearrange("p (z d) -> p z d", z=4)
        f_b = view(D)
        f_c = view(4, D).rearrange("p (z d) -> p z d", z=4)
        f_d = view(D)
        x_first = f_c
        off[0] = 0
        xs4 = view(4, D).rearrange("p (u d) -> p u d", u=4)
        xt4 = view(CH)
        hs4 = view(CH)
        hn4 = view(CH)
        p4 = view(2, CH).rearrange("p (z c) -> p z c", z=2)
        q4 = view(2, CH).rearrange("p (z c) -> p z c", z=2)
        squares = view(2, 2 * CH).rearrange("p (h c) -> p h c", h=2)
        is_zero = view(CH)
        mask = view(CH)
        fill = view(CH)
        score_a = view(CH)
        score_b = view(CH)
        weights = view(CH)
        row_max = view(8)
        row_sum = view(8)
        row_inv = view(8)
        off[0] = 0
        block_now = view(4, P).rearrange("p (z c) -> p z c", z=4)
        n_sb = view(2, 2, D).rearrange("p (z b d) -> p z b d", z=2, b=2)
        n_full = view(2, 2, D).rearrange("p (z b d) -> p z b d", z=2, b=2)
        xd = view(4, D).rearrange("p (z d) -> p z d", z=4)
        agg_a = view(2, D).rearrange("p (z d) -> p z d", z=2)

        wide = [ctx.enter_context(nc.psum_tensor(f"wide{h}", [P, 2 * CH], F32)) for h in range(3)]
        misc_a = ctx.enter_context(nc.psum_tensor("misc_a", [P, CH], F32))
        sums = [ctx.enter_context(nc.psum_tensor("sums", [P, CH], F32)), wide[2][:, 0:CH]]
        misc_b = wide[2][:, CH:2 * CH]
        near_sums = sums[0]
        near_t, near_p = misc_a[:, 0:P], misc_a[:, P:4 * P]

        loaded = {k: sem(f"loaded_{k}") for k in ("x_first", "x", "ident", "block_of", "adj", "sel", "raw", "flat", "row", "col")}
        consts = sem("consts")
        wt_filled, wt_out = sem("wt_filled"), sem("wt_out")
        prep = sem("prep")
        b2c_filled, b2c_out = sem("b2c_filled"), sem("b2c_out")
        norm_steps = [sem(f"norm_steps{n}") for n in range(4)]
        node_zero = sem("node_zero")
        waited = sem("waited")
        stats_done = [sem(f"stats_done{n}") for n in range(4)]
        std_done = [sem(f"std_done{n}") for n in range(4)]
        norm_ready = [sem(f"norm_ready{n}") for n in range(4)]
        dinv_steps = sem("dinv_steps")
        out_done = sem("out_done")
        y_ready, y_act_ready = sem("y_ready"), sem("y_act_ready")
        OUT_DVE = 5

        def alone(eng):
            eng.sem_inc(waited)

        def signals(phase, names):
            return {nm: sem(f"{phase}_{nm}") for nm in names.split()}

        near_names = ("selected staged based windowed t_filled xt_out ac_filled a_out c_out split parts_put flat0 flat1 spreaded maxed "
                      "weighted r_out rt_filled rt_out o_filled o_out fin x_new ")
        near_sems = signals("near", near_names + "first_in0 first_in1 first_in2 first_in3")
        block_names = "turned blocks_out summed_w sum_out"
        feat_names = "staged lin_filled lin_out formed scored adj_in0 adj_in1 inverted weighed "
        feat = {"l1a": signals("l1a", feat_names + "pooled relued masked shifted topped cut exped totalled " + block_names),
                "l2a": signals("l2a", feat_names + "relued y_filled squared std_out " + block_names)}
        first = signals("s", "adj_in0 adj_in1 turned blocks_out")
        agg_names = "staged xs_in block_in t_filled xt_out n_filled n_out n_biased o_filled o_sum x_new"
        agg_sems = signals("agg", agg_names)

        x_dram = inp["x"].rearrange("(u b) i d -> (b i) u d", b=2)
        out_dram = out.rearrange("(u b) i d -> (b i) u d", b=2)
        adj_dram = inp["adj"].rearrange("(u b) i j -> (b i) u j", b=2)
        adj_chunks = inp["adj"].rearrange("(g bb) (ib i) j -> g (bb ib) (i j)", g=NG, ib=8) \
            .rearrange("g (t q) c -> g q t c", q=4)

        def load_adj_rows(sp, g, z, signal):
            for q in range(4):
                sp.dma_start(adj_rows[32 * q:32 * q + 32, z, :], adj_chunks[g, q]).then_inc(signal, 16)

        def four_unit_rounds(eng, body, total=NU, step=4, between=None):
            body(0)
            if between:
                between()
            with eng.Fori(1, total // step - 1) as r:
                body(r)
            body(total // step - 1)

        def two_rounds(eng, body, total):
            four_unit_rounds(eng, body, total, 2)

        def pe_turn(pe, s, g, src, ready, count, bank, banks=1, sums_too=False):
            pe.wait_ge(ready, count)
            after(pe, s["blocks_out"], 2 * (g + 1 - banks))
            if sums_too:
                after(pe, s["sum_out"], g)
            for i4 in range(4):
                m = nc.tensor.transpose(bank[:, i4 * P:(i4 + 1) * P], src[:, i4 * P:(i4 + 1) * P], ident[:, :])
            m.then_inc(s["turned"], 1)

        def act_blocks(act, s, g, z, before, bank):
            act.wait_ge(s["turned"], g + 1)
            after(act, moved[z], 8 * (before + g - z))
            for par in range(2):
                h = slice(64 * par, 64 * par + 64)
                dst = block_stage[h, z].rearrange("p u (t q i r) -> p (u t) q i r", t=4, q=4, i=4)[:, :, :, :, par]
                src = bank[h, 0:CH].rearrange("p (i q t) -> p t q i", i=4, q=4)
                for q in range(4):
                    c = nc.scalar.copy(dst[:, :, q], src[:, :, q])
                c.then_inc(s["blocks_out"], 1)

        def pe_row_sums(pe, s, g, z, bank):
            pe.wait_ge(s["blocks_out"], 2 * g + 2)
            for u in range(GU):
                m = nc.tensor.matmul(bank[:, u:u + 1], block_stage[:, z, u, :], ones[:, :], start=True, stop=True)
            m.then_inc(s["summed_w"], 1)

        def act_row_sums(act, s, g, dst, bank):
            act.wait_ge(s["summed_w"], g + 1)
            alone(act)
            nc.scalar.copy(node[:, ds(g * GU, GU), dst], bank[:, 0:GU]).then_inc(s["sum_out"], 1)

        def sp_blocks(sp, s, g, z, dst):
            sp.wait_ge(s["blocks_out"], 2 * g + 2)
            alone(sp)
            sp.dma_start(dst[:, ds(g * GU, GU), :], block_stage[:, z]).then_inc(moved[z], 16)

        moved = [sem("moved_even"), sem("moved_odd")]

        def blocks_complete(eng, phases):
            for z in range(2):
                eng.wait_ge(moved[z], phases * 8 * NG)

        class Near:
            def __init__(self, name, wi, wj, w2, b1_row, blocks, moments_in, moments_out):
                self.name, self.s, self.base = name, near_sems, NU * ("l0a", "l0b", "l2b").index(name)
                self.wi, self.wj, self.w2, self.b1_row, self.blocks = wi, wj, w2, b1_row, blocks
                self.moments_in, self.moments_out = moments_in, moments_out
                self.last = self.next = None

        near_phases = {
            "l0a": Near("l0a", wt[:, WI[0], :], wt[:, WJ[0], :], wt[:, W2T[0], :], rows[:, R_B1[0], :],
                        adj_blocks, None, None),
            "l0b": Near("l0b", wt[:, WI[1], :], wt[:, WJ[1], :], wt[:, W2T[1], :], rows[:, R_B1[1], :],
                        adj_blocks, None, 0),
            "l2b": Near("l2b", wl[:, W1A, :], wl[:, W1B, :], wl[:, W2G, :], rows[:, R_B1L2, :],
                        w_blocks, 1, 2),
        }

        near_phases["l0a"].next, near_phases["l0b"].last = near_phases["l0b"], near_phases["l0a"]

        flat = [near_sems["flat0"], near_sems["flat1"]]
        first_in = [near_sems["first_in0"], near_sems["first_in1"], near_sems["first_in2"], near_sems["first_in3"]]

        def phase_of(ph, r, z, step):
            if isinstance(r, int) and r == NU // 4 - 1 and z + step > 3:
                return ph.next
            if isinstance(r, int) and r == 0 and z + step < 0:
                return ph.last
            return ph

        def near_pe(pe, ph):
            s, base = ph.s, ph.base

            def turn(u, z):
                pe.wait_ge(s["staged"], u + 1)
                after(pe, s["c_out"], u)
                after(pe, s["o_out"], u - 3)
                nc.tensor.transpose(near_t, xs[:, z, :], ident[:, :]).then_inc(s["t_filled"], 1)

            def project(u, z, ph):
                pe.wait_ge(s["xt_out"], u + 1)
                after(pe, s["o_out"], u - 3)
                nc.tensor.matmul(near_p[:, 0:P], xt_flat[:, z % 2, plain_xt], ph.wi, start=True, stop=True)
                for b in range(2):
                    m = nc.tensor.matmul(near_p[:, (1 + b) * P:(2 + b) * P], xt_flat[:, z % 2, b * P:(b + 1) * P], ph.wj,
                                         start=True, stop=True)
                m.then_inc(s["ac_filled"], 1)

            def spread_half(u, z, k, b):
                if k == 0 and b == 0:
                    pe.wait_ge(flat[z % 2], 8 * (u - z % 2) + 16)
                n = 8 * z + 2 * k + b
                back = 3 if n >= 3 else (2, 2, 5)[n]
                after(pe, s["maxed"], 8 * u + 2 * k + b + 1 - back)
                for q in range(2):
                    m = nc.tensor.matmul(wide[n % 3][:, q * CH:(q + 1) * CH], sel[:, 2 * b + q, :],
                                         spread[:, z % 2, k * CH:(k + 1) * CH], start=True, stop=True)
                m.then_inc(s["spreaded"], 1)

            def weigh(u, z, k):
                pe.wait_ge(s["maxed"], 8 * u + 2 * k + 2)
                if k == 0:
                    pe.wait_ge(s["windowed"], u + 1)
                    after(pe, s["r_out"], u)
                for q in range(4):
                    m = nc.tensor.matmul(near_sums[32 * q:32 * q + 32, :], windows[:, z, q, 32 * k:32 * k + 32],
                                         pairs[:, k, q * CH:(q + 1) * CH], start=(k == 0), stop=(k == 3))
                m.then_inc(s["weighted"], 1)

            def latest(u):
                return min(u + 4, base + NU) if isinstance(u, int) and not ph.next else u + 4

            def gather(u, z, ph):
                pe.wait_ge(s["selected"], 3 * (u + 1))
                pe.wait_ge(s["c_out"], latest(u))
                for b in range(2):
                    nc.tensor.matmul(near_p[:, b * N:(b + 1) * N], c_pos[:, z, b, :],
                                     ph.blocks[:, ds(u - ph.base, 1), b * N:(b + 1) * N].rearrange("p a c -> p (a c)"),
                                     start=(b == 0), stop=False)
                nc.tensor.matmul(near_p[:, 0:P], r_own[:, z % 2, :], ident[:, :],
                                 start=False, stop=True).then_inc(s["rt_filled"], 1)

            def output(u, z, ph):
                pe.wait_ge(s["rt_out"], u + 1)
                nc.tensor.matmul(near_t, rt_sb[:, z % 2, :], ph.w2, start=True, stop=True).then_inc(s["o_filled"], 1)

            if not ph.last:
                for u in range(2):
                    turn(base + u, u)
                    project(base + u, u, ph)

            def body(r):
                for z in range(4):
                    u = base + 4 * r + z
                    to, of = phase_of(ph, r, z, 2), phase_of(ph, r, z, -1)
                    zm, zp = (z - 1) % 4, (z + 2) % 4
                    for k in range(4):
                        spread_half(u, z, k, 0)
                        if k == 1 and to:
                            turn(u + 2, zp)
                        if k == 2 and to:
                            project(u + 2, zp, to)
                        if k == 3 and of:
                            gather(u - 1, zm, of)
                        spread_half(u, z, k, 1)
                        if k > 0:
                            weigh(u, z, k - 1)
                        elif of:
                            weigh(u - 1, zm, 3)
                        if k == 3 and of:
                            output(u - 1, zm, of)
            four_unit_rounds(pe, body)
            if not ph.next:
                weigh(base + NU - 1, 3, 3)
                gather(base + NU - 1, 3, ph)
                output(base + NU - 1, 3, ph)

        def near_act(act, ph):
            s, base = ph.s, ph.base

            def copy_xt(u, z):
                act.wait_ge(s["t_filled"], u + 1)
                after(act, s["ac_filled"], u - 1)
                src = near_t.rearrange("p (b i) -> p b i", b=2)
                nc.scalar.copy(xt_dup[:, z % 2, :, 0, :], src)
                nc.scalar.copy(xt_dup[:, z % 2, :, 1, :], src).then_inc(s["xt_out"], 1)

            def copy_ac(u, z):
                act.wait_ge(s["ac_filled"], u + 1)
                after(act, s["split"], 5 * (u - 2) + 1)
                nc.scalar.copy(a_sb[:, z % 2, :], near_p[:, 0:P]).then_inc(s["a_out"], 1)
                after(act, s["maxed"], 8 * (u - 3))
                after(act, s["rt_filled"], u - 3)
                src = near_p[:, P:3 * P].rearrange("p (b d) -> p b d", b=2)
                nc.scalar.mul(c_neg[:, z], src, -1.0)
                nc.scalar.copy(c_pos[:, z], src).then_inc(s["c_out"], 1)

            def copy_r(u, z):
                act.wait_ge(s["weighted"], 4 * u + 4)
                after(act, s["selected"], 3 * u)
                for e in range(4):
                    m = nc.scalar.activation(r_sb[:, e, :], near_sums[:, e * D:(e + 1) * D], ACT.Identity,
                                             scale=block_of[:, e:e + 1])
                m.then_inc(s["r_out"], 1)

            def copy_rt(u, z):
                act.wait_ge(s["rt_filled"], u + 1)
                after(act, s["o_filled"], u - 1)
                nc.scalar.copy(rt_sb[:, z % 2, :], near_p[:, 0:P]).then_inc(s["rt_out"], 1)

            def copy_o(u, z):
                act.wait_ge(s["o_filled"], u + 1)
                after(act, s["x_new"], u - 1)
                nc.scalar.copy(o_sb[:, z % 2, :], near_t).then_inc(s["o_out"], 1)

            def scaled(ph, dst, row, u, col):
                return nc.scalar.activation(dst, row, ACT.Identity, scale=node[:, ds(u - ph.base, 1), col])

            def stage(u, z, ph):
                after(act, s["x_new"], u - 3)
                after(act, s["weighted"], 4 * (u - 3))
                alone(act)
                src = x[:, ds(u - ph.base, 1), :].rearrange("p a d -> p (a d)")
                if ph.moments_in is None:
                    nc.scalar.copy(xs[:, z, :], src).then_inc(s["staged"], 1)
                else:
                    nc.scalar.activation(xs[:, z, :], src, ACT.Identity, scale=node[:, ds(u - ph.base, 1), RSTD],
                                         bias=node[:, ds(u - ph.base, 1), SHIFT]).then_inc(s["staged"], 1)
                dst = windows[:, z].rearrange("p q (k c) -> p q k c", k=4)[:, :, :, 0:8]
                blk = ph.blocks[:, ds(u - ph.base, 1), :].rearrange("p a (q k m) -> p (a q) k m", q=4, k=4)
                nc.scalar.copy(dst, blk).then_inc(s["windowed"], 1)

            def stage_rows(u, z, ph):
                after(act, s["x_new"], u - 3)
                alone(act)
                if ph.name == "l2b":
                    scaled(ph, f_c[:, z, :], rows[:, R_BETA, :], u, SUM_ADJ)
                    scaled(ph, f_a[:, z, :], rows[:, R_B2C, :], u, SUM_W).then_inc(s["based"], 1)
                else:
                    scaled(ph, f_a[:, z, :], rows[:, R_B2[1 if ph.name == "l0b" else 0], :], u, SUM_ADJ) \
                        .then_inc(s["based"], 1)

            if not ph.last:
                for u in range(3):
                    stage(base + u, u, ph)
                for u in range(2):
                    copy_xt(base + u, u)
                    copy_ac(base + u, u)
                if ph.name == "l0a":
                    act.wait_ge(prep, 8)
                for u in range(2):
                    stage_rows(base + u, u, ph)

            def body(r):
                for z in range(4):
                    u = base + 4 * r + z
                    to, of = phase_of(ph, r, z, 2), phase_of(ph, r, z, -1)
                    zm, zp = (z - 1) % 4, (z + 2) % 4
                    if of:
                        copy_r(u - 1, zm)
                    if to:
                        copy_xt(u + 2, zp)
                        copy_ac(u + 2, zp)
                    if of:
                        copy_rt(u - 1, zm)
                    if to:
                        stage_rows(u + 2, zp, to)
                    if of:
                        copy_o(u - 1, zm)
                    if phase_of(ph, r, z, 3):
                        stage(u + 3, (z + 3) % 4, phase_of(ph, r, z, 3))

            def rest_loaded():
                act.wait_ge(loaded["x"], 48)
                blocks_complete(act, 1)
            four_unit_rounds(act, body, between=rest_loaded if ph.name == "l0a" else None)
            if not ph.next:
                copy_r(base + NU - 1, 3)
                copy_rt(base + NU - 1, 3)
                copy_o(base + NU - 1, 3)

        def near_dve(v, ph):
            s, base = ph.s, ph.base

            def form(u, z, k, b):
                v.wait_ge(s["spreaded"], 8 * u + 2 * k + b + 1)
                if k == 0 and b == 0:
                    v.wait_ge(s["c_out"], u + 1)
                if b == 0:
                    after(v, s["weighted"], 4 * u + k - 3)
                nc.vector.tensor_tensor(
                    pairs[:, k, b * 2 * CH:(b + 1) * 2 * CH].rearrange("p (i d) -> p i d", d=D),
                    wide[(8 * z + 2 * k + b) % 3][:, :].rearrange("p (i d) -> p i d", d=D),
                    c_neg[:, z, b, :].unsqueeze(1).to_broadcast([P, 8, D]), ALU.max).then_inc(s["maxed"], 1)

            def stats(u):
                v.wait_ge(s["x_new"], u + 1)
                alone(v)
                nc.vector.bn_stats(halves[:, ds(u - ph.base, 1), :].rearrange("p a d -> p (a d)"),
                                   x[:, ds(u - ph.base, 1), :].rearrange("p a d -> p (a d)")) \
                    .then_inc(stats_done[ph.moments_out], 1)

            def body(r):
                for z in range(4):
                    u = base + 4 * r + z
                    behind = ph.moments_out is not None and (not isinstance(r, int) or r > 0 or z >= 2)
                    for k in range(4):
                        for b in range(2):
                            form(u, z, k, b)
                        if behind and k == 1:
                            stats(u - 2)
                        if ph.name == "l0a" and isinstance(r, int) and u == 0 and k == 0:
                            v.wait_ge(loaded["adj"], 64)
                            v.wait_ge(node_zero, 1)
                            nc.vector.tensor_reduce(node[:, :, SUM_ADJ], adj_nodes, AX.X, ALU.add).then_inc(prep, 1)
            four_unit_rounds(v, body)
            if ph.moments_out is not None:
                for u in (base + NU - 2, base + NU - 1):
                    stats(u)

        def near_pool(g_eng, ph):
            s, base = ph.s, ph.base

            def split(u, z, ph):
                g_eng.wait_ge(s["a_out"], u + 1)
                after(g_eng, s["parts_put"], 32 * (u - 1))
                b1 = ph.b1_row
                high, mid, low = (parts[:, z % 2, n, :] for n in range(3))
                nc.gpsimd.tensor_tensor(a_full, a_sb[:, z % 2, :], b1, ALU.add).then_inc(s["split"], 1)
                nc.gpsimd.tensor_tensor(high, a_sb[:, z % 2, :], b1, ALU.add).then_inc(s["split"], 1)
                g_eng.wait_ge(s["split"], 5 * u + 2)
                nc.gpsimd.tensor_tensor(a_rest, a_full, high, ALU.subtract).then_inc(s["split"], 1)
                nc.gpsimd.tensor_tensor(mid, a_full, high, ALU.subtract).then_inc(s["split"], 1)
                g_eng.wait_ge(s["split"], 5 * u + 4)
                nc.gpsimd.tensor_tensor(low, a_rest, mid, ALU.subtract).then_inc(s["split"], 1)

            def sums_of(ph, u):
                each, before = {"l0a": (1, 0), "l0b": (2, NU), "l2b": (2, 3 * NU)}[ph.name]
                return each, each * (u - ph.base) + before

            def select(u, z):
                g_eng.wait_ge(s["r_out"], u + 1)
                after(g_eng, s["rt_filled"], u - 1)
                for h in range(2):
                    nc.gpsimd.tensor_tensor(r_half[:, h, :], r_sb[:, 2 * h, :], r_sb[:, 2 * h + 1, :], ALU.add) \
                        .then_inc(s["selected"], 1)
                g_eng.wait_ge(s["selected"], 3 * u + 2)
                nc.gpsimd.tensor_tensor(r_own[:, z % 2, :], r_half[:, 0, :], r_half[:, 1, :], ALU.add) \
                    .then_inc(s["selected"], 1)

            def begin(u, z, ph):
                each, n = sums_of(ph, u)
                g_eng.wait_ge(s["based"], u + 1)
                after(g_eng, s["x_new"], u)
                if ph.name == "l0b":
                    g_eng.wait_ge(first_in[z], 4 * (u - ph.base - z) + 16)
                nc.gpsimd.tensor_tensor(f_b, f_a[:, z, :], xs[:, z, :], ALU.add).then_inc(s["fin"], 1)
                if each == 2:
                    g_eng.wait_ge(s["fin"], n + 1)
                    nc.gpsimd.tensor_tensor(f_d, f_b, x_first[:, z, :] if ph.name == "l0b" else f_c[:, z, :], ALU.add) \
                        .then_inc(s["fin"], 1)

            def finish(u, z, ph):
                each, n = sums_of(ph, u)
                g_eng.wait_ge(s["fin"], n + each)
                g_eng.wait_ge(s["o_out"], u + 1)
                alone(g_eng)
                dst = x[:, ds(u - ph.base, 1), :].rearrange("p a d -> p (a d)")
                nc.gpsimd.tensor_tensor(dst, f_d if each == 2 else f_b, o_sb[:, z % 2, :], ALU.add) \
                    .then_inc(s["x_new"], 1)

            if not ph.last:
                for u in range(2):
                    split(base + u, u, ph)

            def body(r):
                for z in range(4):
                    u = base + 4 * r + z
                    to, of = phase_of(ph, r, z, 2), phase_of(ph, r, z, -1)
                    if of:
                        begin(u - 1, (z - 1) % 4, of)
                        select(u - 1, (z - 1) % 4)
                    if to:
                        split(u + 2, (z + 2) % 4, to)
                    if of:
                        finish(u - 1, (z - 1) % 4, of)
            four_unit_rounds(g_eng, body)
            if not ph.next:
                begin(base + NU - 1, 3, ph)
                select(base + NU - 1, 3)
                finish(base + NU - 1, 3, ph)

        def near_sp(sp, ph):
            s, base = ph.s, ph.base

            def put_parts(u, z):
                sp.wait_ge(s["split"], 5 * (u + 1))
                alone(sp)
                after(sp, flat[z % 2], 8 * (u - z % 2))
                alone(sp)
                for par in range(2):
                    sp.dma_start(parts_dram[z % 2, par].rearrange("t i d -> i t d"), parts[par::2, z % 2, :, :]) \
                        .then_inc(s["parts_put"], 16)

            def get_parts(u, z):
                sp.wait_ge(s["parts_put"], 32 * (u + 1))
                alone(sp)
                after(sp, s["spreaded"], 8 * (u - 1))
                alone(sp)
                sp.dma_start(spread[0:QROWS, z % 2, :],
                             parts_dram[z % 2].rearrange("a t (q i) d -> (a t q) (i d)", q=4)).then_inc(flat[z % 2], 16)

            def first_input(u, z, ph):
                after(sp, s["x_new"], u - 3)
                alone(sp)
                sp.dma_start(x_first[:, z, :], x_dram[:, ds(u - ph.base, 1), :].rearrange("p a d -> p (a d)")) \
                    .then_inc(first_in[z], 16)

            if not ph.last:
                for u in range(2):
                    put_parts(base + u, u)
                    get_parts(base + u, u)
            if ph.name == "l0a":
                for h in range(1, 4):
                    sp.dma_start(x[:, 16 * h:16 * h + 16, :], x_dram[:, 16 * h:16 * h + 16, :]).then_inc(loaded["x"], 16)

            def body(r):
                for z in range(4):
                    u = base + 4 * r + z
                    staged = phase_of(ph, r, z, 3)
                    if staged and staged.name == "l0b":
                        first_input(u + 3, (z + 3) % 4, staged)
                    if phase_of(ph, r, z, 2):
                        put_parts(u + 2, (z + 2) % 4)
                        get_parts(u + 2, (z + 2) % 4)
            four_unit_rounds(sp, body)

        def dve_var(v, n):
            steps = norm_steps[n]
            even, odd = halves[:, :, 1], halves[:, :, 4]
            v.wait_ge(stats_done[n], NU)
            nc.vector.tensor_tensor(half_sum, even, odd, ALU.add).then_inc(steps, 1)
            nc.vector.tensor_tensor(half_gap, even, odd, ALU.subtract).then_inc(steps, 1)
            nc.vector.tensor_tensor(var, halves[:, :, 2], halves[:, :, 5], ALU.add).then_inc(steps, 1)
            v.wait_ge(steps, 3)
            nc.vector.tensor_scalar(node_mean, half_sum, 0.5, None, ALU.mult).then_inc(steps, 1)
            nc.vector.scalar_tensor_tensor(out=gap_sq, in0=half_gap, scalar=0.25, in1=half_gap,
                                           op0=ALU.mult, op1=ALU.mult).then_inc(steps, 1)
            v.wait_ge(steps, 5)
            nc.vector.scalar_tensor_tensor(out=var_eps, in0=var, scalar=1.0 / D, in1=gap_sq,
                                           op0=ALU.mult, op1=ALU.add).then_inc(steps, 1)

        def act_std(act, n):
            act.wait_ge(norm_steps[n], 6)
            nc.scalar.activation(std, var_eps, ACT.Sqrt, bias=cols[:, C_EPS:C_EPS + 1]) \
                .then_inc(std_done[n], 1)

        def dve_rstd(v, n):
            v.wait_ge(std_done[n], 1)
            nc.vector.reciprocal(node[:, :, RSTD], std).then_inc(norm_steps[n], 1)
            v.wait_ge(norm_steps[n], 7)
            nc.vector.scalar_tensor_tensor(out=node[:, :, SHIFT], in0=node_mean, scalar=-1.0,
                                           in1=node[:, :, RSTD], op0=ALU.mult, op1=ALU.mult) \
                .then_inc(norm_ready[n], 1)

        class Feat:
            def __init__(self, name, moments_in):
                self.name, self.s, self.moments_in = name, feat[name], moments_in
                self.l1 = name == "l1a"
                self.groups_before = NG if self.l1 else 2 * NG
                self.project_at = (0, 2, 5, 7, 10) if self.l1 else (1, 4, 7)
                self.dve_tiles = 12 if self.l1 else TILES
                if self.l1:
                    self.chain = [(WSELF, "x", "hs"), (WNB, "x", "hn"), (A1I, "hs", "p"), (A1J, "hn", "q")]
                else:
                    self.chain = [(W1A, "x", "p"), (W1B, "x", "q")]
                self.steps = 1 + len(self.chain)

        NQ = NU // QU
        TILES = 16
        feat_phases = {"l1a": Feat("l1a", 0), "l2a": Feat("l2a", 1)}
        DVE_GRAPHS, POOL_GRAPHS = (0, 1, 2, 4, 5, 6), (3, 7)
        pool_tile = [pairs[:, 3, :], squares.rearrange("p h c -> p (h c)")]

        def place(pos):
            if pos % 4 == 3:
                m = pos // 4
                return True, m, POOL_GRAPHS[m // 2], m % 2
            n = pos - pos // 4
            return False, n, DVE_GRAPHS[n // 2], n % 2

        BLOCKS_AT = ((0, 12), (1, 1))

        def feat_pe(pe, ph):
            s = ph.s
            src_of = {"x": xt4, "hs": hs4, "hn": hn4}

            def project(quad, j):
                after(pe, s["lin_out"], ph.steps * quad + j)
                if j == 0:
                    pe.wait_ge(s["staged"], QU * (quad + 1))
                    for n in range(QU):
                        m = nc.tensor.transpose(misc_a[:, n * P:(n + 1) * P], xs4[:, n, :], ident[:, :])
                else:
                    w, src, _ = ph.chain[j - 1]
                    m = nc.tensor.matmul(misc_a[:, :], wl[:, w, :], src_of[src], start=True, stop=True)
                m.then_inc(s["lin_filled"], 1)

            def score_c(qz, bb, gz):
                t = 16 * qz + 2 * bb
                mov = q4[:, qz, bb * N:(bb + 1) * N].unsqueeze(1).to_broadcast([P, 8, N])
                for q in range(4):
                    nc.tensor.matmul(sums[gz][32 * q:32 * q + 32, :].rearrange("p (i j) -> p i j", j=N),
                                     window_two[:, 31 - t:63 - t], mov, start=False, stop=False)

            def score(quad, qz, pos, gz):
                pooled, n, bb, ih = place(pos)
                t = TILES * qz + 2 * bb + ih
                if pooled:
                    pe.wait_ge(s["relued"], 4 * quad + n + 1)
                    tile = pool_tile[n % 2]
                else:
                    pe.wait_ge(s["formed"], 12 * quad + n + 1)
                    tile = pairs[:, n % 3, :]
                for q in range(4):
                    m = nc.tensor.matmul(sums[gz][32 * q:32 * q + 32, :], window_a2[:, 31 - t:63 - t],
                                         tile[:, q * CH:(q + 1) * CH], start=(t == 0), stop=(t == 31))
                m.then_inc(s["scored"], 1)
                if not pooled and ih == 1:
                    score_c(qz, bb, gz)

            def square_in(quad, tau, h):
                tile = TILES * quad + tau
                if h == 0:
                    pe.wait_ge(s["relued"], tile + 1)
                after(pe, s["squared"], 2 * tile + h - 1)
                for c in range(2):
                    m = nc.tensor.matmul(wide[h][:, c * CH:(c + 1) * CH], wl[:, W2, :],
                                         pairs[:, tau % 4, (2 * h + c) * CH:(2 * h + c + 1) * CH],
                                         start=True, stop=True)
                m.then_inc(s["y_filled"], 1)

            def mean(tile, t, gz):
                pe.wait_ge(s["squared"], 2 * tile + 2)
                for q in range(4):
                    m = nc.tensor.matmul(sums[gz][32 * q:32 * q + 32, :], window_mean[:, 31 - t:63 - t],
                                         squares[:, q // 2, (q % 2) * CH:(q % 2 + 1) * CH],
                                         start=(t == 0), stop=(t == 31))
                m.then_inc(s["scored"], 1)

            def finish(g, gz):
                pe_turn(pe, s, g, weights, s["weighed"], g + 1, misc_b, sums_too=not ph.l1)

            for j in range(ph.steps):
                project(0, j)

            def body_gz(g, gz):
                for qz in range(2):
                    quad = 2 * g + qz
                    static = isinstance(g, int)
                    ahead = not static or quad + 1 < NQ
                    behind = not static or g >= 1
                    pe.wait_ge(s["lin_out"], ph.steps * (quad + 1))
                    if qz == 0:
                        after(pe, s["shifted"] if ph.l1 else s["std_out"], g - 1)
                    for tau in range(TILES):
                        t = TILES * qz + tau
                        if ph.l1:
                            score(quad, qz, tau, gz)
                        else:
                            square_in(quad, tau, 0)
                            if t > 0:
                                mean(TILES * quad + tau - 1, t - 1, gz)
                            elif behind:
                                mean(TILES * quad + tau - 1, 31, 1 - gz)
                            square_in(quad, tau, 1)
                        if ahead and tau in ph.project_at:
                            project(quad + 1, ph.project_at.index(tau))
                        if behind and (qz, tau) == BLOCKS_AT[ph.l1]:
                            finish(g - 1, 1 - gz)
                        if behind and not ph.l1 and (qz, tau) == (0, 14):
                            pe_row_sums(pe, s, g - 1, 1 - gz, misc_b)

            def body(r):
                for gz in range(2):
                    body_gz(2 * r + gz, gz)
            two_rounds(pe, body, NG)
            if not ph.l1:
                mean(32 * NG - 1, 31, 1)
            finish(NG - 1, 1)
            if not ph.l1:
                pe_row_sums(pe, s, NG - 1, 1, misc_b)

        def feat_act(act, ph):
            s = ph.s
            dst_of = {"hs": hs4, "hn": hn4}

            def project(quad, qz, j):
                act.wait_ge(s["lin_filled"], ph.steps * quad + j + 1)
                if j == 0:
                    nc.scalar.copy(xt4, misc_a[:, :]).then_inc(s["lin_out"], 1)
                    return
                w, _, dst = ph.chain[j - 1]
                if dst in ("p", "q"):
                    after(act, s["formed"], ph.dve_tiles * (quad - 1))
                    if ph.l1:
                        after(act, s["pooled"], 4 * (quad - 1))
                    if ph.l1 and dst == "q":
                        after(act, s["scored"], TILES * (quad - 1))
                if dst == "q":
                    out_q = q4[:, qz, :]
                    if ph.l1:
                        nc.scalar.mul(out_q, misc_a[:, :], -1.0).then_inc(s["lin_out"], 1)
                    else:
                        nc.scalar.copy(out_q, misc_a[:, :]).then_inc(s["lin_out"], 1)
                    return
                bias = {"hs": C_BSELF, "hn": C_BNB, "p": C_A1B if ph.l1 else C_B1}[dst]
                d = p4[:, qz, :] if dst == "p" else dst_of[dst]
                nc.scalar.activation(d, misc_a[:, :], ACT.Identity, bias=cols[:, bias:bias + 1]).then_inc(s["lin_out"], 1)

            def relu_pooled(quad, m):
                act.wait_ge(s["pooled"], 4 * quad + m + 1)
                nc.scalar.activation(pool_tile[m % 2], pool_tile[m % 2], ACT.Relu).then_inc(s["relued"], 1)

            def relu(tile, slot):
                act.wait_ge(s["formed"], tile + 1)
                nc.scalar.activation(pairs[:, slot, :], pairs[:, slot, :], ACT.Relu).then_inc(s["relued"], 1)

            def square(tile, h):
                act.wait_ge(s["y_filled"], 2 * tile + h + 1)
                after(act, s["scored"], tile)
                nc.scalar.activation(squares[:, h, :], wide[h][:, :], ACT.Square,
                                     bias=cols[:, C_B2C:C_B2C + 1]).then_inc(s["squared"], 1)

            def weigh(g, gz):
                if ph.l1:
                    act.wait_ge(s["cut"], g + 1)
                    after(act, s["weighed"], g)
                    nc.scalar.activation(score_a, score_b, ACT.Exp).then_inc(s["exped"], 1)
                else:
                    act.wait_ge(s["scored"], 32 * (g + 1))
                    after(act, s["inverted"], g)
                    nc.scalar.activation(score_a, sums[gz][:, :], ACT.Sqrt,
                                         bias=cols[:, C_EPS:C_EPS + 1]).then_inc(s["std_out"], 1)

            def stage(quad):
                after(act, s["lin_filled"], ph.steps * (quad - 1) + 1)
                alone(act)
                for n in range(QU):
                    u = QU * quad + n
                    nc.scalar.activation(xs4[:, n, :], x[:, ds(u, 1), :].rearrange("p a d -> p (a d)"), ACT.Identity,
                                         scale=node[:, ds(u, 1), RSTD], bias=node[:, ds(u, 1), SHIFT]) \
                        .then_inc(s["staged"], 1)

            stage(0)
            for j in range(ph.steps):
                project(0, 0, j)
            stage(1)
            if not ph.l1:
                relu(0, 0)

            def body_gz(g, gz):
                for qz in range(2):
                    quad = 2 * g + qz
                    static = isinstance(g, int)
                    ahead = not static or quad + 1 < NQ
                    behind = not static or g >= 1
                    for tau in range(TILES):
                        tile = TILES * quad + tau
                        if not ph.l1:
                            if not static or tile + 1 < 32 * NG:
                                relu(tile + 1, (tau + 1) % 4)
                            square(tile, 0)
                            square(tile, 1)
                        elif tau % 4 == 1:
                            relu_pooled(quad, tau // 4)
                        if ahead and tau in ph.project_at:
                            project(quad + 1, 1 - qz, ph.project_at.index(tau))
                        if tau == 15 and (not static or quad + 2 < NQ):
                            stage(quad + 2)
                        if behind and qz == 0 and tau == (6 if ph.l1 else 3):
                            weigh(g - 1, 1 - gz)
                        if behind and (qz, tau) == BLOCKS_AT[ph.l1]:
                            act_blocks(act, s, g - 1, 1 - gz, ph.groups_before, misc_b)
                        if behind and not ph.l1 and (qz, tau) == (0, 14):
                            act_row_sums(act, s, g - 1, SUM_W, misc_b)

            def body(r):
                for gz in range(2):
                    body_gz(2 * r + gz, gz)
            two_rounds(act, body, NG)
            weigh(NG - 1, 1)
            act_blocks(act, s, NG - 1, 1, ph.groups_before, misc_b)
            if not ph.l1:
                act_row_sums(act, s, NG - 1, SUM_W, misc_b)

        def feat_dve(v, ph):
            s = ph.s

            def form(quad, qz, n):
                if ph.l1:
                    bb, ih, slot = DVE_GRAPHS[n // 2], n % 2, n % 3
                    after(v, s["scored"], TILES * quad + (n - 2 + (n - 3) // 3 if n >= 3 else n - 3))
                else:
                    bb, ih, slot = n // 2, n % 2, n % 4
                    after(v, s["y_filled"], 2 * (TILES * quad + n - 3))
                i0 = bb * N + ih * 32
                a = p4[:, qz, i0:i0 + 32].unsqueeze(2).to_broadcast([P, 32, N])
                c = q4[:, qz, bb * N:(bb + 1) * N].unsqueeze(1).to_broadcast([P, 32, N])
                nc.vector.tensor_tensor(pairs[:, slot, :].rearrange("p (i j) -> p i j", j=N), a, c,
                                        ALU.max if ph.l1 else ALU.add).then_inc(s["formed"], 1)

            def r3(t):
                return t.rearrange("p (i j) -> p i j", j=N)

            def b3(t):
                return t.unsqueeze(2).to_broadcast([P, 8, N])

            def shift(g, gz):
                v.wait_ge(s["scored"], 32 * (g + 1))
                v.wait_ge(s["masked"], 3 * (g + 1))
                nc.vector.scalar_tensor_tensor(out=score_a, in0=sums[gz][:, :], scalar=cols[:, C_A2B:C_A2B + 1],
                                               in1=mask, op0=ALU.add, op1=ALU.mult).then_inc(s["shifted"], 1)

            def top(g):
                v.wait_ge(s["topped"], 2 * g + 1)
                nc.vector.tensor_reduce(row_max, r3(score_b), AX.X, ALU.max).then_inc(s["topped"], 1)

            def cut(g):
                v.wait_ge(s["topped"], 2 * g + 2)
                nc.vector.tensor_tensor(r3(score_b), r3(score_b), b3(row_max), ALU.subtract).then_inc(s["cut"], 1)

            def total(g):
                v.wait_ge(s["exped"], g + 1)
                nc.vector.tensor_reduce(row_sum, r3(score_a), AX.X, ALU.add).then_inc(s["totalled"], 1)

            def invert(g):
                if ph.l1:
                    v.wait_ge(s["totalled"], g + 1)
                    nc.vector.reciprocal(row_inv, row_sum).then_inc(s["inverted"], 1)
                else:
                    v.wait_ge(s["std_out"], g + 1)
                    after(v, s["weighed"], g)
                    nc.vector.reciprocal(score_b, score_a).then_inc(s["inverted"], 1)

            def end_step(g, gz, tau):
                if ph.l1:
                    if tau == 1:
                        shift(g, gz)
                    if tau == 3:
                        top(g)
                    if tau == 4:
                        cut(g)
                    if tau == 6:
                        total(g)
                    if tau == 7:
                        invert(g)
                elif tau == 6:
                    invert(g)

            v.wait_ge(s["lin_out"], ph.steps)

            def body_gz(g, gz):
                for qz in range(2):
                    quad = 2 * g + qz
                    behind = not isinstance(g, int) or g >= 1
                    v.wait_ge(s["lin_out"], ph.steps * (quad + 1))
                    for tau in range(ph.dve_tiles):
                        form(quad, qz, tau)
                        if behind and qz == 0:
                            end_step(g - 1, 1 - gz, tau)

            def body(r):
                for gz in range(2):
                    body_gz(2 * r + gz, gz)
            two_rounds(v, body, NG)
            for tau in range(10):
                end_step(NG - 1, 1, tau)

        def feat_pool(g_eng, ph):
            s = ph.s

            def masks(g, gz):
                g_eng.wait_ge([s["adj_in0"], s["adj_in1"]][gz], 32 * (g - gz) + 64)
                after(g_eng, s["shifted"], g)
                alone(g_eng)
                nc.gpsimd.tensor_scalar(is_zero, adj_rows[:, gz, :], 0.0, None, ALU.is_equal).then_inc(s["masked"], 1)
                g_eng.wait_ge(s["masked"], 3 * g + 1)
                alone(g_eng)
                nc.gpsimd.tensor_scalar(mask, is_zero, -1.0, 1.0, ALU.mult, ALU.add).then_inc(s["masked"], 1)
                nc.gpsimd.tensor_scalar(fill, is_zero, -NEG, None, ALU.mult).then_inc(s["masked"], 1)

            def fill_in(g):
                g_eng.wait_ge(s["shifted"], g + 1)
                nc.gpsimd.tensor_tensor(score_b, score_a, fill, ALU.add).then_inc(s["topped"], 1)

            def weigh(g, gz):
                after(g_eng, s["turned"], g)
                g_eng.wait_ge(s["inverted"], g + 1)
                if ph.l1:
                    nc.gpsimd.tensor_tensor(weights.rearrange("p (i j) -> p i j", j=N),
                                            score_a.rearrange("p (i j) -> p i j", j=N),
                                            row_inv.unsqueeze(2).to_broadcast([P, 8, N]), ALU.mult) \
                        .then_inc(s["weighed"], 1)
                else:
                    g_eng.wait_ge([s["adj_in0"], s["adj_in1"]][gz], 32 * (g - gz) + 64)
                    nc.gpsimd.tensor_tensor(weights, score_b, adj_rows[:, gz, :], ALU.mult).then_inc(s["weighed"], 1)

            def form(quad, qz, m):
                g_eng.wait_ge(s["lin_out"], ph.steps * (quad + 1))
                after(g_eng, s["scored"], TILES * quad + 4 * m - 4)
                bb, i0 = POOL_GRAPHS[m // 2], POOL_GRAPHS[m // 2] * N + (m % 2) * 32
                a = p4[:, qz, i0:i0 + 32].unsqueeze(2).to_broadcast([P, 32, N])
                c = q4[:, qz, bb * N:(bb + 1) * N].unsqueeze(1).to_broadcast([P, 32, N])
                nc.gpsimd.tensor_tensor(pool_tile[m % 2].rearrange("p (i j) -> p i j", j=N), a, c,
                                        ALU.subtract).then_inc(s["pooled"], 1)

            def body_gz(g, gz):
                behind = not isinstance(g, int) or g >= 1
                if not ph.l1:
                    if behind:
                        weigh(g - 1, 1 - gz)
                    return
                for m in range(4):
                    form(2 * g, 0, m)
                    if behind and m == 0:
                        fill_in(g - 1)
                    if behind and m == 3:
                        weigh(g - 1, 1 - gz)
                for m in range(4):
                    form(2 * g + 1, 1, m)
                    if m == 1:
                        masks(g, gz)

            def body(r):
                for gz in range(2):
                    body_gz(2 * r + gz, gz)
            two_rounds(g_eng, body, NG)
            if ph.l1:
                fill_in(NG - 1)
            weigh(NG - 1, 1)

        def feat_sp(sp, ph):
            s = ph.s

            def body(r):
                for gz in range(2):
                    g = 2 * r + gz
                    after(sp, s["weighed"], g - 1)
                    alone(sp)
                    load_adj_rows(sp, g, gz, [s["adj_in0"], s["adj_in1"]][gz])
                    if not isinstance(g, int) or g >= 1:
                        sp_blocks(sp, s, g - 1, 1 - gz, w_blocks)
            two_rounds(sp, body, NG)
            sp_blocks(sp, s, NG - 1, 1, w_blocks)

        class Agg:
            def __init__(self, name, blocks, w_self, w_nb, moments_in, moments_out):
                self.name, self.s, self.base = name, agg_sems, NU * ("l1b", "l3").index(name)
                self.blocks, self.w_self, self.w_nb = blocks, w_self, w_nb
                self.moments_in, self.moments_out = moments_in, moments_out
                self.l1 = name == "l1b"

        agg_phases = {"l1b": Agg("l1b", w_blocks, wl[:, WSELF, :], wl[:, WNB, :], 0, 1),
                      "l3": Agg("l3", adj_blocks, wt[:, L3T, :], wt[:, L3T, :], 2, 3)}

        def agg_pool(g_eng, ph):
            s, base = ph.s, ph.base

            def bias(u, z):
                g_eng.wait_ge(s["n_out"], u + 1)
                after(g_eng, s["o_filled"], u - 1)
                b = rows[:, R_BNB, :].unsqueeze(1).to_broadcast([P, 2, D])
                nc.gpsimd.tensor_tensor(n_full[:, z % 2], n_sb[:, z % 2], b, ALU.add).then_inc(s["n_biased"], 1)

            def body(r):
                for z in range(4):
                    bias(base + 4 * r + z, z)
            if ph.l1:
                four_unit_rounds(g_eng, body)

        def agg_pe(pe, ph):
            s, base = ph.s, ph.base

            def turn(u, z):
                pe.wait_ge(s["staged"], u + 1)
                after(pe, s["xt_out"], u)
                src = xs[:, z, :] if ph.l1 else xd[:, z, :]
                nc.tensor.transpose(misc_a[:, 0:P], src, ident[:, :]).then_inc(s["t_filled"], 1)

            def neighbours(u, z):
                pe.wait_ge(s["xt_out"], u + 1)
                after(pe, s["n_out"], u)
                for b in range(2):
                    m = nc.tensor.matmul(misc_b[:, b * D:(b + 1) * D], xt_flat[:, z, b * P:(b + 1) * P], ph.w_nb,
                                         start=True, stop=True)
                m.then_inc(s["n_filled"], 1)

            def combine(u, z):
                pe.wait_ge(s["block_in"], u + 1)
                after(pe, s["o_sum"], u - 1)
                pe.wait_ge(s["n_biased"] if ph.l1 else s["n_out"], u + 1)
                n = n_full if ph.l1 else n_sb
                for b in range(2):
                    nc.tensor.matmul(sums[z % 2][b * N:(b + 1) * N, 0:D], block_now[:, z, b * N:(b + 1) * N],
                                     n[:, z % 2, b, :], start=True, stop=False)
                nc.tensor.matmul(sums[z % 2][:, 0:D], xt_flat[:, z, plain_xt], ph.w_self,
                                 start=False, stop=True).then_inc(s["o_filled"], 1)

            turn(base, 0)
            turn(base + 1, 1)
            neighbours(base, 0)
            neighbours(base + 1, 1)

            def body(r):
                for z in range(4):
                    u = base + 4 * r + z
                    if not isinstance(r, int) or r < NU // 4 - 1 or z < 2:
                        turn(u + 2, (z + 2) % 4)
                    combine(u, z)
                    if not isinstance(r, int) or r < NU // 4 - 1 or z < 2:
                        neighbours(u + 2, (z + 2) % 4)
            four_unit_rounds(pe, body)

        def agg_act(act, ph):
            s, base = ph.s, ph.base

            def stage(u, z):
                at = ds(u - ph.base, 1)
                src = x[:, at, :].rearrange("p a d -> p (a d)")
                if ph.l1:
                    after(act, s["x_new"], u - 3)
                    alone(act)
                    nc.scalar.activation(xs[:, z, :], src, ACT.Identity, scale=node[:, at, RSTD],
                                         bias=node[:, at, SHIFT]).then_inc(s["staged"], 1)
                else:
                    after(act, s["t_filled"], u - 3)
                    alone(act)
                    nc.scalar.activation(xd[:, z, :], src, ACT.Identity, scale=node[:, at, RSTD_DINV],
                                         bias=node[:, at, SHIFT_DINV]).then_inc(s["staged"], 1)

            def copy_xt(u, z):
                act.wait_ge(s["t_filled"], u + 1)
                src = misc_a[:, 0:P].rearrange("p (b i) -> p b i", b=2)
                nc.scalar.copy(xt_dup[:, z, :, 0, :], src)
                nc.scalar.copy(xt_dup[:, z, :, 1, :], src).then_inc(s["xt_out"], 1)

            def copy_n(u, z):
                act.wait_ge(s["n_filled"], u + 1)
                after(act, s["n_biased"] if ph.l1 else s["o_filled"], u - 1)
                nc.scalar.copy(n_sb[:, z % 2], misc_b[:, 0:2 * D].rearrange("p (b d) -> p b d", b=2)) \
                    .then_inc(s["n_out"], 1)

            for u in range(3):
                stage(base + u, u)
            copy_xt(base, 0)
            copy_xt(base + 1, 1)
            copy_n(base, 0)
            copy_n(base + 1, 1)

            def body(r):
                for z in range(4):
                    u = base + 4 * r + z
                    static = isinstance(r, int)
                    if not static or r < NU // 4 - 1 or z < 2:
                        copy_xt(u + 2, (z + 2) % 4)
                    if not static or r < NU // 4 - 1 or z < 1:
                        stage(u + 3, (z + 3) % 4)
                    if not static or r < NU // 4 - 1 or z < 2:
                        copy_n(u + 2, (z + 2) % 4)
            four_unit_rounds(act, body)

        def agg_dve(v, ph):
            s, base = ph.s, ph.base

            def fetch(u, z):
                after(v, s["o_filled"], u - 3)
                nc.vector.tensor_copy(block_now[:, z, :], ph.blocks[:, ds(u - ph.base, 1), :].rearrange("p a c -> p (a c)")) \
                    .then_inc(s["block_in"], 1)

            def normalise(u, z):
                after(v, s["x_new"], u - 3)
                at = ds(u - ph.base, 1)
                nc.vector.tensor_scalar(xs[:, z, :], x[:, at, :].rearrange("p a d -> p (a d)"), node[:, at, RSTD],
                                        node[:, at, SHIFT], ALU.mult, ALU.add).then_inc(s["xs_in"], 1)

            def take(u, z):
                v.wait_ge(s["o_filled"], u + 1)
                after(v, s["x_new"], u - 1)
                o = sums[z % 2][:, 0:D]
                if ph.l1:
                    nc.vector.tensor_tensor(agg_a[:, z % 2, :], o, rows[:, R_BSELF, :], ALU.add) \
                        .then_inc(s["o_sum"], 1)
                else:
                    nc.vector.scalar_tensor_tensor(out=agg_a[:, z % 2, :], in0=o,
                                                   scalar=node[:, ds(u - ph.base, 1), DINV],
                                                   in1=rows[:, R_L3B, :], op0=ALU.mult, op1=ALU.add) \
                        .then_inc(s["o_sum"], 1)

            def add(u, z):
                v.wait_ge(s["o_sum"], u + 1)
                if not ph.l1:
                    v.wait_ge(s["xs_in"], u - ph.base + 1)
                nc.vector.scalar_tensor_tensor(out=x[:, ds(u - ph.base, 1), :].rearrange("p a d -> p (a d)"),
                                               in0=agg_a[:, z % 2, :], scalar=0.0, in1=xs[:, z, :],
                                               op0=ALU.max, op1=ALU.add).then_inc(s["x_new"], 1)

            def stats(u):
                v.wait_ge(s["x_new"], u + 1)
                alone(v)
                nc.vector.bn_stats(halves[:, ds(u - ph.base, 1), :].rearrange("p a d -> p (a d)"),
                                   x[:, ds(u - ph.base, 1), :].rearrange("p a d -> p (a d)")) \
                    .then_inc(stats_done[ph.moments_out], 1)

            def body(r):
                for z in range(4):
                    u = base + 4 * r + z
                    take(u, z)
                    if not isinstance(r, int) or r > 0 or z > 0:
                        stats(u - 1)
                    add(u, z)
                    if not isinstance(r, int) or r < NU // 4 - 1 or z < 1:
                        fetch(u + 3, (z + 3) % 4)
                        if not ph.l1:
                            normalise(u + 3, (z + 3) % 4)
            for u in range(3):
                fetch(base + u, u)
                if not ph.l1:
                    normalise(base + u, u)
            four_unit_rounds(v, body)
            stats(base + NU - 1)

        block = ctx.enter_context(nc.Block())
        NRAW, NROW, NCOL = 5, 11, 6

        @block.sync
        def _(sp):
            sp.dma_start(ident[:, :], ident_d).then_inc(loaded["ident"], 16)
            sp.dma_start(block_of[:, :], block_of_d).then_inc(loaded["block_of"], 16)
            load_adj_rows(sp, 0, 0, first["adj_in0"])
            load_adj_rows(sp, 1, 1, first["adj_in1"])
            for l in range(2):
                sp.dma_start(wraw[:, 3 * l:3 * l + 2, :], inp["L0_gnn_w1"][l].rearrange("o (h d) -> o h d", h=2)) \
                    .then_inc(loaded["raw"], 16)
                sp.dma_start(wraw[:, 3 * l + 2, :], inp["L0_gnn_w2"][l]).then_inc(loaded["raw"], 16)
            sp.dma_start(wraw[:, 6, :], inp["L3_gnn_W"]).then_inc(loaded["raw"], 16)
            sp.dma_start(sel_f[:, :, :], sel_d).then_inc(loaded["sel"], 16)
            for k, v in ((WSELF, inp["L1_gnn_W_self_w"]), (WNB, inp["L1_gnn_W_nb_w"]),
                         (A1I, inp["L1_gnn_A1_w"][0:D, :]), (A1J, inp["L1_gnn_A1_w"][D:2 * D, :]),
                         (W1A, inp["L2_gnn_W1"][0:D, :]), (W1B, inp["L2_gnn_W1"][D:2 * D, :]),
                         (W2G, inp["L2_gnn_W2"])):
                sp.dma_start(wl[:, k, :], v).then_inc(loaded["flat"], 16)
            sp.dma_start(x[:, 0:16, :], x_dram[:, 0:16, :]).then_inc(loaded["x_first"], 16)
            for g in range(NG):
                sp_blocks(sp, first, g, g % 2, adj_blocks)
                if g + 2 < NG:
                    load_adj_rows(sp, g + 2, g % 2, [first["adj_in0"], first["adj_in1"]][g % 2])
                if g % 2 == 0:
                    quarter = slice(8 * g, 8 * g + 16)
                    sp.dma_start(adj_nodes[:, quarter, :], adj_dram[:, quarter, :]).then_inc(loaded["adj"], 16)
            near_sp(sp, near_phases["l0a"])
            near_sp(sp, near_phases["l0b"])
            feat_sp(sp, feat_phases["l1a"])
            feat_sp(sp, feat_phases["l2a"])
            near_sp(sp, near_phases["l2b"])
            for g in range(NG):
                sp.wait_ge(y_ready, OUT_DVE * (g + 1))
                sp.wait_ge(y_act_ready, (GU - OUT_DVE) * (g + 1))
                sp.dma_start(out_dram[:, GU * g:GU * g + GU, :], x[:, GU * g:GU * g + GU, :]).then_inc(out_done, 16)
            sp.wait_ge(out_done, 16 * NG)

        def pool_windows(g_eng, phase_ready):
            nc.gpsimd.memset(windows.rearrange("p z q c -> p (z q c)"), 0.0).then_inc(phase_ready, 1)
            nc.gpsimd.memset(spread.rearrange("p z c -> p (z c)"), 0.0).then_inc(phase_ready, 1)

        windows_zero = [sem("windows_zero0"), sem("windows_zero1")]

        @block.gpsimd
        def _(g_eng):
            nc.gpsimd.memset(block_stage[:, :, :, :].rearrange("p z u c -> p (z u c)"), 0.0).then_inc(consts, 1)
            nc.gpsimd.memset(sel[:, :, :].rearrange("p q c -> p (q c)"), 0.0).then_inc(consts, 1)
            for w in (window_a2, window_two, window_mean):
                nc.gpsimd.memset(w[:, :], 0.0).then_inc(consts, 1)
            nc.gpsimd.memset(ones[:, :], 1.0).then_inc(consts, 1)
            nc.gpsimd.memset(node[:, :, :], 0.0).then_inc(node_zero, 1)
            for k, v in ((R_B1[0], inp["L0_gnn_b1"][0:1, :]), (R_B1[1], inp["L0_gnn_b1"][1:2, :]),
                         (R_B2[0], inp["L0_gnn_b2"][0:1, :]), (R_B2[1], inp["L0_gnn_b2"][1:2, :]),
                         (R_BSELF, inp["L1_gnn_W_self_b"][None, :]), (R_BNB, inp["L1_gnn_W_nb_b"][None, :]),
                         (R_B2C, inp["L2_gnn_b2"][None, :]), (R_GAMMA, inp["L2_gnn_gamma"][None, :]),
                         (R_BETA, inp["L2_gnn_beta"][None, :]), (R_L3B, inp["L3_gnn_b"][None, :]),
                         (R_B1L2, inp["L2_gnn_b1"][None, :])):
                g_eng.dma_start(rows[:, k, :], v.to_broadcast([P, D])).then_inc(loaded["row"], 16)
            for k, v in ((C_BSELF, inp["L1_gnn_W_self_b"][:, None]), (C_BNB, inp["L1_gnn_W_nb_b"][:, None]),
                         (C_A1B, inp["L1_gnn_A1_b"][:, None]), (C_B1, inp["L2_gnn_b1"][:, None]),
                         (C_A2, inp["L1_gnn_A2_w"]),
                         (C_A2B, inp["L1_gnn_A2_b"][None, :].to_broadcast([P, 1]))):
                g_eng.dma_start(cols[:, k:k + 1], v).then_inc(loaded["col"], 16)
            g_eng.wait_ge(consts, 6)
            nc.gpsimd.memset(window_mean[:, 31:32], 1.0 / D).then_inc(consts, 1)
            g_eng.wait_ge(loaded["col"], 16 * NCOL)
            nc.gpsimd.memset(cols[:, C_EPS:C_EPS + 1], EPS).then_inc(consts, 1)
            nc.gpsimd.tensor_copy(window_a2[:, 31:32], cols[:, C_A2:C_A2 + 1]).then_inc(consts, 1)
            for k in (31, 32):
                nc.gpsimd.tensor_scalar(window_two[:, k:k + 1], cols[:, C_A2:C_A2 + 1], -1.0, None, ALU.mult) \
                    .then_inc(consts, 1)
            g_eng.wait_ge(loaded["sel"], 16)
            nc.gpsimd.tensor_copy(sel[0:QROWS, :, :], sel_f[:, :, :]).then_inc(consts, 1)
            pool_windows(g_eng, windows_zero[0])
            g_eng.wait_ge(loaded["row"], 16 * NROW)
            near_pool(g_eng, near_phases["l0a"])
            near_pool(g_eng, near_phases["l0b"])
            feat_pool(g_eng, feat_phases["l1a"])
            agg_pool(g_eng, agg_phases["l1b"])
            feat_pool(g_eng, feat_phases["l2a"])
            g_eng.wait_ge(feat["l2a"]["sum_out"], NG)
            pool_windows(g_eng, windows_zero[1])
            near_pool(g_eng, near_phases["l2b"])
            agg_pool(g_eng, agg_phases["l3"])

        @block.vector
        def _(v):
            v.wait_ge(loaded["flat"], 16 * 7)
            v.wait_ge(loaded["row"], 16 * NROW)
            nc.vector.tensor_reduce(w2_mean[:, 0:1], wl[:, W2G, :], AX.X, ALU.add).then_inc(prep, 1)
            nc.vector.tensor_reduce(w2_mean[:, 1:2], rows[:, R_B2C, :], AX.X, ALU.add).then_inc(prep, 1)
            v.wait_ge(prep, 2)
            nc.vector.tensor_scalar(w2_mean[:, :], w2_mean[:, :], 1.0 / D, None, ALU.mult).then_inc(prep, 1)
            v.wait_ge(prep, 3)
            nc.vector.tensor_scalar(wl[:, W2, :], wl[:, W2G, :], w2_mean[:, 0:1], None, ALU.subtract).then_inc(prep, 1)
            nc.vector.tensor_scalar(rows[:, 11, :], rows[:, R_B2C, :], w2_mean[:, 1:2], None, ALU.subtract) \
                .then_inc(prep, 1)
            v.wait_ge(prep, 5)
            nc.vector.tensor_tensor(wl[:, W2G, :], wl[:, W2, :], rows[:, R_GAMMA, :], ALU.mult).then_inc(prep, 1)
            nc.vector.tensor_tensor(rows[:, R_B2C, :], rows[:, 11, :], rows[:, R_GAMMA, :], ALU.mult).then_inc(prep, 1)
            near_dve(v, near_phases["l0a"])
            near_dve(v, near_phases["l0b"])
            dve_var(v, 0)
            dve_rstd(v, 0)
            feat_dve(v, feat_phases["l1a"])
            blocks_complete(v, 2)
            agg_dve(v, agg_phases["l1b"])
            dve_var(v, 1)
            dve_rstd(v, 1)
            feat_dve(v, feat_phases["l2a"])
            v.wait_ge(dinv_steps, 2)
            nc.vector.reciprocal(node[:, :, DINV], degree[:, :]).then_inc(dinv_steps, 1)
            near_dve(v, near_phases["l2b"])
            dve_var(v, 2)
            dve_rstd(v, 2)
            v.wait_ge(norm_ready[2], 1)
            for dst, src in ((RSTD_DINV, RSTD), (SHIFT_DINV, SHIFT)):
                nc.vector.tensor_tensor(node[:, :, dst], node[:, :, src], node[:, :, DINV], ALU.mult) \
                    .then_inc(norm_ready[2], 1)
            agg_dve(v, agg_phases["l3"])
            dve_var(v, 3)
            dve_rstd(v, 3)
            v.wait_ge(norm_ready[3], 1)
            for g in range(NG):
                for n in range(OUT_DVE):
                    u = GU * g + n
                    nc.vector.tensor_scalar(x[:, u, :], x[:, u, :], node[:, u, RSTD:RSTD + 1],
                                            node[:, u, SHIFT:SHIFT + 1], ALU.mult, ALU.add).then_inc(y_ready, 1)

        @block.scalar
        def _(act):
            act.wait_ge(consts, 1)
            for g in range(NG):
                act_blocks(act, first, g, g % 2, 0, wide[g % 2])
            for k in range(7):
                act.wait_ge(wt_filled, k + 1)
                nc.scalar.copy(wt[:, k, :], (misc_a if k % 2 else misc_b)[:, 0:P]).then_inc(wt_out, 1)
            act.wait_ge(b2c_filled, 1)
            nc.scalar.copy(cols[:, C_B2C:C_B2C + 1], misc_a[:, 0:1]).then_inc(b2c_out, 1)

            act.wait_ge(windows_zero[0], 2)
            act.wait_ge(loaded["x_first"], 16)
            act.wait_ge(loaded["block_of"], 16)
            act.wait_ge(loaded["row"], 16 * NROW)
            act.wait_ge(moved[0], 16)
            near_act(act, near_phases["l0a"])
            near_act(act, near_phases["l0b"])
            act_std(act, 0)
            act.wait_ge(norm_ready[0], 1)
            feat_act(act, feat_phases["l1a"])
            blocks_complete(act, 2)
            agg_act(act, agg_phases["l1b"])
            act_std(act, 1)
            act.wait_ge(norm_ready[1], 1)
            feat_act(act, feat_phases["l2a"])
            nc.scalar.activation(degree[:, :], node[:, :, SUM_ADJ], ACT.Copy, bias=1.0 + 1e-6).then_inc(dinv_steps, 1)
            act.wait_ge(dinv_steps, 1)
            nc.scalar.activation(degree[:, :], degree[:, :], ACT.Sqrt).then_inc(dinv_steps, 1)
            act.wait_ge(dinv_steps, 3)
            act.wait_ge(windows_zero[1], 2)
            act.wait_ge(feat["l2a"]["sum_out"], NG)
            blocks_complete(act, 3)
            near_act(act, near_phases["l2b"])
            act_std(act, 2)
            act.wait_ge(norm_ready[2], 3)
            agg_act(act, agg_phases["l3"])
            act_std(act, 3)
            act.wait_ge(norm_ready[3], 1)
            for g in range(NG):
                for n in range(OUT_DVE, GU):
                    u = GU * g + n
                    nc.scalar.activation(x[:, u, :], x[:, u, :], ACT.Identity,
                                         scale=node[:, u, RSTD:RSTD + 1], bias=node[:, u, SHIFT:SHIFT + 1]) \
                        .then_inc(y_act_ready, 1)

        @block.tensor
        def _(pe):
            pe.wait_ge(consts, 6)
            pe.wait_ge(loaded["ident"], 16)
            for g in range(NG):
                pe_turn(pe, first, g, adj_rows[:, g % 2, :], [first["adj_in0"], first["adj_in1"]][g % 2],
                        64 * (g // 2 + 1), wide[g % 2], banks=2)
            pe.wait_ge(loaded["raw"], 16 * NRAW)
            for k in range(7):
                after(pe, wt_out, k - 1)
                nc.tensor.transpose((misc_a if k % 2 else misc_b)[:, 0:P], wraw[:, k, :], ident[:, :]) \
                    .then_inc(wt_filled, 1)
            pe.wait_ge(prep, 7)
            pe.wait_ge(wt_out, 7)
            nc.tensor.matmul(misc_a[:, 0:1], rows[0:1, 11, :], ones[0:1, :], start=True, stop=True) \
                .then_inc(b2c_filled, 1)
            pe.wait_ge(b2c_out, 1)
            pe.wait_ge(consts, 12)
            pe.wait_ge(first["blocks_out"], 2 * NG)
            near_pe(pe, near_phases["l0a"])
            near_pe(pe, near_phases["l0b"])
            feat_pe(pe, feat_phases["l1a"])
            agg_pe(pe, agg_phases["l1b"])
            feat_pe(pe, feat_phases["l2a"])
            near_pe(pe, near_phases["l2b"])
            agg_pe(pe, agg_phases["l3"])


def constants():
    ident = np.eye(P, dtype=np.float32)
    sel = np.zeros((QROWS, 4, P), np.float32)
    for q in range(4):
        for par in range(2):
            for part in range(3):
                sel[(3 * par + part) * 4 + q, q, par * N:(par + 1) * N] = 1.0
    block_of = np.zeros((P, 4), np.float32)
    for row in range(P):
        block_of[row, (row % 8) // 2] = 1.0
    return {"ident_d": ident, "sel_d": sel, "block_of_d": block_of}


def kernel(**inputs):
    import concourse.bacc as bacc
    from concourse.bass_utils import run_bass_kernel_spmd

    nc = bacc.Bacc("TRN2", target_bir_lowering=False, num_devices=1)
    arrays, aps = {}, {}
    for name in INPUTS:
        arrays[f"in_{name}"] = np.ascontiguousarray(inputs[name])
    for name, value in constants().items():
        arrays[f"in_{name}"] = value
    for name, a in arrays.items():
        aps[name[3:]] = nc.dram_tensor(name, a.shape, mybir.dt.from_np(a.dtype), kind="ExternalInput").ap()
    out = nc.dram_tensor("out", (NB, N, D), F32, kind="ExternalOutput").ap()
    parts_dram = nc.dram_tensor("parts_dram", (2, 2, 3, N, D), BF16, kind="Internal").ap()
    program(nc, out, parts_dram, **aps)
    r = run_bass_kernel_spmd(nc, [arrays], core_ids=[0])
    return r.results[0]["out"]
```
